# Optimizing a Trainium2 kernel written in Bass

```python
import numpy as np
import jax
import jax.numpy as jnp

def _softmax(x, axis=-1):
    return jax.nn.softmax(x, axis=axis)

def _gelu(x):
    return jax.nn.gelu(x, approximate=True)

def _silu(x):
    return jax.nn.silu(x)

def _sigmoid(x):
    return jax.nn.sigmoid(x)

def _layernorm(x, axis=-1, eps=1e-05):
    m = jnp.mean(x, axis=axis, keepdims=True)
    v = jnp.var(x, axis=axis, keepdims=True)
    return (x - m) / jnp.sqrt(v + eps)

def _scatter_add(tgt, idx, src, axis=0):
    return tgt.at[idx].add(src)

def _segment_sum(src, seg, n):
    return jax.ops.segment_sum(src, seg, n)
kernel_name = 'mk_early_fusion_d2_tok_img768_r4_3024fa'

def setup_inputs(seed: int=0):
    np.random.seed(seed)
    _w = jnp.asarray

    def _rec_inputs():
        import jax
        import jax.numpy as jnp
        _rk = jax.random.key(seed)
        x = 7.57192e-06 + 1.00007 * jax.random.normal(jax.random.fold_in(_rk, 1), (16, 3, 128, 128), jnp.float32)
        txt = -0.000584974 + 1.00063 * jax.random.normal(jax.random.fold_in(_rk, 2), (16, 32, 192), jnp.float32)
        return (x, txt)
    x, txt = _rec_inputs()

    def _L0_tok_setup():
        import jax, jax.numpy as jnp
        import numpy as np
        PATCH = 16

        def _shift2d(x, shift):
            l, r, t, b = shift
            H, W = (x.shape[2], x.shape[3])
            xp = jnp.pad(x, ((0, 0), (0, 0), (max(t, 0), max(b, 0)), (max(l, 0), max(r, 0))))
            h0 = max(-t, 0)
            w0 = max(-l, 0)
            return xp[:, :, h0:h0 + H, w0:w0 + W]
        key = jax.random.key(seed)
        k1, k2 = jax.random.split(key)
        B, C, H, W = (64, 3, 224, 224)
        dim = 192
        patch_dim = PATCH * PATCH * 5 * C
        x = jax.random.normal(k1, (B, C, H, W), dtype=jnp.float32)
        ln_weight = jnp.ones((patch_dim,), dtype=jnp.float32)
        ln_bias = jnp.zeros((patch_dim,), dtype=jnp.float32)
        proj_weight = jax.random.normal(k2, (dim, patch_dim), dtype=jnp.float32) * patch_dim ** (-0.5)
        proj_bias = jnp.zeros((dim,), dtype=jnp.float32)
        return {'x': x, 'ln_weight': ln_weight, 'ln_bias': ln_bias, 'proj_weight': proj_weight, 'proj_bias': proj_bias}
    _L0_tok_all = _L0_tok_setup()
    _L0_tok_in = {k: v for k, v in _L0_tok_all.items() if k in ('ln_weight', 'ln_bias', 'proj_weight', 'proj_bias')}
    del _L0_tok_all

    def _L0_attn_setup():
        import jax, jax.numpy as jnp
        import numpy as np
        HEADS = 12
        SPLIT = 4
        key = jax.random.key(seed)
        ks = jax.random.split(key, 4)
        B, N, C = (4, 1024, 192)
        C1 = C // 2
        x = jax.random.normal(ks[0], (B, N, C), dtype=jnp.float32)
        W_reduce = jax.random.normal(ks[1], (C, C1), dtype=jnp.float32) * C ** (-0.5)
        b_reduce = jnp.zeros((C1,), dtype=jnp.float32)
        W_qkv = jax.random.normal(ks[2], (C1, 3 * C1), dtype=jnp.float32) * C1 ** (-0.5)
        b_qkv = jnp.zeros((3 * C1,), dtype=jnp.float32)
        W_proj = jax.random.normal(ks[3], (C1, C), dtype=jnp.float32) * C1 ** (-0.5)
        b_proj = jnp.zeros((C,), dtype=jnp.float32)
        return {'x': x, 'W_reduce': W_reduce, 'b_reduce': b_reduce, 'W_qkv': W_qkv, 'b_qkv': b_qkv, 'W_proj': W_proj, 'b_proj': b_proj}
    _L0_attn_all = _L0_attn_setup()
    _L0_attn_in = {k: v for k, v in _L0_attn_all.items() if k in ('W_reduce', 'b_reduce', 'W_qkv', 'b_qkv', 'W_proj', 'b_proj')}
    del _L0_attn_all

    def _L0_ffn_setup():
        import jax, jax.numpy as jnp
        import numpy as np
        NUM_EXPERTS = 8
        TOP_K = 2
        CAPACITY_FACTOR = 1.25
        MAX_GROUP_SIZE = 1024
        MIN_EXPERT_CAPACITY = 4

        def _moe_forward(x, w_router, wi, wo):
            B, T, D = x.shape
            E = NUM_EXPERTS
            num_tokens = B * T
            G = max(num_tokens // MAX_GROUP_SIZE, E)
            while num_tokens % G != 0 or G % E != 0:
                G += 1
            S = num_tokens // G
            C = max(int(TOP_K * CAPACITY_FACTOR * S / E), MIN_EXPERT_CAPACITY)
            xg = x.reshape(G, S, D)
            logits = jnp.einsum('gsd,de->gse', xg.astype(jnp.float32), w_router.astype(jnp.float32))
            probs = jax.nn.softmax(logits, axis=-1)
            gate, idx = jax.lax.top_k(probs, TOP_K)
            idx_kf = jnp.swapaxes(idx, 1, 2).reshape(G, TOP_K * S)
            mask = jax.nn.one_hot(idx_kf, E, dtype=jnp.int32)
            prio = jnp.cumsum(mask, axis=1) * mask - 1
            prio = jnp.swapaxes(prio.reshape(G, TOP_K, S, E), 1, 2)
            prio_se = prio.max(axis=2)
            gate_se = jnp.einsum('gsk,gske->gse', gate, jax.nn.one_hot(idx, E, dtype=gate.dtype))
            dispatch = jax.nn.one_hot(prio_se, C, dtype=x.dtype)
            combine = dispatch * gate_se[..., None].astype(x.dtype)
            expert_in = jnp.einsum('gsec,gsd->egcd', dispatch, xg)
            h = jax.nn.relu(jnp.einsum('egcd,edf->egcf', expert_in, wi))
            expert_out = jnp.einsum('egcf,efd->egcd', h, wo)
            out = jnp.einsum('gsec,egcd->gsd', combine, expert_out)
            return out.reshape(B, T, D)
        key = jax.random.key(seed)
        k1, k2, k3, k4 = jax.random.split(key, 4)
        B, T, D, F = (8, 256, 192, 768)
        x = jax.random.normal(k1, (B, T, D), jnp.float32)
        w_router = jax.random.normal(k2, (D, NUM_EXPERTS), jnp.float32) * D ** (-0.5)
        wi = jax.random.normal(k3, (NUM_EXPERTS, D, F), jnp.float32) * D ** (-0.5)
        wo = jax.random.normal(k4, (NUM_EXPERTS, F, D), jnp.float32) * F ** (-0.5)
        return {'x': x, 'w_router': w_router, 'wi': wi, 'wo': wo}
    _L0_ffn_all = _L0_ffn_setup()
    _L0_ffn_in = {k: v for k, v in _L0_ffn_all.items() if k in ('w_router', 'wi', 'wo')}
    del _L0_ffn_all

    def _L1_attn_setup():
        import jax, jax.numpy as jnp
        import numpy as np
        DIM = 192
        HEADS = 12
        HEAD_DIM = DIM // HEADS
        EPS = 1e-12

        def _l1_normalize(t):
            denom = jnp.maximum(jnp.sum(jnp.abs(t), axis=-2, keepdims=True), EPS)
            return t / denom
        key = jax.random.key(seed)
        k1, k2, k3 = jax.random.split(key, 3)
        x = jax.random.normal(k1, (8, 1024, DIM), dtype=jnp.float32)
        s = 1.0 / np.sqrt(DIM)
        w_qkv = jax.random.uniform(k2, (3 * DIM, DIM), dtype=jnp.float32, minval=-s, maxval=s)
        w_proj = jax.random.uniform(k3, (DIM, DIM), dtype=jnp.float32, minval=-s, maxval=s)
        b_proj = jnp.zeros((DIM,), dtype=jnp.float32)
        return {'x': x, 'w_qkv': w_qkv, 'w_proj': w_proj, 'b_proj': b_proj}
    _L1_attn_all = _L1_attn_setup()
    _L1_attn_in = {k: v for k, v in _L1_attn_all.items() if k in ('w_qkv', 'w_proj', 'b_proj')}
    del _L1_attn_all

    def _L1_ffn_setup():
        import jax, jax.numpy as jnp
        import numpy as np
        EPS = 1e-06

        def l2_normalize(x, axis):
            norm = jnp.sqrt(jnp.square(x).sum(axis=axis, keepdims=True))
            return x * (1.0 / (norm + EPS))
        key = jax.random.key(seed)
        ks = jax.random.split(key, 8)
        b, m, d = (32, 256, 192)
        n, p = (8, 4)
        h = d // 8
        X = jax.random.normal(ks[0], (b, m, d), dtype=jnp.float32)
        std_slot = float(np.sqrt(2.0 / (d + n * p)))
        slot_params = jax.random.normal(ks[1], (d, n, p), dtype=jnp.float32) * std_slot
        scale = jnp.ones((), dtype=jnp.float32)
        W_down = jax.random.normal(ks[2], (n, d, h), dtype=jnp.float32) * float(np.sqrt(1.0 / d))
        b_down = jnp.zeros((n, h), dtype=jnp.float32)
        W_up = jax.random.normal(ks[3], (n, h, d), dtype=jnp.float32) * float(np.sqrt(1.0 / h))
        b_up = jnp.zeros((n, d), dtype=jnp.float32)
        return {'X': X, 'slot_params': slot_params, 'scale': scale, 'W_down': W_down, 'b_down': b_down, 'W_up': W_up, 'b_up': b_up}
    _L1_ffn_all = _L1_ffn_setup()
    _L1_ffn_in = {k: v for k, v in _L1_ffn_all.items() if k in ('slot_params', 'scale', 'W_down', 'b_down', 'W_up', 'b_up')}
    del _L1_ffn_all
    return {'x': x, 'txt': txt, 'L0_tok_ln_weight': _L0_tok_in['ln_weight'], 'L0_tok_ln_bias': _L0_tok_in['ln_bias'], 'L0_tok_proj_weight': _L0_tok_in['proj_weight'], 'L0_tok_proj_bias': _L0_tok_in['proj_bias'], 'L0_attn_W_reduce': _L0_attn_in['W_reduce'], 'L0_attn_b_reduce': _L0_attn_in['b_reduce'], 'L0_attn_W_qkv': _L0_attn_in['W_qkv'], 'L0_attn_b_qkv': _L0_attn_in['b_qkv'], 'L0_attn_W_proj': _L0_attn_in['W_proj'], 'L0_attn_b_proj': _L0_attn_in['b_proj'], 'L0_ffn_w_router': _L0_ffn_in['w_router'], 'L0_ffn_wi': _L0_ffn_in['wi'], 'L0_ffn_wo': _L0_ffn_in['wo'], 'L1_attn_w_qkv': _L1_attn_in['w_qkv'], 'L1_attn_w_proj': _L1_attn_in['w_proj'], 'L1_attn_b_proj': _L1_attn_in['b_proj'], 'L1_ffn_slot_params': _L1_ffn_in['slot_params'], 'L1_ffn_scale': _L1_ffn_in['scale'], 'L1_ffn_W_down': _L1_ffn_in['W_down'], 'L1_ffn_b_down': _L1_ffn_in['b_down'], 'L1_ffn_W_up': _L1_ffn_in['W_up'], 'L1_ffn_b_up': _L1_ffn_in['b_up']}

def reference(x, txt, L0_tok_ln_weight, L0_tok_ln_bias, L0_tok_proj_weight, L0_tok_proj_bias, L0_attn_W_reduce, L0_attn_b_reduce, L0_attn_W_qkv, L0_attn_b_qkv, L0_attn_W_proj, L0_attn_b_proj, L0_ffn_w_router, L0_ffn_wi, L0_ffn_wo, L1_attn_w_qkv, L1_attn_w_proj, L1_attn_b_proj, L1_ffn_slot_params, L1_ffn_scale, L1_ffn_W_down, L1_ffn_b_down, L1_ffn_W_up, L1_ffn_b_up):
    import jax
    import jax.numpy as jnp

    def _L0_tok_ref(x, ln_weight, ln_bias, proj_weight, proj_bias):
        import jax, jax.numpy as jnp
        import numpy as np
        PATCH = 16

        def _shift2d(x, shift):
            l, r, t, b = shift
            H, W = (x.shape[2], x.shape[3])
            xp = jnp.pad(x, ((0, 0), (0, 0), (max(t, 0), max(b, 0)), (max(l, 0), max(r, 0))))
            h0 = max(-t, 0)
            w0 = max(-l, 0)
            return xp[:, :, h0:h0 + H, w0:w0 + W]
        shifts = ((1, -1, 0, 0), (-1, 1, 0, 0), (0, 0, 1, -1), (0, 0, -1, 1))
        xc = jnp.concatenate([x] + [_shift2d(x, s) for s in shifts], axis=1)
        B, C5, H, W = xc.shape
        p = PATCH
        h, w = (H // p, W // p)
        t = xc.reshape(B, C5, h, p, w, p)
        t = t.transpose(0, 2, 4, 3, 5, 1).reshape(B, h * w, p * p * C5)
        mu = jnp.mean(t, axis=-1, keepdims=True)
        var = jnp.mean(jnp.square(t - mu), axis=-1, keepdims=True)
        tn = (t - mu) * jax.lax.rsqrt(var + 1e-05) * ln_weight + ln_bias
        return jnp.einsum('bnk,dk->bnd', tn, proj_weight) + proj_bias

    def _L0_attn_ref(x, W_reduce, b_reduce, W_qkv, b_qkv, W_proj, b_proj):
        import jax, jax.numpy as jnp
        import numpy as np
        HEADS = 12
        SPLIT = 4
        B, N, C = x.shape
        C1 = C // 2
        H = HEADS
        hd = C1 // H
        seg = N // SPLIT
        xr = x @ W_reduce + b_reduce
        qkv = (xr @ W_qkv + b_qkv).reshape(B, N, 3, H, hd)
        q, k, v = (qkv[:, :, 0], qkv[:, :, 1], qkv[:, :, 2])

        def blk(t):
            return t.transpose(0, 2, 1, 3).reshape(B, H, SPLIT, seg, hd)
        qb, kb, vb = (blk(q), blk(k), blk(v))
        scale = hd ** (-0.5)
        scores = jnp.einsum('bhsqd,bhskd->bhsqk', qb, kb) * scale
        attn = jax.nn.softmax(scores, axis=-1)
        ob = jnp.einsum('bhsqk,bhskd->bhsqd', attn, vb)
        o = ob.transpose(0, 2, 3, 1, 4).reshape(B, N, C1)
        return o @ W_proj + b_proj

    def _L0_ffn_ref(x, w_router, wi, wo):
        import jax, jax.numpy as jnp
        import numpy as np
        NUM_EXPERTS = 8
        TOP_K = 2
        CAPACITY_FACTOR = 1.25
        MAX_GROUP_SIZE = 1024
        MIN_EXPERT_CAPACITY = 4

        def _moe_forward(x, w_router, wi, wo):
            B, T, D = x.shape
            E = NUM_EXPERTS
            num_tokens = B * T
            G = max(num_tokens // MAX_GROUP_SIZE, E)
            while num_tokens % G != 0 or G % E != 0:
                G += 1
            S = num_tokens // G
            C = max(int(TOP_K * CAPACITY_FACTOR * S / E), MIN_EXPERT_CAPACITY)
            xg = x.reshape(G, S, D)
            logits = jnp.einsum('gsd,de->gse', xg.astype(jnp.float32), w_router.astype(jnp.float32))
            probs = jax.nn.softmax(logits, axis=-1)
            gate, idx = jax.lax.top_k(probs, TOP_K)
            idx_kf = jnp.swapaxes(idx, 1, 2).reshape(G, TOP_K * S)
            mask = jax.nn.one_hot(idx_kf, E, dtype=jnp.int32)
            prio = jnp.cumsum(mask, axis=1) * mask - 1
            prio = jnp.swapaxes(prio.reshape(G, TOP_K, S, E), 1, 2)
            prio_se = prio.max(axis=2)
            gate_se = jnp.einsum('gsk,gske->gse', gate, jax.nn.one_hot(idx, E, dtype=gate.dtype))
            dispatch = jax.nn.one_hot(prio_se, C, dtype=x.dtype)
            combine = dispatch * gate_se[..., None].astype(x.dtype)
            expert_in = jnp.einsum('gsec,gsd->egcd', dispatch, xg)
            h = jax.nn.relu(jnp.einsum('egcd,edf->egcf', expert_in, wi))
            expert_out = jnp.einsum('egcf,efd->egcd', h, wo)
            out = jnp.einsum('gsec,egcd->gsd', combine, expert_out)
            return out.reshape(B, T, D)
        return _moe_forward(x, w_router, wi, wo)

    def _L1_attn_ref(x, w_qkv, w_proj, b_proj):
        import jax, jax.numpy as jnp
        import numpy as np
        DIM = 192
        HEADS = 12
        HEAD_DIM = DIM // HEADS
        EPS = 1e-12

        def _l1_normalize(t):
            denom = jnp.maximum(jnp.sum(jnp.abs(t), axis=-2, keepdims=True), EPS)
            return t / denom
        B, N, C = x.shape
        hd = C // HEADS
        qkv = x @ w_qkv.T
        qkv = qkv.reshape(B, N, 3, HEADS, hd).transpose(2, 0, 3, 1, 4)
        q, k, v = (qkv[0], qkv[1], qkv[2])
        q = _l1_normalize(q)
        k = _l1_normalize(k)
        if N < hd:
            out = jnp.einsum('bhnd,bhmd,bhme->bhne', q, k, v)
        else:
            kv = jnp.einsum('bhnd,bhne->bhde', k, v)
            out = jnp.einsum('bhnd,bhde->bhne', q, kv)
        out = out.transpose(0, 2, 1, 3).reshape(B, N, C)
        return out @ w_proj.T + b_proj

    def _L1_ffn_ref(X, slot_params, scale, W_down, b_down, W_up, b_up):
        import jax, jax.numpy as jnp
        import numpy as np
        EPS = 1e-06

        def l2_normalize(x, axis):
            norm = jnp.sqrt(jnp.square(x).sum(axis=axis, keepdims=True))
            return x * (1.0 / (norm + EPS))
        b, m, d = X.shape
        _, n, p = slot_params.shape
        Xn = l2_normalize(X, axis=-1)
        sp = l2_normalize(slot_params, axis=1) * scale
        logits = jnp.einsum('bmd,dnp->bmnp', Xn, sp)
        D = jax.nn.softmax(logits, axis=1)
        C = jax.nn.softmax(logits.reshape(b, m, n * p), axis=2).reshape(b, m, n, p)
        X_tilde = jnp.einsum('bmd,bmnp->bnpd', Xn, D)
        H = jax.nn.gelu(jnp.einsum('bnpd,ndh->bnph', X_tilde, W_down) + b_down[None, :, None, :], approximate=False)
        Y_tilde = jnp.einsum('bnph,nhd->bnpd', H, W_up) + b_up[None, :, None, :]
        Y = jnp.einsum('bnpd,bmnp->bmd', Y_tilde, C)
        return Y
    h = _L0_tok_ref(x, L0_tok_ln_weight, L0_tok_ln_bias, L0_tok_proj_weight, L0_tok_proj_bias)
    h = jnp.concatenate([h, txt], axis=1)
    h = h + _L0_attn_ref(_layernorm(h, axis=-1), L0_attn_W_reduce, L0_attn_b_reduce, L0_attn_W_qkv, L0_attn_b_qkv, L0_attn_W_proj, L0_attn_b_proj)
    h = h + _L0_ffn_ref(_layernorm(h, axis=-1), L0_ffn_w_router, L0_ffn_wi, L0_ffn_wo)
    h = h + _L1_attn_ref(_layernorm(h, axis=-1), L1_attn_w_qkv, L1_attn_w_proj, L1_attn_b_proj)
    h = h + _L1_ffn_ref(_layernorm(h, axis=-1), L1_ffn_slot_params, L1_ffn_scale, L1_ffn_W_down, L1_ffn_b_down, L1_ffn_W_up, L1_ffn_b_up)
    return h

_drawn_inputs = setup_inputs


def setup_inputs(seed=0):
    import zlib

    import numpy as np

    out = dict(_drawn_inputs(seed))
    spreads = {'L0_tok_ln_weight': (1.0, 0.2),
     'L0_tok_ln_bias': (0.0, 0.1),
     'L0_tok_proj_bias': (0.0, 0.1),
     'L0_attn_b_reduce': (0.0, 0.1),
     'L0_attn_b_qkv': (0.0, 0.1),
     'L0_attn_b_proj': (0.0, 0.1),
     'L1_attn_b_proj': (0.0, 0.1),
     'L1_ffn_b_down': (0.0, 0.488),
     'L1_ffn_b_up': (0.0, 0.276)}
    factors = {'L1_attn_w_qkv': 8.0,
     'L1_attn_w_proj': 8.0,
     'L1_ffn_slot_params': 8.0,
     'L1_ffn_W_down': 8.0,
     'L1_ffn_W_up': 3.334}
    for name, (base, spread) in spreads.items():
        noise = np.random.default_rng([zlib.crc32(name.encode()), seed]).standard_normal(out[name].shape)
        drawn = base * np.exp(spread * noise) if base else spread * noise
        out[name] = jnp.asarray(drawn.astype(out[name].dtype))
    for name, factor in factors.items():
        out[name] = (out[name] * factor).astype(out[name].dtype)
    return out
```

```python
from contextlib import ExitStack

import concourse.bass as bass
from concourse import mybir

ALU = mybir.AluOpType
ACT = mybir.ActivationFunctionType
F32 = mybir.dt.float32
AX_X = mybir.AxisListType.X

B, C, IMG, PATCH = 16, 3, 128, 16
SIDE = IMG // PATCH
IMG_TOK = SIDE * SIDE
TXT_TOK = 32
N = IMG_TOK + TXT_TOK
D = 192
HD = D // 2
PAIRS = B // 2
PATCH_DIM = PATCH * PATCH * 5 * C
K_IN = C * PATCH * PATCH
K_HALO = C * 4 * PATCH
KT_IN = K_IN // 128
KT = KT_IN + 2
HALO2 = K_HALO - 128
W_TILES = 5 * KT_IN + 1

C1, HEADS0, HDIM0, SEGS = 96, 12, 8, 4
SEG = N // SEGS
GRP = 4
NGRP = HEADS0 // GRP
PADSEG = 32
SCALE0 = float(HDIM0) ** -0.5

E, F = 8, 768
S = 2 * N
CAP = int(2 * 1.25 * S / E)
PADCAP = 64
FT = F // 128
SLOTS = PAIRS * CAP

NS, PS_, HS = 8, 4, 24
NP = NS * PS_

LN_EPS = 1e-5
L1_EPS = 1e-12
L2_EPS = 1e-6
TINY = 1e-18

CONSTS = [("ident", 128), ("ones", 128), ("tri", 96), ("l1mask", 96), ("iota", CAP), ("vmask", 32),
          ("upmask", 2 * NS), ("rev", E), ("mult", KT), ("headmask", GRP)]
CONST_AT, _at = {}, 0
for _n, _w in CONSTS:
    CONST_AT[_n] = (_at, _w)
    _at += _w
CONST_W = _at


def build(nc, xin, xhalo, txt, wtok, wtok2, lnw, lnb, tokbias, consts, wred, bred, wqkv0, bqkv0, wproj0, bproj0,
          wrouter, wi, wo, wq1, wkv1, wproj1, bproj1, slots, lscale, wdown, bdown, wup, bup, out):
    with ExitStack() as ctx:
        def sb(name, shape, dt=F32):
            return ctx.enter_context(nc.sbuf_tensor("sb_" + name, shape, dt))

        sems = {}

        def sem(name):
            if name not in sems:
                sems[name] = ctx.enter_context(nc.semaphore(name))
            return sems[name]

        PS = ctx.enter_context(nc.psum_tensor("banks", [128, 8, 512], F32))

        cst = sb("cst", [128, CONST_W])

        def const(name, rows=128):
            a, w = CONST_AT[name]
            return cst[0:rows, a:a + w]

        h = sb("h", [N, B, D])
        shared = sb("w_tok_e_out", [128, PAIRS * E // 2, D])
        w_tok = shared[:, 0:W_TILES]
        w_tok2 = sb("w_tok2", [HALO2, D])
        ln_w = sb("ln_w", [128, W_TILES + 1])
        ln_b = sb("ln_b", [128, W_TILES + 1])
        shared2 = sb("tok_xeT", [128, 2 * E * PAIRS * CAP])
        nx = 2 * KT * 128
        x_k = shared2[:, 0:nx].rearrange("k (q t n) -> k q t n", q=2, t=KT)
        x_sq = shared2[:, nx:2 * nx].rearrange("k (q t n) -> k q t n", q=2, t=KT)
        w_eff = shared2[:, 2 * nx:2 * nx + KT * (D + 1)].rearrange("k (t n) -> k t n", t=KT)
        tok_bias = sb("tok_bias", [128, D])
        bias_row = sb("bias_row", [128, D])
        col_sum = sb("col_sum", [128, D])
        tok_stat = sb("tok_stat", [128, 16])
        tok_mid = sb("tok_mid", [128, D])
        eps_col = sb("eps_col", [128, 2])
        w_red = sb("w_red", [HD, 2, C1])
        b_red = sb("b_red", [C1, 1])
        w_qkv0 = sb("w_qkv0", [C1, 3 * C1])
        b_qkv0 = sb("b_qkv0", [C1, 3])
        w_proj0 = sb("w_proj0", [C1, D])
        b_proj0 = sb("b_proj0", [N, D])
        stat6 = sb("stat6", [N, 4, 6])
        mv = sb("mv", [N, 4, 2])
        rs_tmp = sb("rs_tmp", [128, 8, 4])
        rs = sb("rs", [128, 4])
        xn = sb("xn", [N, 2, D])
        xnT = sb("xnT", [HD, 2, 2 * N])
        xrT = sb("xrT", [C1, 2 * N])
        xr_rep = sb("xr_rep", [C1, 2 * SEGS, GRP, SEG])
        qT = sb("qT", [C1, 2, SEGS, PADSEG])
        k_exp = sb("k_exp", [C1, GRP, 2 * N])
        v_exp = sb("v_exp", [GRP * SEG, 2, SEGS, C1])
        prob = sb("prob", [128, NGRP, 2, GRP * SEG])
        smax = sb("smax", [128, NGRP, 2 * GRP])
        ssum = sb("ssum", [128, NGRP, 2 * GRP])
        probT = sb("probT", [GRP * SEG, 2, NGRP, 128])
        oT = sb("oT", [C1, 2 * N])
        w_router = sb("w_router", [HD, 2, E])
        xn2 = sb("xn2", [N, B, D])
        logits = sb("logits", [N, B, E])
        r_top = sb("r_top", [N, 6, B])
        r_e = sb("r_e", [N, 6, B, E])
        slot_of = sb("slot_of", [N, B, E])
        gate_of = sb("gate_of", [N, B, E])
        x_disp = sb("x_disp", [N, 2, 2, D])
        shared3 = sb("onehot_slots", [N, 4 * E * CAP])
        onehot = shared3[:].rearrange("t (q p s) -> t q p s", q=2, p=2)
        xeT = shared2[0:HD].rearrange("k (a e g c) -> k a e g c", a=2, e=E, g=PAIRS)
        wi_sl = sb("wi_sl", [HD, 2, 2, F])
        wo_sl = sb("wo_sl", [128, 2, FT, D])
        hidT = sb("hidT", [128, 2, FT, SLOTS])
        e_out = shared[:].rearrange("s (g e) d -> s g e d", g=PAIRS)
        comb = sb("comb", [N, 2, E, PADCAP])
        combT = sb("combT", [128, 2, E // 2, N])
        w_q1 = sb("w_q1", [HD, 2, D])
        w_kv1 = sb("w_kv1", [HD, 2, 2 * D])
        w_proj1 = sb("w_proj1", [HD, 2, D])
        b_proj1 = sb("b_proj1", [N, D])
        q1T = sb("q1T", [HD, 2, 2 * N])
        kv1 = sb("kv1", [N, 2, 2 * D])
        abs_k = sb("abs_k", [N, 2, D])
        den = sb("den", [HD, 6, 4])
        kv_bd = sb("kv_bd", [HD, 2, 2, HD])
        o1T = sb("o1T", [HD, 2, 2, N])
        slot_raw = sb("slot_raw", [HD, 2, NP])
        slot_sq = sb("slot_sq", [HD, 2, NP])
        slot_n = sb("slot_n", [HD, 2, NP])
        slot_s = sb("slot_s", [HD, 6, 2 * PS_])
        l_scale = sb("l_scale", [HD, 1])
        w_down = sb("w_down", [HD, 2, D])
        b_down = sb("b_down", [HD, 2])
        w_up = sb("w_up", [HD, 2, D])
        b_up = sb("b_up", [128, D])
        xs = sb("xs", [N, 4, D])
        xsT = sb("xsT", [HD, 2, 4 * N])
        cmb = sb("cmb", [N, 4, NP])
        c_st = sb("c_st", [N, 3, 4])
        cmbT = sb("cmbT", [128, 4, N])
        dspT = sb("dspT", [128, N])
        d_st = sb("d_st", [128, 3])
        dsp = sb("dsp", [N, 4 * NP])
        x_tT = shared3[:, 0:2 * B * NP].rearrange("k (a s) -> k a s", a=2)
        hidS = sb("hidS", [HD, 2, B * NP])
        y_t = shared2[:, 0:4 * D].rearrange("s (j d) -> s j d", j=4)

        ident = const("ident")
        ones = const("ones")

        def stand(eng):
            eng.sem_inc(sem("carried_" + ("ve" if eng is nc.vector else "pe")), 1)

        def flip(dst, src):
            rows = src.shape[0]
            return nc.tensor.transpose(dst, src, ident[0:rows, 0:rows])

        block = ctx.enter_context(nc.Block())

        @block.sync
        def _(sp):
            sp.dma_start(cst[:], consts).then_inc(sem("cst_in"), 16)
            sp.dma_start(ln_w[:], lnw).then_inc(sem("lnwb_in"), 16)
            sp.dma_start(ln_b[:], lnb).then_inc(sem("lnwb_in"), 16)
            sp.dma_start(tok_bias[:], tokbias.partition_broadcast(128)).then_inc(sem("tokbias_in"), 16)
            for c in range(3):
                a, b = c * 10, (c + 1) * 10 + (c == 2)
                sp.dma_start(w_tok[:, a:b], wtok[:, a:b]).then_inc(sem(f"wtok_in{c}"), 16)
            sp.dma_start(w_tok2[:], wtok2).then_inc(sem("wtok2_in"), 16)
            sp.dma_start(h[IMG_TOK:N], txt.rearrange("b t d -> t b d")).then_inc(sem("txt_in"), 16)
            for q in range(2):
                sp.dma_start(x_k[:, q, 0:KT - 1], xin[q]).then_inc(sem(f"x_in{q}"), 16)
                sp.dma_start(x_k[0:HALO2, q, KT - 1], xhalo[q]).then_inc(sem(f"x_in{q}"), 16)
            with sp.Fori(1, PAIRS // 2) as i:
                for q in range(2):
                    sp.wait_ge(sem("tok_ps"), i * 2 + (q - 1))
                    sp.dma_start(x_k[:, q, 0:KT - 1], xin[bass.ds(i * 2 + q, 1)]).then_inc(sem(f"x_in{q}"), 16)
                    sp.dma_start(x_k[0:HALO2, q, KT - 1], xhalo[bass.ds(i * 2 + q, 1)]).then_inc(sem(f"x_in{q}"), 16)
            n = 0
            for dst, src in [(w_red[:], wred), (b_red[:], bred), (w_qkv0[:], wqkv0), (b_qkv0[:], bqkv0),
                             (w_proj0[:], wproj0), (b_proj0[:], bproj0.partition_broadcast(N)),
                             (w_router[:], wrouter)]:
                sp.dma_start(dst, src).then_inc(sem("attn0_in"), 16)
            for dst, src in [(w_q1[:], wq1), (w_kv1[:], wkv1), (w_proj1[:], wproj1),
                             (b_proj1[:], bproj1.partition_broadcast(N)), (slot_raw[:], slots),
                             (l_scale[:], lscale.partition_broadcast(HD)), (w_down[:], wdown), (b_down[:], bdown),
                             (w_up[:], wup), (b_up[:], bup)]:
                sp.dma_start(dst, src).then_inc(sem("layer1_in"), 16)
            with sp.Fori(0, E // 2) as i:
                for q in range(2):
                    sp.wait_ge(sem("eo_ps"), i * 4 + 2 * q + 2)
                    sp.dma_start(wi_sl[:, q], wi[bass.ds(i * 2 + q, 1)]).then_inc(sem(f"wexp_in{q}"), 16)
                    sp.dma_start(wo_sl[:, q], wo[bass.ds(i * 2 + q, 1)]).then_inc(sem(f"wexp_in{q}"), 16)
            out_v = out.rearrange("b t d -> t b d")
            for b in range(0, B, 4):
                sp.wait_ge(sem("y_added"), b + 4)
                sp.dma_start(out_v[:, b:b + 4], h[:, b:b + 4]).then_inc(sem("stored"), 16)
            sp.wait_ge(sem("stored"), 16 * (B // 4))

        @block.gpsimd
        def _(gp):
            gp.memset(qT[:], 0.0).then_inc(sem("pads_zero"), 1)
            gp.memset(comb[:], 0.0).then_inc(sem("pads_zero"), 1)
            gp.wait_ge(sem("w_eff"), KT)
            gp.wait_ge(sem("bias_row_ps"), 1)
            gp.memset(shared[:], 0.0).then_inc(sem("pads_zero"), 1)
            gp.wait_ge(sem("cst_in"), 16)
            gp.tensor_copy(w_eff[:, :, D], const("mult")).then_inc(sem("mult_ready"), 1)
            gp.wait_ge(sem("attn0_in"), 16 * 7)
            with gp.Fori(0, PAIRS) as i:
                gp.wait_ge(sem("a_xn"), i * 2 + 2)
                for p in range(2):
                    hp = h[:, bass.ds(i * 2 + p, 1), :]
                    gp.tensor_tensor(hp, hp, b_proj0[:].unsqueeze(1), ALU.add).then_inc(sem("h_biased"), 1)
                gp.wait_ge(sem("r_xn"), i * 2 + 2)
                gp.tensor_copy(xn2[:, bass.ds(i * 2, 2), :], xn[:]).then_inc(sem("r_kept"), 1)
            with gp.Fori(0, PAIRS // 2) as i:
                for q in range(2):
                    gp.wait_ge(sem("disp_ps"), i * 4 + 2 * q + 2)
                    if q == 0:
                        gp.wait_ge(sem("r_kept"), PAIRS)
                    gp.tensor_copy(x_disp[:, q], xn2[:, bass.ds(i * 4 + 2 * q, 2), :]).then_inc(sem("xdisp"), 1)
            gp.wait_ge(sem("layer1_in"), 16 * 10)
            with gp.Fori(0, PAIRS) as i:
                gp.wait_ge(sem("b_xn"), i * 2 + 2)
                for p in range(2):
                    hp = h[:, bass.ds(i * 2 + p, 1), :]
                    gp.tensor_tensor(hp, hp, b_proj1[:].unsqueeze(1), ALU.add).then_inc(sem("h_biased"), 1)

        @block.tensor
        def _(pe):
            pe.sem_inc(sem("disp_ps"), 4)
            pe.sem_inc(sem("eo_ps"), 4)
            pe.wait_ge(sem("lnwb_in"), 32)
            for t in range(W_TILES):
                if t % 10 == 0 and t < 30:
                    pe.wait_ge(sem(f"wtok_in{t // 10}"), 16)
                nc.tensor.matmul(PS[:, 0, 0:D], ln_b[:, t:t + 1].to_broadcast([128, 128]), w_tok[:, t],
                                 start=(t == 0), stop=False)
            pe.wait_ge(sem("wtok2_in"), 16)
            nc.tensor.matmul(PS[:, 0, 0:D], ln_b[0:HALO2, W_TILES:W_TILES + 1].to_broadcast([HALO2, 128]), w_tok2[:],
                             start=False, stop=True).then_inc(sem("bias_row_ps"), 1)
            pe.wait_ge(sem("w_eff"), KT)
            for t in range(KT):
                rows = 128 if t < KT - 1 else HALO2
                mm = nc.tensor.matmul(PS[:, 1, 0:D], ones[0:rows], w_eff[0:rows, t, 0:D], start=(t == 0), stop=(t == KT - 1))
            mm.then_inc(sem("col_sum_ps"), 1)
            pe.wait_ge(sem("mult_ready"), 1)
            with pe.Fori(0, PAIRS // 2) as i:
                for q in range(2):
                    pe.wait_ge(sem(f"x_in{q}"), i * 32 + 32)
                    pe.wait_ge(sem("tok_mid"), i * 2 + q + 1)
                    for t in range(KT):
                        rows = 128 if t < KT - 1 else HALO2
                        nc.tensor.matmul(PS[:, 2 + q, 0:D + 1], x_k[0:rows, q, t], w_eff[0:rows, t],
                                         start=(t == 0), stop=(t == KT - 1))
                    pe.wait_ge(sem("x_sq"), i * 2 + q + 1)
                    for t in range(KT):
                        rows = 128 if t < KT - 1 else HALO2
                        mm = nc.tensor.matmul(PS[:, 2 + q, 200:201], x_sq[0:rows, q, t], const("mult")[0:rows, t:t + 1],
                                              start=(t == 0), stop=(t == KT - 1))
                    mm.then_inc(sem("tok_ps"), 1)

            pe.wait_ge(sem("attn0_in"), 16 * 7)
            pe.wait_ge(sem("pads_zero"), 3)
            with pe.Fori(0, PAIRS) as i:
                pe.wait_ge(sem("a_xn"), i * 2 + 2)
                for p in range(2):
                    for kh in range(2):
                        mm = flip(PS[0:HD, 0, (kh * 2 + p) * N:(kh * 2 + p + 1) * N], xn[:, p, kh * HD:(kh + 1) * HD])
                mm.then_inc(sem("a_xnT_ps"), 1)
                pe.wait_ge(sem("a_xnT"), i + 1)
                for kh in range(2):
                    mm = nc.tensor.matmul(PS[0:C1, 1, 0:2 * N], w_red[:, kh], xnT[:, kh], start=(kh == 0), stop=(kh == 1))
                mm.then_inc(sem("a_xr_ps"), 1)
                pe.wait_ge(sem("a_xrT"), i * 2 + 1)
                for j in range(2):
                    mm = nc.tensor.matmul(PS[0:C1, 2, j * 2 * N:(j + 1) * 2 * N], w_qkv0[:, j * C1:(j + 1) * C1], xrT[:],
                                          start=True, stop=True)
                mm.then_inc(sem("a_qk_ps"), 1)
                pe.wait_ge(sem("a_xrT"), i * 2 + 2)
                for p in range(2):
                    for s in range(SEGS):
                        mm = nc.tensor.matmul(PS[0:GRP * SEG, 3 + p, s * C1:(s + 1) * C1],
                                              xr_rep[:, p * SEGS + s].rearrange("c r t -> c (r t)"), w_qkv0[:, 2 * C1:3 * C1],
                                              start=True, stop=True)
                    mm.then_inc(sem("a_v_ps"), 1)
                pe.wait_ge(sem("a_qT"), i + 1)
                pe.wait_ge(sem("a_kexp"), i + 1)
                stand(pe)
                for g in range(NGRP):
                    rows = slice(g * 32, g * 32 + 32)
                    for p in range(2):
                        for s in range(SEGS):
                            mm = nc.tensor.matmul(
                                PS[s * 32:s * 32 + 32, 5 + g, p * GRP * SEG:(p + 1) * GRP * SEG], qT[rows, p, s],
                                k_exp[rows, :, p * N + s * SEG:p * N + (s + 1) * SEG], start=True, stop=True)
                mm.then_inc(sem("a_s_ps"), 1)
                for p in range(2):
                    pe.wait_ge(sem("a_prob"), i + 1)
                    pe.wait_ge(sem("a_vexp"), i * 2 + p + 1)
                    for g in range(NGRP):
                        mm = flip(PS[0:GRP * SEG, 3 + p, g * 128:(g + 1) * 128], prob[:, g, p])
                    mm.then_inc(sem("a_probT_ps"), 1)
                for p in range(2):
                    pe.wait_ge(sem("a_probT"), i * 2 + p + 1)
                    for s in range(SEGS):
                        for g in range(NGRP):
                            mm = nc.tensor.matmul(
                                PS[g * 32:g * 32 + 32, 2, p * N + s * SEG:p * N + (s + 1) * SEG],
                                v_exp[:, p, s, g * 32:g * 32 + 32], probT[:, p, g, s * PADSEG:s * PADSEG + SEG],
                                start=True, stop=True)
                mm.then_inc(sem("a_oT_ps"), 1)
                pe.wait_ge(sem("a_oT"), i + 1)
                for p in range(2):
                    mm = nc.tensor.matmul(PS[0:N, 0, p * D:(p + 1) * D], oT[:, p * N:(p + 1) * N], w_proj0[:],
                                          start=True, stop=True)
                mm.then_inc(sem("a_proj_ps"), 1)
                pe.wait_ge(sem("r_xn"), i * 2 + 2)
                for p in range(2):
                    for kh in range(2):
                        mm = flip(PS[0:HD, 1, (kh * 2 + p) * N:(kh * 2 + p + 1) * N], xn[:, p, kh * HD:(kh + 1) * HD])
                mm.then_inc(sem("r_xnT_ps"), 1)
                pe.wait_ge(sem("r_xnT"), i + 1)
                for p in range(2):
                    for kh in range(2):
                        mm = nc.tensor.matmul(PS[0:N, 2, p * E:(p + 1) * E], xnT[:, kh, p * N:(p + 1) * N], w_router[:, kh],
                                              start=(kh == 0), stop=(kh == 1))
                mm.then_inc(sem("r_logit_ps"), 1)

            pe.wait_ge(sem("r_choice"), 2)
            tri, one96 = const("tri", N), ones[0:N, 0:N]
            first, second = r_e[:, 2].rearrange("t (g p) e -> t p g e", p=2), r_e[:, 4].rearrange("t (g p) e -> t p g e", p=2)
            for k, p, terms in [(0, 0, [(tri, first[:, 0])]),
                                (0, 1, [(one96, first[:, 0]), (tri, first[:, 1])]),
                                (1, 0, [(one96, first[:, 0]), (one96, first[:, 1]), (tri, second[:, 0])]),
                                (1, 1, [(one96, first[:, 0]), (one96, first[:, 1]), (one96, second[:, 0]),
                                        (tri, second[:, 1])])]:
                dst = PS[0:N, 3, (k * 2 + p) * PAIRS * E:(k * 2 + p + 1) * PAIRS * E]
                for j, (lhs, rhs) in enumerate(terms):
                    mm = nc.tensor.matmul(dst, lhs, rhs, start=(j == 0), stop=(j == len(terms) - 1))
            mm.then_inc(sem("r_count_ps"), 1)

            with pe.Fori(0, PAIRS // 2) as i:
                for q in range(2):
                    pe.wait_ge(sem("xdisp"), i * 2 + q + 1)
                    pe.wait_ge(sem("onehot"), i * 4 + 2 * q + 2)
                    pe.wait_ge(sem("xeT"), i * 4 + 2 * q + 2)
                    for dh in range(2):
                        for p in range(2):
                            mm = nc.tensor.matmul(PS[0:HD, 4 + 2 * q + dh, 0:E * CAP],
                                                  x_disp[:, q, p, dh * HD:(dh + 1) * HD], onehot[:, q, p],
                                                  start=(p == 0), stop=(p == 1))
                        mm.then_inc(sem("disp_ps"), 1)

            pe.wait_ge(sem("xeT"), 2 * PAIRS + 4)
            with pe.Fori(0, E // 2) as i:
                for q in range(2):
                    pe.wait_ge(sem(f"wexp_in{q}"), i * 32 + 32)
                    for f in range(FT):
                        pe.wait_ge(sem("hidT"), i * 2 * FT + q * FT + f + 1)
                        for kh in range(2):
                            mm = nc.tensor.matmul(PS[:, f % 2, 0:SLOTS], wi_sl[:, q, kh, f * 128:(f + 1) * 128],
                                                  xeT[:, kh, bass.ds(i * 2 + q, 1)].rearrange("k e g c -> k (e g c)"),
                                                  start=(kh == 0), stop=(kh == 1))
                        mm.then_inc(sem("hid_ps"), 1)
                    for half in range(2):
                        pe.wait_ge(sem("e_out"), i * 8 + 4 * q + 2 * half + 2)
                        for gp_ in range(2):
                            for f in range(FT):
                                if half == 0 and gp_ == 0:
                                    pe.wait_ge(sem("hidT"), i * 2 * FT + q * FT + f + 3)
                                for z in range(2):
                                    g = half * 4 + gp_ * 2 + z
                                    mm = nc.tensor.matmul(PS[64 * z:64 * z + CAP, 2 + half, gp_ * D:(gp_ + 1) * D],
                                                          hidT[:, q, f, g * CAP:(g + 1) * CAP], wo_sl[:, q, f],
                                                          start=(f == 0), stop=(f == FT - 1), skip_group_check=True)
                        mm.then_inc(sem("eo_ps"), 1)

            pe.wait_ge(sem("e_out"), 4 * E + 4)
            pe.wait_ge(sem("layer1_in"), 16 * 10)
            with pe.Fori(0, PAIRS) as i:
                for p in range(2):
                    pe.wait_ge(sem("comb"), i * 2 + p + 1)
                    for ep in range(E // 2):
                        mm = flip(PS[:, p, ep * N:(ep + 1) * N], comb[:, p, 2 * ep:2 * ep + 2].rearrange("t e c -> t (e c)"))
                    mm.then_inc(sem("combT_ps"), 1)
                for p in range(2):
                    pe.wait_ge(sem("combT"), i * 2 + p + 1)
                    for ep in range(E // 2):
                        mm = nc.tensor.matmul(PS[0:N, 2, p * D:(p + 1) * D], combT[:, p, ep],
                                              e_out[:, bass.ds(i, 1), ep].rearrange("s g d -> s (g d)"),
                                              start=(ep == 0), stop=(ep == E // 2 - 1))
                mm.then_inc(sem("moe_ps"), 1)
                pe.wait_ge(sem("b_xn"), i * 2 + 2)
                for p in range(2):
                    for kh in range(2):
                        mm = flip(PS[0:HD, 3, (kh * 2 + p) * N:(kh * 2 + p + 1) * N], xn[:, p, kh * HD:(kh + 1) * HD])
                mm.then_inc(sem("b_xnT_ps"), 1)
                pe.wait_ge(sem("b_xnT"), i + 1)
                for p in range(2):
                    for kh in range(2):
                        mm = nc.tensor.matmul(PS[0:N, 5 + p, 0:2 * D], xnT[:, kh, p * N:(p + 1) * N], w_kv1[:, kh],
                                              start=(kh == 0), stop=(kh == 1))
                    mm.then_inc(sem("b_kv_ps"), 1)
                for mh in range(2):
                    for kh in range(2):
                        mm = nc.tensor.matmul(PS[0:HD, 4, mh * 2 * N:(mh + 1) * 2 * N], w_q1[:, kh, mh * HD:(mh + 1) * HD],
                                              xnT[:, kh], start=(kh == 0), stop=(kh == 1))
                mm.then_inc(sem("b_q_ps"), 1)
                for p in range(2):
                    pe.wait_ge(sem("b_kv"), i * 2 + p + 1)
                    for mh in range(2):
                        mm = nc.tensor.matmul(PS[0:HD, 3, (p * 2 + mh) * HD:(p * 2 + mh + 1) * HD],
                                              kv1[:, p, mh * HD:(mh + 1) * HD], kv1[:, p, D + mh * HD:D + (mh + 1) * HD],
                                              start=True, stop=True)
                    pe.wait_ge(sem("b_absk"), i * 2 + p + 1)
                    for mh in range(2):
                        mm = nc.tensor.matmul(PS[0:HD, 7, p * 2 + mh:p * 2 + mh + 1], abs_k[:, p, mh * HD:(mh + 1) * HD],
                                              ones[0:N, 0:1], start=True, stop=True)
                mm.then_inc(sem("b_kvp_ps"), 1)
                pe.wait_ge(sem("b_kvbd"), i * 4 + 4)
                pe.wait_ge(sem("b_q1T"), i + 1)
                for p in range(2):
                    for mh in range(2):
                        mm = nc.tensor.matmul(PS[0:HD, 4, (p * 2 + mh) * N:(p * 2 + mh + 1) * N], kv_bd[:, p, mh],
                                              q1T[:, mh, p * N:(p + 1) * N], start=True, stop=True)
                mm.then_inc(sem("b_oT_ps"), 1)
                pe.wait_ge(sem("b_o1T"), i + 1)
                for p in range(2):
                    for mh in range(2):
                        mm = nc.tensor.matmul(PS[0:N, 2, p * D:(p + 1) * D], o1T[:, p, mh], w_proj1[:, mh],
                                              start=(mh == 0), stop=(mh == 1))
                mm.then_inc(sem("b_proj_ps"), 1)

            pe.wait_ge(sem("slot_n"), 2)
            with pe.Fori(0, 4) as i:
                for p in range(4):
                    pe.wait_ge(sem("s_xs"), i * 4 + p + 1)
                    for kh in range(2):
                        mm = flip(PS[0:HD, kh, p * N:(p + 1) * N], xs[:, p, kh * HD:(kh + 1) * HD])
                mm.then_inc(sem("s_xsT_ps"), 1)
                pe.wait_ge(sem("s_xsT"), i * 2 + 2)
                for p in range(4):
                    for kh in range(2):
                        mm = nc.tensor.matmul(PS[0:N, 2, p * NP:(p + 1) * NP], xsT[:, kh, p * N:(p + 1) * N], slot_n[:, kh],
                                              start=(kh == 0), stop=(kh == 1))
                mm.then_inc(sem("s_log_ps"), 1)
                for kh in range(2):
                    for p in range(4):
                        mm = nc.tensor.matmul(PS[p * NP:(p + 1) * NP, 3, 0:N], slot_n[:, kh], xsT[:, kh, p * N:(p + 1) * N],
                                              start=(kh == 0), stop=(kh == 1), skip_group_check=True)
                mm.then_inc(sem("s_logT_ps"), 1)
                pe.wait_ge(sem("s_dspT"), i + 1)
                flip(PS[0:N, 4, 0:128], dspT[:]).then_inc(sem("s_dsp_ps"), 1)
                pe.wait_ge(sem("s_cmb"), i + 1)
                flip(PS[:, 5, 0:N], cmb[:].rearrange("t p n -> t (p n)")).then_inc(sem("s_cmbT_ps"), 1)
                pe.wait_ge(sem("s_dsp"), i + 1)
                for p in range(4):
                    for dh in range(2):
                        mm = nc.tensor.matmul(PS[0:HD, 6, dh * 128 + p * NP:dh * 128 + (p + 1) * NP],
                                              xs[:, p, dh * HD:(dh + 1) * HD], dsp[:, p * NP:(p + 1) * NP],
                                              start=True, stop=True)
                mm.then_inc(sem("s_xt_ps"), 1)
            pe.wait_ge(sem("s_xtT"), 4)
            for mh in range(2):
                for kh in range(2):
                    mm = nc.tensor.matmul(PS[0:HD, mh], w_down[:, kh, mh * HD:(mh + 1) * HD], x_tT[:, kh],
                                          start=(kh == 0), stop=(kh == 1))
                mm.then_inc(sem("s_hid_ps"), 1)
            pe.wait_ge(sem("s_hidm"), 2)
            for j in range(4):
                if j >= 2:
                    pe.wait_ge(sem("s_yt"), j - 1)
                for mh in range(2):
                    mm = nc.tensor.matmul(PS[:, 2 + j % 2, 0:D], hidS[:, mh, j * 128:(j + 1) * 128], w_up[:, mh],
                                          start=(mh == 0), stop=(mh == 1))
                mm.then_inc(sem("s_yt_ps"), 1)
            for b in range(B):
                j, p = b // 4, b % 4
                pe.wait_ge(sem("s_yt"), j + 1)
                if b >= 4:
                    pe.wait_ge(sem("y_added"), b - 3)
                rows = slice(p * NP, (p + 1) * NP)
                nc.tensor.matmul(PS[0:N, 4 + b % 4, 0:D], cmbT[rows, j], y_t[rows, j], start=True,
                                 stop=True).then_inc(sem("s_y_ps"), 1)

        @block.scalar
        def _(act):
            def rsqrt_seed(var, tmp, dst, eps, done):
                nc.scalar.activation(tmp, var, ACT.Ln, bias=eps).then_inc(sem("act_ln"), 1)
                act.wait_ge(sem("act_ln"), done)
                return nc.scalar.activation(dst, tmp, ACT.Exp, scale=-0.5)

            act.sem_inc(sem("xeT"), 4)
            act.sem_inc(sem("hidT"), 2)
            eps = eps_col[:, 0:1]
            act.preload_act_table_set("natural_log_exp_and_others")
            act.wait_ge(sem("eps_ready"), 2)
            with act.Fori(0, PAIRS // 2) as i:
                for q in range(2):
                    act.wait_ge(sem(f"x_in{q}"), i * 32 + 32)
                    nc.scalar.activation(x_sq[:, q, 0:KT - 1], x_k[:, q, 0:KT - 1], ACT.Square)
                    nc.scalar.activation(x_sq[0:HALO2, q, KT - 1], x_k[0:HALO2, q, KT - 1], ACT.Square).then_inc(sem("x_sq"), 1)
                    act.wait_ge(sem("tok_var"), i * 2 + q + 1)
                    rsqrt_seed(tok_stat[:, 3:4], tok_stat[:, 4:5], tok_stat[:, 5:6], eps,
                               i * 2 + q + 1).then_inc(sem("tok_seed"), 1)
            LN0 = PAIRS
            act.wait_ge(sem("attn0_in"), 16 * 7)
            act.wait_ge(sem("pads_zero"), 3)
            with act.Fori(0, PAIRS) as i:
                act.wait_ge(sem("a_mv"), i * 2 + 2)
                rsqrt_seed(mv[:, 0:2, 1], rs_tmp[0:N, 0, 0:2], rs_tmp[0:N, 1, 0:2], eps[0:N],
                           i * 2 + LN0 + 1).then_inc(sem("a_seed"), 1)
                act.wait_ge(sem("a_xnT_ps"), i + 1)
                nc.scalar.copy(xnT[:].rearrange("k a t -> k (a t)"), PS[0:HD, 0, 0:4 * N]).then_inc(sem("a_xnT"), 1)
                act.wait_ge(sem("a_xr_ps"), i + 1)
                nc.scalar.activation(xrT[:], PS[0:C1, 1, 0:2 * N], ACT.Identity, bias=b_red[:]).then_inc(sem("a_xrT"), 1)
                nc.scalar.activation(xr_rep[:], PS[0:C1, 1, 0:2 * N].rearrange("c (a t) -> c a t", t=SEG).unsqueeze(2)
                                     .to_broadcast([C1, 2 * SEGS, GRP, SEG]), ACT.Identity, bias=b_red[:]
                                     ).then_inc(sem("a_xrT"), 1)
                act.wait_ge(sem("a_kexp"), i + 1)
                nc.scalar.activation(qT[:, :, :, 0:SEG], PS[0:C1, 2, 0:2 * N].rearrange("c (p s t) -> c p s t", p=2, s=SEGS),
                                     ACT.Identity, bias=b_qkv0[:, 0:1]).then_inc(sem("a_qT"), 1)
                act.wait_ge(sem("a_sub"), i + 1)
                nc.scalar.activation(prob[:], prob[:], ACT.Exp, scale=SCALE0).then_inc(sem("a_exp"), 1)
                for p in range(2):
                    act.wait_ge(sem("a_probT_ps"), i * 2 + p + 1)
                    nc.scalar.copy(probT[:, p].rearrange("k g t -> k (g t)"),
                                   PS[0:GRP * SEG, 3 + p, 0:NGRP * 128]).then_inc(sem("a_probT"), 1)
                act.wait_ge(sem("a_oT_ps"), i + 1)
                nc.scalar.activation(oT[:], PS[0:C1, 2, 0:2 * N], ACT.Identity, bias=b_qkv0[:, 2:3]).then_inc(sem("a_oT"), 1)
                act.wait_ge(sem("r_mv"), i * 2 + 2)
                rsqrt_seed(mv[:, 0:2, 1], rs_tmp[0:N, 0, 0:2], rs_tmp[0:N, 1, 0:2], eps[0:N],
                           i * 2 + LN0 + 2).then_inc(sem("r_seed"), 1)
                act.wait_ge(sem("r_xnT_ps"), i + 1)
                nc.scalar.copy(xnT[:].rearrange("k a t -> k (a t)"), PS[0:HD, 1, 0:4 * N]).then_inc(sem("r_xnT"), 1)
                act.wait_ge(sem("r_logit_ps"), i + 1)
                nc.scalar.copy(logits[:, bass.ds(i * 2, 2), :], PS[0:N, 2, 0:2 * E].rearrange("t (p e) -> t p e", p=2)
                               ).then_inc(sem("r_logit"), 1)
            LN1 = LN0 + 2 * PAIRS
            act.wait_ge(sem("r_shift"), 1)
            nc.scalar.activation(r_e[:, 1], r_e[:, 0], ACT.Exp).then_inc(sem("r_exp"), 1)
            with act.Fori(0, PAIRS // 2) as i:
                for q in range(2):
                    for dh in range(2):
                        act.wait_ge(sem("disp_ps"), i * 4 + 2 * q + dh + 5)
                        nc.scalar.copy(xeT[:, dh, :, bass.ds(i * 2 + q, 1)].rearrange("k e g c -> k e (g c)"),
                                       PS[0:HD, 4 + 2 * q + dh, 0:E * CAP].rearrange("k (e c) -> k e c", e=E)
                                       ).then_inc(sem("xeT"), 1)
            with act.Fori(0, E // 2) as i:
                for q in range(2):
                    for f in range(FT):
                        act.wait_ge(sem("hid_ps"), i * 2 * FT + q * FT + f + 1)
                        if f == 0:
                            act.wait_ge(sem("eo_ps"), i * 4 + 2 * q + 2)
                        nc.scalar.activation(hidT[:, q, f], PS[:, f % 2, 0:SLOTS], ACT.Relu).then_inc(sem("hidT"), 1)
            with act.Fori(0, PAIRS) as i:
                for p in range(2):
                    act.wait_ge(sem("combT_ps"), i * 2 + p + 1)
                    nc.scalar.copy(combT[:, p].rearrange("s e t -> s (e t)"), PS[:, p, 0:E // 2 * N]).then_inc(sem("combT"), 1)
                act.wait_ge(sem("b_mv"), i * 2 + 2)
                rsqrt_seed(mv[:, 0:2, 1], rs_tmp[0:N, 0, 0:2], rs_tmp[0:N, 1, 0:2], eps[0:N],
                           i + LN1 + 1).then_inc(sem("b_seed"), 1)
                act.wait_ge(sem("b_xnT_ps"), i + 1)
                nc.scalar.copy(xnT[:].rearrange("k a t -> k (a t)"), PS[0:HD, 3, 0:4 * N]).then_inc(sem("b_xnT"), 1)
                for p in range(2):
                    act.wait_ge(sem("b_kv"), i * 2 + p + 1)
                    nc.scalar.activation(abs_k[:, p], PS[0:N, 5 + p, 0:D], ACT.Abs).then_inc(sem("b_absk"), 1)
                act.wait_ge(sem("b_q_ps"), i + 1)
                nc.scalar.copy(q1T[:].rearrange("k a t -> k (a t)"), PS[0:HD, 4, 0:4 * N]).then_inc(sem("b_q1T"), 1)
                act.wait_ge(sem("b_oT_ps"), i + 1)
                nc.scalar.copy(o1T[:].rearrange("k p a t -> k (p a t)"), PS[0:HD, 4, 0:4 * N]).then_inc(sem("b_o1T"), 1)
            LN2 = LN1 + PAIRS
            act.wait_ge(sem("slot_ss"), 1)
            rsqrt_seed(slot_s[:, 0], slot_s[:, 1], slot_s[:, 2], 0.0, LN2 + 1).then_inc(sem("slot_seed"), 1)
            LN3 = LN2 + 1
            with act.Fori(0, 4) as i:
                act.wait_ge(sem("s_mv"), i * 4 + 4)
                rsqrt_seed(mv[:, :, 1], rs_tmp[0:N, 0], rs_tmp[0:N, 1], eps[0:N], i * 2 + LN3 + 1).then_inc(sem("s_seed"), 1)
                act.wait_ge(sem("s_varmax"), i + 1)
                rsqrt_seed(rs_tmp[0:N, 5], rs_tmp[0:N, 6], rs_tmp[0:N, 7], 0.0, i * 2 + LN3 + 2).then_inc(sem("s_seed"), 1)
                act.wait_ge(sem("s_xsT_ps"), i + 1)
                for kh in range(2):
                    nc.scalar.copy(xsT[:, kh], PS[0:HD, kh, 0:4 * N]).then_inc(sem("s_xsT"), 1)
                act.wait_ge(sem("s_dmax"), i + 1)
                nc.scalar.activation(dspT[:], PS[:, 3, 0:N], ACT.Exp, bias=d_st[:, 0:1],
                                     accum_out=d_st[:, 1:2]).then_inc(sem("s_dexp"), 1)
                act.wait_ge(sem("s_csub"), i + 1)
                nc.scalar.activation(cmb[:], cmb[:], ACT.Exp).then_inc(sem("s_cexp"), 1)
                act.wait_ge(sem("s_dsp_ps"), i + 1)
                nc.scalar.copy(dsp[:], PS[0:N, 4, 0:128]).then_inc(sem("s_dsp"), 1)
                act.wait_ge(sem("s_cmbT_ps"), i + 1)
                nc.scalar.copy(cmbT[:, bass.ds(i, 1), :], PS[:, 5:6, 0:N]).then_inc(sem("s_cmbT"), 1)
                act.wait_ge(sem("s_xt_ps"), i + 1)
                nc.scalar.copy(x_tT[:, :, bass.ds(i * 128, 128)], PS[0:HD, 6, 0:256].rearrange("k (a s) -> k a s", a=2)
                               ).then_inc(sem("s_xtT"), 1)
            for mh in range(2):
                act.wait_ge(sem("s_hid_ps"), mh + 1)
                nc.scalar.activation(hidS[:, mh], PS[0:HD, mh], ACT.Gelu, bias=b_down[:, mh:mh + 1]).then_inc(sem("s_gelu"), 1)

        @block.vector
        def _(ve):

            def refine(var, eps, seed, t, dst, base, per, i, k):
                def tick(ins, j):
                    ins.then_inc(sem("dve_newton"), 1)
                    ve.wait_ge(sem("dve_newton"), i * (4 * per) + (base + 4 * k + j))
                tick(ve.scalar_tensor_tensor(t[0], var, eps, seed, ALU.add, ALU.mult), 1)
                tick(ve.tensor_tensor(t[1], t[0], seed, ALU.mult), 2)
                tick(ve.tensor_scalar(t[2], t[1], -0.5, 1.5, ALU.mult, ALU.add), 3)
                tick(ve.tensor_tensor(dst, t[2], seed, ALU.mult), 4)

            ve.sem_inc(sem("e_out"), 4)
            ve.memset(eps_col[:, 0:1], LN_EPS).then_inc(sem("eps_ready"), 1)
            ve.memset(eps_col[:, 1:2], 0.0).then_inc(sem("eps_ready"), 1)
            ve.wait_ge(sem("lnwb_in"), 32)
            ve.wait_ge(sem("wtok_in0"), 16)
            n = 0
            for t in range(KT - 1):
                shifts = range(5 * t, 5 * t + 5) if t < KT_IN else range(5 * t, 5 * t + 1)
                for k in shifts:
                    if k in (10, 20):
                        ve.wait_ge(sem(f"wtok_in{k // 10}"), 16)
                    dst = w_eff[:, t, 0:D]
                    if k == shifts[0]:
                        ins = ve.tensor_scalar(dst, w_tok[:, k], ln_w[:, k:k + 1], None, ALU.mult)
                    else:
                        ve.wait_ge(sem("fold"), n)
                        ins = ve.scalar_tensor_tensor(dst, w_tok[:, k], ln_w[:, k:k + 1], dst, ALU.mult, ALU.add)
                    if k == shifts[-1]:
                        ins.then_inc(sem("w_eff"), 1)
                    else:
                        ins.then_inc(sem("fold"), 1)
                        n += 1
            ve.wait_ge(sem("wtok2_in"), 16)
            ve.tensor_scalar(w_eff[0:HALO2, KT - 1, 0:D], w_tok2[:], ln_w[0:HALO2, W_TILES:W_TILES + 1], None,
                             ALU.mult).then_inc(sem("w_eff"), 1)
            ve.wait_ge(sem("bias_row_ps"), 1)
            ve.wait_ge(sem("tokbias_in"), 16)
            ve.tensor_tensor(bias_row[:], PS[:, 0, 0:D], tok_bias[:], ALU.add).then_inc(sem("bias_row"), 1)
            ve.wait_ge(sem("col_sum_ps"), 1)
            ve.tensor_copy(col_sum[:], PS[:, 1, 0:D]).then_inc(sem("bias_row"), 1)
            ve.wait_ge(sem("bias_row"), 2)
            ve.sem_inc(sem("tok_mid"), 2)
            st = tok_stat
            with ve.Fori(0, PAIRS // 2) as i:
                for q in range(2):
                    ps = PS[:, 2 + q]
                    ve.wait_ge(sem("tok_ps"), i * 2 + q + 1)
                    ve.tensor_scalar(st[:, 0:1], ps[:, D:D + 1], -1.0 / PATCH_DIM, None, ALU.mult).then_inc(sem("tok_m"), 1)
                    ve.tensor_scalar(st[:, 1:2], ps[:, 200:201], 1.0 / PATCH_DIM, None, ALU.mult).then_inc(sem("tok_m"), 1)
                    ve.wait_ge(sem("tok_m"), i * 6 + q * 3 + 2)
                    ve.tensor_tensor(st[:, 2:3], st[:, 0:1], st[:, 0:1], ALU.mult).then_inc(sem("tok_m"), 1)
                    ve.wait_ge(sem("tok_m"), i * 6 + q * 3 + 3)
                    ve.tensor_tensor(st[:, 3:4], st[:, 1:2], st[:, 2:3], ALU.subtract).then_inc(sem("tok_var"), 1)
                    ve.scalar_tensor_tensor(tok_mid[:], col_sum[:], st[:, 0:1], ps[:, 0:D], ALU.mult, ALU.add
                                            ).then_inc(sem("tok_mid"), 1)
                    ve.wait_ge(sem("tok_seed"), i * 2 + q + 1)
                    refine(st[:, 3:4], LN_EPS, st[:, 5:6], [st[:, 6:7], st[:, 7:8], st[:, 8:9]], st[:, 9:10], 0, 2, i, q)
                    ve.wait_ge(sem("tok_mid"), i * 2 + q + 3)
                    for p in range(2):
                        rows = slice(p * IMG_TOK, (p + 1) * IMG_TOK)
                        ve.scalar_tensor_tensor(h[0:IMG_TOK, bass.ds(i * 4 + 2 * q + p, 1), :].rearrange("t b d -> t (b d)"),
                                                tok_mid[rows], st[rows, 9:10], bias_row[rows], ALU.mult, ALU.add
                                                ).then_inc(sem("h_tok"), 1)
            NW0 = 4 * PAIRS

            def moments(i, np_, name, base, per):
                stand(ve)
                for p in range(np_):
                    ve.bn_stats(stat6[:, p], h[:, bass.ds(i * np_ + p, 1), :].rearrange("t b d -> t (b d)")
                                ).then_inc(sem("stat6"), 1)
                for p in range(np_):
                    ve.wait_ge(sem("stat6"), i * per + (base + p + 1))
                    stand(ve)
                    ve.bn_aggr(mv[:, p], stat6[:, p]).then_inc(sem(name + "_mv"), 1)

            def normalize(i, np_, name, dst, scale):
                for p in range(np_):
                    ve.tensor_scalar(dst[:, p], h[:, bass.ds(i * np_ + p, 1), :].rearrange("t b d -> t (b d)"),
                                     mv[:, p, 0:1], scale[0:N, p:p + 1], ALU.subtract, ALU.mult).then_inc(sem(name), 1)

            tmp3 = [rs_tmp[0:N, 2, 0:2], rs_tmp[0:N, 3, 0:2], rs_tmp[0:N, 4, 0:2]]
            ve.wait_ge(sem("txt_in"), 16)
            ve.wait_ge(sem("h_tok"), B)
            ve.wait_ge(sem("attn0_in"), 16 * 7)
            hm = const("headmask", C1).unsqueeze(2).to_broadcast([C1, GRP, 2 * N])
            vm = const("vmask", GRP * SEG)
            with ve.Fori(0, PAIRS) as i:
                moments(i, 2, "a", 0, 4)
                ve.wait_ge(sem("a_seed"), i + 1)
                refine(mv[:, 0:2, 1], LN_EPS, rs_tmp[0:N, 1, 0:2], tmp3, rs[0:N, 0:2], NW0, 2, i, 0)
                normalize(i, 2, "a_xn", xn, rs)
                ve.wait_ge(sem("a_qk_ps"), i + 1)
                ve.scalar_tensor_tensor(k_exp[:], PS[0:C1, 2, 2 * N:4 * N].unsqueeze(1).to_broadcast([C1, GRP, 2 * N]),
                                        b_qkv0[:, 1:2], hm, ALU.add, ALU.mult).then_inc(sem("a_kexp"), 1)
                for p in range(2):
                    ve.wait_ge(sem("a_v_ps"), i * 2 + p + 1)
                    ve.tensor_tensor(v_exp[:, p].rearrange("k s (g c) -> k (s g) c", g=NGRP),
                                     PS[0:GRP * SEG, 3 + p, 0:SEGS * C1].rearrange("k (a c) -> k a c", c=32),
                                     vm.unsqueeze(1).to_broadcast([GRP * SEG, SEGS * NGRP, 32]), ALU.mult
                                     ).then_inc(sem("a_vexp"), 1)
                s_ps = PS[:, 5:5 + NGRP, 0:2 * GRP * SEG].rearrange("q g (h k) -> q g h k", k=SEG)
                pr = prob[:].rearrange("q g p (h k) -> q g (p h) k", k=SEG)
                every_key = [128, NGRP, 2 * GRP, SEG]
                ve.wait_ge(sem("a_s_ps"), i + 1)
                ve.tensor_reduce(smax[:], s_ps, AX_X, ALU.max).then_inc(sem("a_max"), 1)
                ve.wait_ge(sem("a_max"), i + 1)
                ve.tensor_tensor(pr, s_ps, smax[:].unsqueeze(3).to_broadcast(every_key), ALU.subtract
                                 ).then_inc(sem("a_sub"), 1)
                ve.wait_ge(sem("a_exp"), i + 1)
                ve.tensor_reduce(ssum[:], pr, AX_X, ALU.add).then_inc(sem("a_sum"), 1)
                ve.wait_ge(sem("a_sum"), i * 2 + 1)
                ve.reciprocal(ssum[:], ssum[:]).then_inc(sem("a_sum"), 1)
                ve.wait_ge(sem("a_sum"), i * 2 + 2)
                ve.tensor_tensor(pr, pr, ssum[:].unsqueeze(3).to_broadcast(every_key), ALU.mult
                                 ).then_inc(sem("a_prob"), 1)
                ve.wait_ge(sem("a_proj_ps"), i + 1)
                ve.wait_ge(sem("h_biased"), i * 2 + 2)
                hp = h[:, bass.ds(i * 2, 2), :]
                ve.tensor_tensor(hp, hp, PS[0:N, 0, 0:2 * D].rearrange("t (p d) -> t p d", p=2), ALU.add
                                 ).then_inc(sem("a_h"), 1)
                ve.wait_ge(sem("a_h"), i + 1)
                moments(i, 2, "r", 2, 4)
                ve.wait_ge(sem("r_seed"), i + 1)
                refine(mv[:, 0:2, 1], LN_EPS, rs_tmp[0:N, 1, 0:2], tmp3, rs[0:N, 0:2], NW0, 2, i, 1)
                normalize(i, 2, "r_xn", xn, rs)
                ve.wait_ge(sem("r_kept"), i + 1)
                ve.wait_ge(sem("r_xnT_ps"), i + 1)
            NW1 = NW0 + 8 * PAIRS

            def wide(x):
                return x.unsqueeze(2).to_broadcast([N, B, E])

            step = [0]

            def then(ins):
                step[0] += 1
                ins.then_inc(sem("r_step"), 1)
                ve.wait_ge(sem("r_step"), step[0])

            rev = const("rev", N).unsqueeze(1).to_broadcast([N, B, E])
            ve.wait_ge(sem("r_logit"), PAIRS)
            then(ve.tensor_reduce(r_top[:, 0], logits[:], AX_X, ALU.max))
            ve.tensor_tensor(r_e[:, 0], logits[:], wide(r_top[:, 0]), ALU.subtract).then_inc(sem("r_shift"), 1)

            def pick(src, best, tmp, dst):
                then(ve.tensor_tensor(tmp, src, wide(best), ALU.is_equal))
                then(ve.tensor_tensor(tmp, tmp, rev, ALU.mult))
                then(ve.tensor_reduce(r_top[:, 1], tmp, AX_X, ALU.max))
                return ve.tensor_tensor(dst, tmp, wide(r_top[:, 1]), ALU.is_equal)

            then(pick(logits[:], r_top[:, 0], r_e[:, 5], r_e[:, 2]))
            then(ve.scalar_tensor_tensor(r_e[:, 3], r_e[:, 2], -3e38, logits[:], ALU.mult, ALU.add))
            then(ve.tensor_reduce(r_top[:, 2], r_e[:, 3], AX_X, ALU.max))
            pick(r_e[:, 3], r_top[:, 2], r_e[:, 5], r_e[:, 4]).then_inc(sem("r_choice"), 2)
            ve.wait_ge(sem("r_choice"), 2)
            ve.wait_ge(sem("r_exp"), 1)
            then(ve.tensor_reduce(r_top[:, 3], r_e[:, 1], AX_X, ALU.add))
            then(ve.reciprocal(r_top[:, 4], r_top[:, 3]))
            then(ve.tensor_tensor(r_e[:, 0], r_e[:, 1], wide(r_top[:, 4]), ALU.mult))
            then(ve.tensor_tensor(r_e[:, 5], r_e[:, 2], r_e[:, 4], ALU.add))
            then(ve.tensor_tensor(gate_of[:], r_e[:, 0], r_e[:, 5], ALU.mult))
            ve.wait_ge(sem("r_count_ps"), 1)
            count = PS[0:N, 3, 0:4 * PAIRS * E].rearrange("t (k p g e) -> t k g p e", k=2, p=2, g=PAIRS)
            four = lambda x: x.rearrange("t (g p) e -> t g p e", p=2)
            then(ve.tensor_tensor(four(r_e[:, 0]), four(r_e[:, 2]), count[:, 0], ALU.mult))
            then(ve.tensor_tensor(four(r_e[:, 1]), four(r_e[:, 4]), count[:, 1], ALU.mult))
            then(ve.scalar_tensor_tensor(slot_of[:], r_e[:, 0], -1.0, r_e[:, 1], ALU.add, ALU.add))

            iota = const("iota", N).unsqueeze(1).to_broadcast([N, E, CAP])

            def place(b):
                return slot_of[:, bass.ds(b, 1), :].rearrange("t b e -> t (b e)").unsqueeze(2).to_broadcast([N, E, CAP])

            with ve.Fori(0, PAIRS // 2) as i:
                for q in range(2):
                    ve.wait_ge(sem("disp_ps"), i * 4 + 2 * q + 2)
                    for p in range(2):
                        ve.tensor_tensor(onehot[:, q, p].rearrange("t (e c) -> t e c", e=E), iota,
                                         place(i * 4 + (2 * q + p)), ALU.is_equal).then_inc(sem("onehot"), 1)
            ve.wait_ge(sem("pads_zero"), 3)
            with ve.Fori(0, E // 2) as i:
                for q in range(2):
                    for half in range(2):
                        ve.wait_ge(sem("eo_ps"), i * 4 + 2 * q + half + 5)
                        for z in range(2):
                            ve.tensor_copy(
                                e_out[64 * q:64 * q + CAP, half * 4 + z:half * 4 + z + 3:2, bass.ds(i, 1)].rearrange("s g e d -> s g (e d)"),
                                PS[64 * z:64 * z + CAP, 2 + half, 0:2 * D].rearrange("s (g d) -> s g d", g=2)
                            ).then_inc(sem("e_out"), 1)
            ve.wait_ge(sem("layer1_in"), 16 * 10)
            l1m = const("l1mask", HD)
            with ve.Fori(0, PAIRS) as i:
                for p in range(2):
                    cm = comb[:, p, :, 0:CAP]
                    ve.tensor_tensor(cm, iota, place(i * 2 + p), ALU.is_equal).then_inc(sem("comb_hot"), 1)
                    ve.wait_ge(sem("comb_hot"), i * 2 + p + 1)
                    g = gate_of[:, bass.ds(i * 2 + p, 1), :].rearrange("t b e -> t (b e)").unsqueeze(2).to_broadcast([N, E, CAP])
                    ve.tensor_tensor(cm, cm, g, ALU.mult).then_inc(sem("comb"), 1)
                ve.wait_ge(sem("moe_ps"), i + 1)
                hp = h[:, bass.ds(i * 2, 2), :]
                ve.tensor_tensor(hp, hp, PS[0:N, 2, 0:2 * D].rearrange("t (p d) -> t p d", p=2), ALU.add
                                 ).then_inc(sem("moe_h"), 1)
                ve.wait_ge(sem("moe_h"), i + 1)
                moments(i, 2, "b", 4 * PAIRS, 2)
                ve.wait_ge(sem("b_seed"), i + 1)
                refine(mv[:, 0:2, 1], LN_EPS, rs_tmp[0:N, 1, 0:2], tmp3, rs[0:N, 0:2], NW1, 1, i, 0)
                normalize(i, 2, "b_xn", xn, rs)
                for p in range(2):
                    ve.wait_ge(sem("b_kv_ps"), i * 2 + p + 1)
                    ve.tensor_copy(kv1[:, p], PS[0:N, 5 + p, 0:2 * D]).then_inc(sem("b_kv"), 1)
                ve.wait_ge(sem("b_q1T"), i + 1)
                for mh in range(2):
                    ve.tensor_reduce(den[:, 0].rearrange("k (p a) -> k a p", a=2)[:, mh],
                                     q1T[:, mh].rearrange("k (p t) -> k p t", p=2), AX_X, ALU.add,
                                     apply_absolute_value=True).then_inc(sem("b_den"), 1)
                ve.wait_ge(sem("b_den"), i * 6 + 2)
                ve.tensor_scalar(den[:, 1], den[:, 0], L1_EPS, None, ALU.max).then_inc(sem("b_den"), 1)
                ve.wait_ge(sem("b_kvp_ps"), i + 1)
                ve.tensor_scalar(den[:, 2], PS[0:HD, 7, 0:4], L1_EPS, None, ALU.max).then_inc(sem("b_den"), 1)
                ve.wait_ge(sem("b_den"), i * 6 + 4)
                ve.reciprocal(den[:, 3:5], den[:, 1:3]).then_inc(sem("b_den"), 1)
                ve.wait_ge(sem("b_den"), i * 6 + 5)
                ve.tensor_tensor(den[:, 5], den[:, 3], den[:, 4], ALU.mult).then_inc(sem("b_den"), 1)
                ve.wait_ge(sem("b_den"), i * 6 + 6)
                for p in range(2):
                    for mh in range(2):
                        j = p * 2 + mh
                        ve.scalar_tensor_tensor(kv_bd[:, p, mh], PS[0:HD, 3, j * HD:(j + 1) * HD], den[:, 5, j:j + 1], l1m,
                                                ALU.mult, ALU.mult).then_inc(sem("b_kvbd"), 1)
                ve.wait_ge(sem("b_proj_ps"), i + 1)
                ve.wait_ge(sem("h_biased"), i * 2 + (2 * PAIRS + 2))
                ve.tensor_tensor(hp, hp, PS[0:N, 2, 0:2 * D].rearrange("t (p d) -> t p d", p=2), ALU.add
                                 ).then_inc(sem("b_h"), 1)
            NW2 = NW1 + 4 * PAIRS

            ve.tensor_tensor(slot_sq[:], slot_raw[:], slot_raw[:], ALU.mult).then_inc(sem("slot_step"), 1)
            ve.wait_ge(sem("slot_step"), 1)
            ve.tensor_reduce(slot_s[:, 3].rearrange("k (a s) -> k a s", a=2),
                             slot_sq[:].rearrange("k a (n s) -> k a s n", n=NS), AX_X, ALU.add).then_inc(sem("slot_step"), 1)
            ve.wait_ge(sem("slot_step"), 2)
            ve.tensor_scalar(slot_s[:, 0], slot_s[:, 3], TINY, None, ALU.max).then_inc(sem("slot_ss"), 1)
            ve.wait_ge(sem("slot_seed"), 1)
            refine(slot_s[:, 0], 0.0, slot_s[:, 2], [slot_s[:, 4], slot_s[:, 5], slot_s[:, 1]], slot_s[:, 4], NW2, 0, 0, 0)
            NW3 = NW2 + 4
            ve.tensor_tensor(slot_s[:, 5], slot_s[:, 3], slot_s[:, 4], ALU.mult).then_inc(sem("slot_step"), 1)
            ve.wait_ge(sem("slot_step"), 3)
            ve.tensor_scalar(slot_s[:, 1], slot_s[:, 5], L2_EPS, None, ALU.add).then_inc(sem("slot_step"), 1)
            ve.wait_ge(sem("slot_step"), 4)
            ve.reciprocal(slot_s[:, 2], slot_s[:, 1]).then_inc(sem("slot_step"), 1)
            ve.wait_ge(sem("slot_step"), 5)
            ve.tensor_scalar(slot_s[:, 5], slot_s[:, 2], l_scale[:], None, ALU.mult).then_inc(sem("slot_step"), 1)
            ve.wait_ge(sem("slot_step"), 6)
            for a in range(2):
                ve.tensor_tensor(slot_n[:, a].rearrange("k (n s) -> k n s", n=NS),
                                 slot_raw[:, a].rearrange("k (n s) -> k n s", n=NS),
                                 slot_s[:, 5, a * PS_:(a + 1) * PS_].unsqueeze(1).to_broadcast([HD, NS, PS_]), ALU.mult
                                 ).then_inc(sem("slot_n"), 1)
            ve.wait_ge(sem("b_h"), PAIRS)
            tmp4 = [rs_tmp[0:N, 2], rs_tmp[0:N, 3], rs_tmp[0:N, 4]]
            with ve.Fori(0, 4) as i:
                moments(i, 4, "s", 6 * PAIRS, 4)
                ve.wait_ge(sem("s_mv"), i * 4 + 4)
                ve.tensor_scalar(rs_tmp[0:N, 5], mv[:, :, 1], TINY, None, ALU.max).then_inc(sem("s_varmax"), 1)
                ve.wait_ge(sem("s_varmax"), i + 1)
                ve.wait_ge(sem("s_seed"), i * 2 + 2)
                refine(mv[:, :, 1], LN_EPS, rs_tmp[0:N, 1], tmp4, rs[0:N], NW3, 2, i, 0)
                refine(rs_tmp[0:N, 5], 0.0, rs_tmp[0:N, 7], tmp4, rs_tmp[0:N, 6], NW3, 2, i, 1)

                def tick(ins, j):
                    ins.then_inc(sem("s_scale"), 1)
                    ve.wait_ge(sem("s_scale"), i * 5 + j)
                tick(ve.tensor_tensor(rs_tmp[0:N, 2], mv[:, :, 1], rs_tmp[0:N, 6], ALU.mult), 1)
                tick(ve.scalar_tensor_tensor(rs_tmp[0:N, 3], rs_tmp[0:N, 2], float(D) ** 0.5, rs[0:N], ALU.mult, ALU.mult), 2)
                tick(ve.tensor_scalar(rs_tmp[0:N, 4], rs_tmp[0:N, 3], L2_EPS, None, ALU.add), 3)
                tick(ve.reciprocal(rs_tmp[0:N, 2], rs_tmp[0:N, 4]), 4)
                tick(ve.tensor_tensor(rs_tmp[0:N, 3], rs_tmp[0:N, 2], rs[0:N], ALU.mult), 5)
                normalize(i, 4, "s_xs", xs, rs_tmp[:, 3])
                log = PS[0:N, 2, 0:4 * NP].rearrange("t (p n) -> t p n", p=4)
                ve.wait_ge(sem("s_log_ps"), i + 1)
                ve.tensor_reduce(c_st[:, 0], log, AX_X, ALU.max).then_inc(sem("s_soft"), 1)
                ve.wait_ge(sem("s_soft"), i * 4 + 1)
                ve.tensor_tensor(cmb[:], log, c_st[:, 0].unsqueeze(2).to_broadcast([N, 4, NP]), ALU.subtract
                                 ).then_inc(sem("s_csub"), 1)
                ve.wait_ge(sem("s_logT_ps"), i + 1)
                ve.tensor_reduce(d_st[:, 0:1], PS[:, 3, 0:N], AX_X, ALU.max, negate=True).then_inc(sem("s_dmax"), 1)
                ve.wait_ge(sem("s_dexp"), i + 1)
                ve.reciprocal(d_st[:, 2:3], d_st[:, 1:2]).then_inc(sem("s_soft"), 1)
                ve.wait_ge(sem("s_soft"), i * 4 + 2)
                ve.tensor_scalar(dspT[:], dspT[:], d_st[:, 2:3], None, ALU.mult).then_inc(sem("s_dspT"), 1)
                ve.wait_ge(sem("s_cexp"), i + 1)
                ve.tensor_reduce(c_st[:, 1], cmb[:], AX_X, ALU.add).then_inc(sem("s_soft"), 1)
                ve.wait_ge(sem("s_soft"), i * 4 + 3)
                ve.reciprocal(c_st[:, 2], c_st[:, 1]).then_inc(sem("s_soft"), 1)
                ve.wait_ge(sem("s_soft"), i * 4 + 4)
                ve.tensor_tensor(cmb[:], cmb[:], c_st[:, 2].unsqueeze(2).to_broadcast([N, 4, NP]), ALU.mult
                                 ).then_inc(sem("s_cmb"), 1)
                ve.wait_ge(sem("s_xt_ps"), i + 1)
            upm = const("upmask", HD)
            for mh in range(2):
                ve.wait_ge(sem("s_gelu"), mh + 1)
                m = upm[:, mh * NS:(mh + 1) * NS].unsqueeze(2).to_broadcast([HD, NS, PS_]).unsqueeze(1)
                hv = hidS[:, mh].rearrange("k (b n s) -> k b n s", b=B, n=NS)
                for n in range(NS):
                    hn = hv[:, :, n]
                    ins = ve.tensor_scalar(hn, hn, upm[:, mh * NS + n:mh * NS + n + 1], None, ALU.mult)
                ins.then_inc(sem("s_hidm"), 1)
            for j in range(4):
                ve.wait_ge(sem("s_yt_ps"), j + 1)
                ve.tensor_tensor(y_t[:, j], PS[:, 2 + j % 2, 0:D], b_up[:], ALU.add).then_inc(sem("s_yt"), 1)
            for b in range(B):
                ve.wait_ge(sem("s_y_ps"), b + 1)
                ve.tensor_tensor(h[:, b], h[:, b], PS[0:N, 4 + b % 4, 0:D], ALU.add).then_inc(sem("y_added"), 1)


def constants():
    import numpy as np
    c = {}
    c["ident"] = np.eye(128)
    c["ones"] = np.ones((128, 128))
    c["tri"] = np.triu(np.ones((N, N)))
    r = np.arange(128)
    c["l1mask"] = (r[:HD, None] // 16 == r[None, :HD] // 16)
    c["iota"] = np.tile(np.arange(CAP), (128, 1))
    c["vmask"] = (r[:GRP * SEG, None] // SEG == r[None, :32] // HDIM0)
    c["upmask"] = np.concatenate([(r[:HD, None] // HS + mh * 4 == r[None, :NS]) for mh in range(2)], axis=1)
    c["rev"] = np.tile(E - np.arange(E), (128, 1))
    i = np.arange(PATCH)
    inner = (i > 0).astype(int) + (i < PATCH - 1)
    m = np.zeros((KT, 128))
    m[:KT_IN] = np.tile((1 + inner[:, None] + inner[None, :]).reshape(-1), C).reshape(KT_IN, 128)
    m[KT_IN] = 1
    m[KT_IN + 1, :HALO2] = 1
    c["mult"] = m.T
    c["headmask"] = ((r[:C1, None] % 32) // HDIM0 == r[None, :GRP])
    out = np.zeros((128, CONST_W), np.float32)
    for name, (a, w) in CONST_AT.items():
        out[:c[name].shape[0], a:a + w] = c[name]
    return out


def halo(t):
    import numpy as np
    return np.concatenate([t[..., 1:-1, 0], t[..., 1:-1, -1], t[..., 0, 1:-1], t[..., -1, 1:-1]], axis=-1)


def kernel(**inputs):
    import numpy as np
    import concourse.bacc as bacc
    from concourse.bass_utils import run_bass_kernel_spmd

    v = {k: np.ascontiguousarray(a) for k, a in inputs.items()}
    P = PATCH
    xp = np.zeros((B, C, IMG + 2, IMG + 2), np.float32)
    xp[:, :, 1:-1, 1:-1] = v["x"]
    win = np.stack([np.stack([xp[:, :, P * a:P * a + P + 2, P * b:P * b + P + 2] for b in range(SIDE)], 2)
                    for a in range(SIDE)], 2)
    inner = win[..., 1:-1, 1:-1].reshape(B, C, IMG_TOK, P * P).transpose(1, 3, 0, 2).reshape(K_IN, B * IMG_TOK)
    outer = halo(win).reshape(B, C, IMG_TOK, 4 * P).transpose(1, 3, 0, 2).reshape(K_HALO, B * IMG_TOK)
    allk = np.concatenate([inner, outer], 0)
    xin = allk[:(KT - 1) * 128].reshape(KT - 1, 128, PAIRS, 128).transpose(2, 1, 0, 3)
    xhalo = allk[(KT - 1) * 128:].reshape(HALO2, PAIRS, 128).transpose(1, 0, 2)

    def fold(t):
        t = t.reshape(-1, P, P, 5, C).transpose(3, 4, 1, 2, 0)
        win = np.zeros((5, C, P + 2, P + 2, t.shape[-1]), np.float32)
        for s, (dy, dx) in enumerate([(0, 0), (0, -1), (0, 1), (-1, 0), (1, 0)]):
            win[s, :, 1 + dy:1 + dy + P, 1 + dx:1 + dx + P] = t[s]
        inn = win[:, :, 1:-1, 1:-1].reshape(5, KT_IN, 128, -1).transpose(2, 1, 0, 3).reshape(128, 5 * KT_IN, -1)
        ring = [win[1][:, 1:-1, 0], win[2][:, 1:-1, -1], win[3][:, 0, 1:-1], win[4][:, -1, 1:-1]]
        ring = np.stack(ring, 1).reshape(K_HALO, -1)
        return np.concatenate([inn, ring[:128, None]], 1), ring[128:]

    wtok, wtok2 = fold(v["L0_tok_proj_weight"])

    def columns(t):
        a, b = fold(t[None])
        out = np.zeros((128, W_TILES + 1), np.float32)
        out[:, :W_TILES] = a[..., 0]
        out[:HALO2, W_TILES] = b[:, 0]
        return out

    def halves(w):
        return w.reshape(2, HD, -1).transpose(1, 0, 2)

    wqkv1 = v["L1_attn_w_qkv"].T
    arrays = {
        "xin": xin, "xhalo": xhalo, "txt": v["txt"], "wtok": wtok, "wtok2": wtok2,
        "lnw": columns(v["L0_tok_ln_weight"]), "lnb": columns(v["L0_tok_ln_bias"]), "tokbias": v["L0_tok_proj_bias"],
        "consts": constants(),
        "wred": halves(v["L0_attn_W_reduce"]), "bred": v["L0_attn_b_reduce"][:, None], "wqkv0": v["L0_attn_W_qkv"],
        "bqkv0": v["L0_attn_b_qkv"].reshape(3, C1).T, "wproj0": v["L0_attn_W_proj"], "bproj0": v["L0_attn_b_proj"],
        "wrouter": halves(v["L0_ffn_w_router"]),
        "wi": v["L0_ffn_wi"].reshape(E, 2, HD, F).transpose(0, 2, 1, 3),
        "wo": v["L0_ffn_wo"].reshape(E, FT, 128, D).transpose(0, 2, 1, 3),
        "wq1": halves(wqkv1[:, :D]), "wkv1": halves(wqkv1[:, D:]), "wproj1": halves(v["L1_attn_w_proj"].T),
        "bproj1": v["L1_attn_b_proj"],
        "slots": halves(v["L1_ffn_slot_params"].reshape(D, NP)), "lscale": v["L1_ffn_scale"].reshape(1),
        "wdown": halves(v["L1_ffn_W_down"].transpose(1, 0, 2).reshape(D, NS * HS)),
        "bdown": v["L1_ffn_b_down"].reshape(2, HD).T,
        "wup": halves(v["L1_ffn_W_up"].reshape(NS * HS, D)),
        "bup": np.tile(np.repeat(v["L1_ffn_b_up"], PS_, axis=0), (4, 1)),
    }
    nc = bacc.Bacc("TRN2", target_bir_lowering=False, num_devices=1)
    feeds, args = {}, {}
    for name, a in arrays.items():
        a = np.ascontiguousarray(a)
        feeds[f"in_{name}"] = a
        args[name] = nc.dram_tensor(f"in_{name}", a.shape, F32, kind="ExternalInput").ap()
    args["out"] = nc.dram_tensor("out_0", (B, N, D), F32, kind="ExternalOutput").ap()
    build(nc, **args)
    r = run_bass_kernel_spmd(nc, [feeds], core_ids=[0])
    return r.results[0]["out_0"]
```

```python
from contextlib import ExitStack

import concourse.bass as bass
from concourse import mybir

ALU = mybir.AluOpType
ACT = mybir.ActivationFunctionType
F32 = mybir.dt.float32
AX_X = mybir.AxisListType.X

B, C, IMG, PATCH = 16, 3, 128, 16
SIDE = IMG // PATCH
IMG_TOK = SIDE * SIDE
TXT_TOK = 32
N = IMG_TOK + TXT_TOK
D = 192
HD = D // 2
PAIRS = B // 2
PATCH_DIM = PATCH * PATCH * 5 * C
K_IN = C * PATCH * PATCH
K_HALO = C * 4 * PATCH
KT_IN = K_IN // 128
KT = KT_IN + 2
HALO2 = K_HALO - 128
W_TILES = 5 * KT_IN + 1

C1, HEADS0, HDIM0, SEGS = 96, 12, 8, 4
SEG = N // SEGS
GRP = 4
NGRP = HEADS0 // GRP
PADSEG = 32
SCALE0 = float(HDIM0) ** -0.5

E, F = 8, 768
S = 2 * N
CAP = int(2 * 1.25 * S / E)
PADCAP = 64
FT = F // 128
SLOTS = PAIRS * CAP

NS, PS_, HS = 8, 4, 24
NP = NS * PS_

LN_EPS = 1e-5
L1_EPS = 1e-12
L2_EPS = 1e-6
TINY = 1e-18

CONSTS = [("ident", 128), ("ones", 128), ("tri", 96), ("l1mask", 96), ("iota", CAP), ("vmask", 32),
          ("upmask", 2 * NS), ("rev", E), ("mult", KT), ("headmask", GRP)]
CONST_AT, _at = {}, 0
for _n, _w in CONSTS:
    CONST_AT[_n] = (_at, _w)
    _at += _w
CONST_W = _at


def build(nc, xin, xhalo, txt, wtok, wtok2, lnw, lnb, tokbias, consts, wred, bred, wqkv0, bqkv0, wproj0, bproj0,
          wrouter, wi, wo, wq1, wkv1, wproj1, bproj1, slots, lscale, wdown, bdown, wup, bup, out):
    with ExitStack() as ctx:
        def sb(name, shape, dt=F32):
            return ctx.enter_context(nc.sbuf_tensor("sb_" + name, shape, dt))

        sems = {}

        def sem(name):
            if name not in sems:
                sems[name] = ctx.enter_context(nc.semaphore(name))
            return sems[name]

        PS = ctx.enter_context(nc.psum_tensor("banks", [128, 8, 512], F32))

        cst = sb("cst", [128, CONST_W])

        def const(name, rows=128):
            a, w = CONST_AT[name]
            return cst[0:rows, a:a + w]

        h_all = sb("h", [N, B + 8, D])
        h = h_all[:, 4:4 + B]
        shared = sb("w_tok_e_out", [128, PAIRS * E // 2, D])
        w_tok = shared[:, 0:W_TILES]
        w_tok2 = sb("w_tok2", [HALO2, D])
        ln_w = sb("ln_w", [128, W_TILES + 1])
        ln_b = sb("ln_b", [128, W_TILES + 1])
        shared2 = sb("tok_xeT", [128, 2 * E * PAIRS * CAP])
        nx = 2 * KT * 128
        x_k = shared2[:, 0:nx].rearrange("k (q t n) -> k q t n", q=2, t=KT)
        x_sq = shared2[:, nx:2 * nx].rearrange("k (q t n) -> k q t n", q=2, t=KT)
        w_eff = shared2[:, 2 * nx:2 * nx + KT * (D + 1)].rearrange("k (t n) -> k t n", t=KT)
        tok_bias = sb("tok_bias", [128, D])
        bias_row = sb("bias_row", [128, D])
        col_sum = sb("col_sum", [128, D])
        tok_stat = sb("tok_stat", [128, 16])
        tok_mid = sb("tok_mid", [128, D])
        eps_col = sb("eps_col", [128, 2])
        w_red = sb("w_red", [HD, 2, C1])
        b_red = sb("b_red", [C1, 1])
        w_qkv0 = sb("w_qkv0", [C1, 3 * C1])
        b_qkv0 = sb("b_qkv0", [C1, 3])
        w_proj0 = sb("w_proj0", [C1, D])
        b_proj0 = sb("b_proj0", [N, D])
        stat6 = sb("stat6", [N, 4, 6])
        mv = sb("mv", [N, 4, 2])
        rs_tmp = sb("rs_tmp", [128, 8, 4])
        rs = sb("rs", [128, 4])
        xn = sb("xn", [N, 4, D])
        xnr = sb("xnr", [N, 4, D])
        xnT = sb("xnT", [HD, 2, 2, 2 * N])
        xrT = sb("xrT", [C1, 2, 2 * N])
        xr_rep = sb("xr_rep", [C1, 2, 2 * SEGS, GRP, SEG])
        qT = sb("qT", [C1, 2, 2, SEGS, PADSEG])
        k_exp = sb("k_exp", [C1, 2, GRP, 2 * N])
        smax = sb("smax", [128, 2, NGRP, 2 * GRP])
        ssum = sb("ssum", [128, 2, NGRP, 2 * GRP])
        oT = sb("oT", [C1, 2, 2 * N])
        shared4 = sb("hidT_attn", [128, 2 * FT * SLOTS])
        v_exp = shared4[0:GRP * SEG, 0:1536].rearrange("k (q p s c) -> k q p s c", q=2, p=2, s=SEGS)
        prob = shared4[:, 1536:1536 + 1152].rearrange("t (q g p k) -> t q g p k", q=2, g=NGRP, p=2)
        probT = shared4[0:GRP * SEG, 2688:2688 + 1536].rearrange("k (q p g t) -> k q p g t", q=2, p=2, g=NGRP)
        w_router = sb("w_router", [HD, 2, E])
        xn2_all = sb("xn2", [N, B + 4, D])
        xn2 = xn2_all[:, 4:]
        logits_all = sb("logits", [N, B + 4, E])
        logits = logits_all[:, 4:]
        r_top = sb("r_top", [N, 6, B])
        r_e = sb("r_e", [N, 6, B, E])
        slot_of = sb("slot_of", [N, B, E])
        gate_of = sb("gate_of", [N, B, E])
        shared3 = sb("dispatch_comb_slots", [N, 4 * E * CAP + 4 * D])
        onehot = shared3[:, 0:4 * E * CAP].rearrange("t (q p s) -> t q p s", q=2, p=2)
        x_disp = shared3[:, 4 * E * CAP:].rearrange("t (q p d) -> t q p d", q=2, p=2)
        comb = shared3[:, 0:4 * E * PADCAP].rearrange("t (q p e c) -> t q p e c", q=2, p=2, e=E)
        xeT = shared2[0:HD].rearrange("k (a e g c) -> k a e g c", a=2, e=E, g=PAIRS)
        wi_sl = sb("wi_sl", [HD, 2, 2, F])
        wo_sl = sb("wo_sl", [128, 2, FT, D])
        hidT = shared4[:].rearrange("f (q t s) -> f q t s", q=2, t=FT)
        e_out = shared[:].rearrange("s (g e) d -> s g e d", g=PAIRS)
        combT = sb("combT", [128, 2, 2, E // 2, N])
        w_q1 = sb("w_q1", [HD, 2, D])
        w_kv1 = sb("w_kv1", [HD, 2, 2 * D])
        w_proj1 = sb("w_proj1", [HD, 2, D])
        b_proj1 = sb("b_proj1", [N, D])
        q1T = shared4[0:HD, 0:768].rearrange("k (q a t) -> k q a t", q=2, a=2)
        kv1 = shared4[0:N, 768:768 + 1536].rearrange("t (q p n) -> t q p n", q=2, p=2)
        abs_k = shared4[0:N, 2304:2304 + 768].rearrange("t (q p n) -> t q p n", q=2, p=2)
        kv_bd = shared4[0:HD, 3072:3072 + 768].rearrange("k (q p a n) -> k q p a n", q=2, p=2, a=2)
        o1T = shared4[0:HD, 3840:3840 + 768].rearrange("k (q p a t) -> k q p a t", q=2, p=2, a=2)
        den = sb("den", [HD, 2, 6, 4])
        slot_raw = sb("slot_raw", [HD, 2, NP])
        slot_sq = sb("slot_sq", [HD, 2, NP])
        slot_n = sb("slot_n", [HD, 2, NP])
        slot_s = sb("slot_s", [HD, 6, 2 * PS_])
        l_scale = sb("l_scale", [HD, 1])
        w_down = sb("w_down", [HD, 2, D])
        b_down = sb("b_down", [HD, 2])
        w_up = sb("w_up", [HD, 2, D])
        b_up = sb("b_up", [128, D])
        xs = shared2[0:N, 4 * D:12 * D].rearrange("t (r p d) -> t r p d", r=2, p=4)
        xsT = shared2[0:HD, 12 * D:12 * D + 8 * N].rearrange("k (a t) -> k a t", a=2)
        cmb = sb("cmb", [N, 4, NP])
        c_st = sb("c_st", [N, 3, 4])
        cmbT = sb("cmbT", [128, 4, N])
        dspT = sb("dspT", [128, N])
        d_st = sb("d_st", [128, 3])
        dsp = sb("dsp", [N, 4 * NP])
        x_tT = shared3[:, 0:2 * B * NP].rearrange("k (a s) -> k a s", a=2)
        hidS = shared4[0:HD, 4608:4608 + 2 * B * NP].rearrange("k (a s) -> k a s", a=2)
        y_t = shared2[:, 0:4 * D].rearrange("s (j d) -> s j d", j=4)

        ident = const("ident")
        ones = const("ones")

        def stand(eng):
            eng.sem_inc(sem("carried_" + ("ve" if eng is nc.vector else "pe")), 1)

        def flip(dst, src):
            rows = src.shape[0]
            return nc.tensor.transpose(dst, src, ident[0:rows, 0:rows])

        block = ctx.enter_context(nc.Block())

        @block.sync
        def _(sp):
            sp.dma_start(cst[:], consts).then_inc(sem("cst_in"), 16)
            sp.dma_start(ln_w[:], lnw).then_inc(sem("lnwb_in"), 16)
            sp.dma_start(ln_b[:], lnb).then_inc(sem("lnwb_in"), 16)
            sp.dma_start(tok_bias[:], tokbias.partition_broadcast(128)).then_inc(sem("tokbias_in"), 16)
            for c in range(3):
                a, b = c * 10, (c + 1) * 10 + (c == 2)
                sp.dma_start(w_tok[:, a:b], wtok[:, a:b]).then_inc(sem(f"wtok_in{c}"), 16)
            sp.dma_start(w_tok2[:], wtok2).then_inc(sem("wtok2_in"), 16)
            sp.dma_start(h[IMG_TOK:N], txt.rearrange("b t d -> t b d")).then_inc(sem("txt_in"), 16)
            for q in range(2):
                sp.dma_start(x_k[:, q, 0:KT - 1], xin[q]).then_inc(sem(f"x_in{q}"), 16)
                sp.dma_start(x_k[0:HALO2, q, KT - 1], xhalo[q]).then_inc(sem(f"x_in{q}"), 16)
            with sp.Fori(1, PAIRS // 2) as i:
                for q in range(2):
                    sp.wait_ge(sem("tok_ps"), i * 2 + (q - 1))
                    sp.dma_start(x_k[:, q, 0:KT - 1], xin[bass.ds(i * 2 + q, 1)]).then_inc(sem(f"x_in{q}"), 16)
                    sp.dma_start(x_k[0:HALO2, q, KT - 1], xhalo[bass.ds(i * 2 + q, 1)]).then_inc(sem(f"x_in{q}"), 16)
            n = 0
            for dst, src in [(w_red[:], wred), (b_red[:], bred), (w_qkv0[:], wqkv0), (b_qkv0[:], bqkv0),
                             (w_proj0[:], wproj0), (b_proj0[:], bproj0.partition_broadcast(N)),
                             (w_router[:], wrouter)]:
                sp.dma_start(dst, src).then_inc(sem("attn0_in"), 16)
            for dst, src in [(w_q1[:], wq1), (w_kv1[:], wkv1), (w_proj1[:], wproj1),
                             (b_proj1[:], bproj1.partition_broadcast(N)), (slot_raw[:], slots),
                             (l_scale[:], lscale.partition_broadcast(HD)), (w_down[:], wdown), (b_down[:], bdown),
                             (w_up[:], wup), (b_up[:], bup)]:
                sp.dma_start(dst, src).then_inc(sem("layer1_in"), 16)
            with sp.Fori(0, E // 2) as i:
                for q in range(2):
                    sp.wait_ge(sem("eo_ps"), i * 4 + 2 * q + 2)
                    sp.dma_start(wi_sl[:, q], wi[bass.ds(i * 2 + q, 1)]).then_inc(sem(f"wexp_in{q}"), 16)
                    sp.dma_start(wo_sl[:, q], wo[bass.ds(i * 2 + q, 1)]).then_inc(sem(f"wexp_in{q}"), 16)
            out_v = out.rearrange("b t d -> t b d")
            for b in range(0, B, 4):
                sp.wait_ge(sem("y_added"), b + 4)
                sp.dma_start(out_v[:, b:b + 4], h[:, b:b + 4]).then_inc(sem("stored"), 16)
            sp.wait_ge(sem("stored"), 16 * (B // 4))

        @block.gpsimd
        def _(gp):
            gp.memset(qT[:], 0.0).then_inc(sem("pads_zero"), 1)
            gp.memset(h_all[:, 0:4], 0.0).then_inc(sem("pads_zero"), 1)
            gp.memset(h_all[:, B + 4:B + 8], 0.0).then_inc(sem("pads_zero"), 1)
            gp.wait_ge(sem("w_eff"), KT)
            gp.wait_ge(sem("bias_row_ps"), 1)
            gp.memset(shared[:], 0.0).then_inc(sem("pads_zero"), 1)
            gp.wait_ge(sem("cst_in"), 16)
            gp.tensor_copy(w_eff[:, :, D], const("mult")).then_inc(sem("mult_ready"), 1)
            gp.wait_ge(sem("attn0_in"), 16 * 7)
            def keep_normalized(i):
                gp.wait_ge(sem("r_xn"), i * 4 + 4)
                gp.tensor_copy(xn2_all[:, bass.ds(i * 4, 4), :], xnr[:]).then_inc(sem("r_kept"), 1)

            with gp.Fori(0, B // 4) as i:
                gp.wait_ge(sem("a_xn"), i * 4 + 4)
                for p in range(4):
                    hp = h_all[:, bass.ds(i * 4 + (4 + p), 1), :]
                    gp.tensor_tensor(hp, hp, b_proj0[:].unsqueeze(1), ALU.add).then_inc(sem("h_biased"), 1)
                keep_normalized(i)
            keep_normalized(B // 4)
            with gp.Fori(0, PAIRS // 2) as i:
                for q in range(2):
                    gp.wait_ge(sem("disp_ps"), i * 4 + 2 * q + 2)
                    if q == 0:
                        gp.wait_ge(sem("r_kept"), B // 4 + 1)
                    gp.tensor_copy(x_disp[:, q], xn2[:, bass.ds(i * 4 + 2 * q, 2), :]).then_inc(sem("xdisp"), 1)
            gp.wait_ge(sem("layer1_in"), 16 * 10)
            gp.wait_ge(sem("xeT"), 2 * PAIRS + 4)
            gp.memset(shared3[:], 0.0).then_inc(sem("pads_zero"), 1)
            with gp.Fori(0, B // 4) as i:
                gp.wait_ge(sem("b_xn"), i * 4 + 4)
                for p in range(4):
                    hp = h[:, bass.ds(i * 4 + p, 1), :]
                    gp.tensor_tensor(hp, hp, b_proj1[:].unsqueeze(1), ALU.add).then_inc(sem("h_biased"), 1)

        @block.tensor
        def _(pe):
            pe.sem_inc(sem("disp_ps"), 4)
            pe.sem_inc(sem("eo_ps"), 4)
            pe.sem_inc(sem("b_h"), 2)
            pe.sem_inc(sem("s_xt_ps"), 1)
            pe.wait_ge(sem("lnwb_in"), 32)
            for t in range(W_TILES):
                if t % 10 == 0 and t < 30:
                    pe.wait_ge(sem(f"wtok_in{t // 10}"), 16)
                nc.tensor.matmul(PS[:, 0, 0:D], ln_b[:, t:t + 1].to_broadcast([128, 128]), w_tok[:, t],
                                 start=(t == 0), stop=False)
            pe.wait_ge(sem("wtok2_in"), 16)
            nc.tensor.matmul(PS[:, 0, 0:D], ln_b[0:HALO2, W_TILES:W_TILES + 1].to_broadcast([HALO2, 128]), w_tok2[:],
                             start=False, stop=True).then_inc(sem("bias_row_ps"), 1)
            pe.wait_ge(sem("w_eff"), KT)
            for t in range(KT):
                rows = 128 if t < KT - 1 else HALO2
                mm = nc.tensor.matmul(PS[:, 1, 0:D], ones[0:rows], w_eff[0:rows, t, 0:D], start=(t == 0), stop=(t == KT - 1))
            mm.then_inc(sem("col_sum_ps"), 1)
            pe.wait_ge(sem("mult_ready"), 1)
            with pe.Fori(0, PAIRS // 2) as i:
                for q in range(2):
                    pe.wait_ge(sem(f"x_in{q}"), i * 32 + 32)
                    pe.wait_ge(sem("tok_mid"), i * 2 + q + 1)
                    for t in range(KT):
                        rows = 128 if t < KT - 1 else HALO2
                        nc.tensor.matmul(PS[:, 2 + q, 0:D + 1], x_k[0:rows, q, t], w_eff[0:rows, t],
                                         start=(t == 0), stop=(t == KT - 1))
                    pe.wait_ge(sem("x_sq"), i * 2 + q + 1)
                    for t in range(KT):
                        rows = 128 if t < KT - 1 else HALO2
                        mm = nc.tensor.matmul(PS[:, 2 + q, 200:201], x_sq[0:rows, q, t], const("mult")[0:rows, t:t + 1],
                                              start=(t == 0), stop=(t == KT - 1))
                    mm.then_inc(sem("tok_ps"), 1)

            pe.wait_ge(sem("attn0_in"), 16 * 7)
            pe.wait_ge(sem("pads_zero"), 4)
            def route_products(i):
                for q in range(2):
                    pe.wait_ge(sem("r_xn"), i * 4 + 2 * q + 2)
                    if not isinstance(i, int):
                        pe.wait_ge(sem("a_vexp"), i * 4 + 2 * q + 2)
                    for p in range(2):
                        for kh in range(2):
                            mm = flip(PS[0:HD, 4 * q + 3, (kh * 2 + p) * N:(kh * 2 + p + 1) * N],
                                      xnr[:, 2 * q + p, kh * HD:(kh + 1) * HD])
                    mm.then_inc(sem("r_xnT_ps"), 1)
                for q in range(2):
                    pe.wait_ge(sem("r_xnT"), i * 2 + q + 1)
                    for p in range(2):
                        for kh in range(2):
                            mm = nc.tensor.matmul(PS[0:N, 4 * q + 3, 4 * N + p * E:4 * N + (p + 1) * E],
                                                  xnT[:, q, kh, p * N:(p + 1) * N], w_router[:, kh],
                                                  start=(kh == 0), stop=(kh == 1))
                    mm.then_inc(sem("r_logit_ps"), 1)

            with pe.Fori(0, B // 4) as i:
                for q in range(2):
                    pe.wait_ge(sem("a_xn"), i * 4 + 2 * q + 2)
                    for p in range(2):
                        for kh in range(2):
                            mm = flip(PS[0:HD, 4 * q, (kh * 2 + p) * N:(kh * 2 + p + 1) * N],
                                      xn[:, 2 * q + p, kh * HD:(kh + 1) * HD])
                    mm.then_inc(sem("a_xnT_ps"), 1)
                for q in range(2):
                    pe.wait_ge(sem("a_xnT"), i * 2 + q + 1)
                    for kh in range(2):
                        mm = nc.tensor.matmul(PS[0:C1, 4 * q + 1, 0:2 * N], w_red[:, kh], xnT[:, q, kh],
                                              start=(kh == 0), stop=(kh == 1))
                    mm.then_inc(sem("a_xr_ps"), 1)
                for q in range(2):
                    pe.wait_ge(sem("a_xrT"), i * 4 + 2 * q + 1)
                    for j in range(2):
                        mm = nc.tensor.matmul(PS[0:C1, 4 * q, j * 2 * N:(j + 1) * 2 * N], w_qkv0[:, j * C1:(j + 1) * C1],
                                              xrT[:, q], start=True, stop=True)
                    mm.then_inc(sem("a_qk_ps"), 1)
                for q in range(2):
                    pe.wait_ge(sem("a_xrT"), i * 4 + 2 * q + 2)
                    for p in range(2):
                        for s in range(SEGS):
                            mm = nc.tensor.matmul(PS[0:GRP * SEG, 4 * q + 2 + p, s * C1:(s + 1) * C1],
                                                  xr_rep[:, q, p * SEGS + s].rearrange("c r t -> c (r t)"),
                                                  w_qkv0[:, 2 * C1:3 * C1], start=True, stop=True)
                        mm.then_inc(sem("a_v_ps"), 1)
                for q in range(2):
                    pe.wait_ge(sem("a_qT"), i * 2 + q + 1)
                    pe.wait_ge(sem("a_kexp"), i * 2 + q + 1)
                    stand(pe)
                    for g in range(NGRP):
                        if g == 2:
                            pe.wait_ge(sem("a_vexp"), i * 4 + 2 * q + 1)
                            stand(pe)
                        rows = slice(g * 32, g * 32 + 32)
                        for p in range(2):
                            for s in range(SEGS):
                                mm = nc.tensor.matmul(
                                    PS[s * 32:s * 32 + 32, 4 * q + g, p * GRP * SEG:(p + 1) * GRP * SEG],
                                    qT[rows, q, p, s], k_exp[rows, q, :, p * N + s * SEG:p * N + (s + 1) * SEG],
                                    start=True, stop=True)
                    mm.then_inc(sem("a_s_ps"), 1)
                route_products(i)
                for q in range(2):
                    pe.wait_ge(sem("a_prob"), i * 2 + q + 1)
                    pe.wait_ge(sem("r_logit"), i * 2 + q + 1)
                    pe.wait_ge(sem("a_vexp"), i * 4 + 2 * q + 2)
                    for p in range(2):
                        for g in range(NGRP):
                            mm = flip(PS[0:GRP * SEG, 4 * q + (0 if p else 3), g * 128:(g + 1) * 128], prob[:, q, g, p])
                        mm.then_inc(sem("a_probT_ps"), 1)
                for q in range(2):
                    for p in range(2):
                        pe.wait_ge(sem("a_probT"), i * 4 + 2 * q + p + 1)
                        for s in range(SEGS):
                            for g in range(NGRP):
                                mm = nc.tensor.matmul(
                                    PS[g * 32:g * 32 + 32, 4 * q + 1, p * N + s * SEG:p * N + (s + 1) * SEG],
                                    v_exp[:, q, p, s, g * 32:g * 32 + 32], probT[:, q, p, g, s * PADSEG:s * PADSEG + SEG],
                                    start=True, stop=True)
                    mm.then_inc(sem("a_oT_ps"), 1)
                for q in range(2):
                    pe.wait_ge(sem("a_oT"), i * 2 + q + 1)
                    for p in range(2):
                        mm = nc.tensor.matmul(PS[0:N, 4 * q + 2, p * D:(p + 1) * D], oT[:, q, p * N:(p + 1) * N], w_proj0[:],
                                              start=True, stop=True)
                    mm.then_inc(sem("a_proj_ps"), 1)
            route_products(B // 4)

            pe.wait_ge(sem("r_choice"), 2)
            tri, one96 = const("tri", N), ones[0:N, 0:N]
            first, second = r_e[:, 2].rearrange("t (g p) e -> t p g e", p=2), r_e[:, 4].rearrange("t (g p) e -> t p g e", p=2)
            for k, p, terms in [(0, 0, [(tri, first[:, 0])]),
                                (0, 1, [(one96, first[:, 0]), (tri, first[:, 1])]),
                                (1, 0, [(one96, first[:, 0]), (one96, first[:, 1]), (tri, second[:, 0])]),
                                (1, 1, [(one96, first[:, 0]), (one96, first[:, 1]), (one96, second[:, 0]),
                                        (tri, second[:, 1])])]:
                dst = PS[0:N, 3, (k * 2 + p) * PAIRS * E:(k * 2 + p + 1) * PAIRS * E]
                for j, (lhs, rhs) in enumerate(terms):
                    mm = nc.tensor.matmul(dst, lhs, rhs, start=(j == 0), stop=(j == len(terms) - 1))
            mm.then_inc(sem("r_count_ps"), 1)

            with pe.Fori(0, PAIRS // 2) as i:
                for q in range(2):
                    pe.wait_ge(sem("xdisp"), i * 2 + q + 1)
                    pe.wait_ge(sem("onehot"), i * 4 + 2 * q + 2)
                    pe.wait_ge(sem("xeT"), i * 4 + 2 * q + 2)
                    for dh in range(2):
                        for p in range(2):
                            mm = nc.tensor.matmul(PS[0:HD, 4 + 2 * q + dh, 0:E * CAP],
                                                  x_disp[:, q, p, dh * HD:(dh + 1) * HD], onehot[:, q, p],
                                                  start=(p == 0), stop=(p == 1))
                        mm.then_inc(sem("disp_ps"), 1)

            pe.wait_ge(sem("xeT"), 2 * PAIRS + 4)
            with pe.Fori(0, E // 2) as i:
                for q in range(2):
                    pe.wait_ge(sem(f"wexp_in{q}"), i * 32 + 32)
                    for f in range(FT):
                        pe.wait_ge(sem("hidT"), i * 2 * FT + q * FT + f + 1)
                        for kh in range(2):
                            mm = nc.tensor.matmul(PS[:, f % 2, 0:SLOTS], wi_sl[:, q, kh, f * 128:(f + 1) * 128],
                                                  xeT[:, kh, bass.ds(i * 2 + q, 1)].rearrange("k e g c -> k (e g c)"),
                                                  start=(kh == 0), stop=(kh == 1))
                        mm.then_inc(sem("hid_ps"), 1)
                    for half in range(2):
                        pe.wait_ge(sem("e_out"), i * 8 + 4 * q + 2 * half + 2)
                        for gp_ in range(2):
                            for f in range(FT):
                                if half == 0 and gp_ == 0:
                                    pe.wait_ge(sem("hidT"), i * 2 * FT + q * FT + f + 3)
                                for z in range(2):
                                    g = half * 4 + gp_ * 2 + z
                                    mm = nc.tensor.matmul(PS[64 * z:64 * z + CAP, 2 + half, gp_ * D:(gp_ + 1) * D],
                                                          hidT[:, q, f, g * CAP:(g + 1) * CAP], wo_sl[:, q, f],
                                                          start=(f == 0), stop=(f == FT - 1), skip_group_check=True)
                        mm.then_inc(sem("eo_ps"), 1)

            pe.wait_ge(sem("e_out"), 4 * E + 4)
            pe.wait_ge(sem("layer1_in"), 16 * 10)
            def turn_comb(i):
                for q in range(2):
                    for p in range(2):
                        pe.wait_ge(sem("comb"), i * 4 + 2 * q + p + 1)
                        for ep in range(E // 2):
                            mm = flip(PS[:, 4 * q + p, ep * N:(ep + 1) * N],
                                      comb[:, q, p, 2 * ep:2 * ep + 2].rearrange("t e c -> t (e c)"))
                        mm.then_inc(sem("combT_ps"), 1)

            def combine(i):
                for q in range(2):
                    for p in range(2):
                        pe.wait_ge(sem("combT"), i * 4 + 2 * q + p + 1)
                        for ep in range(E // 2):
                            mm = nc.tensor.matmul(PS[0:N, 4 * q + 2, p * D:(p + 1) * D], combT[:, q, p, ep],
                                                  e_out[:, bass.ds(i * 2 + q, 1), ep].rearrange("s g d -> s (g d)"),
                                                  start=(ep == 0), stop=(ep == E // 2 - 1))
                    mm.then_inc(sem("moe_ps"), 1)

            def linear_inputs(i):
                for q in range(2):
                    pe.wait_ge(sem("b_xn"), i * 4 + 2 * q + 2)
                    for p in range(2):
                        for kh in range(2):
                            mm = flip(PS[0:HD, 4 * q + 3, (kh * 2 + p) * N:(kh * 2 + p + 1) * N],
                                      xn[:, 2 * q + p, kh * HD:(kh + 1) * HD])
                    mm.then_inc(sem("b_xnT_ps"), 1)
                for q in range(2):
                    pe.wait_ge(sem("b_xnT"), i * 2 + q + 1)
                    pe.wait_ge(sem("b_h"), i * 2 + q + 1)
                    for p in range(2):
                        for kh in range(2):
                            mm = nc.tensor.matmul(PS[0:N, 4 * q + p, 0:2 * D], xnT[:, q, kh, p * N:(p + 1) * N],
                                                  w_kv1[:, kh], start=(kh == 0), stop=(kh == 1))
                        mm.then_inc(sem("b_kv_ps"), 1)
                    for mh in range(2):
                        for kh in range(2):
                            mm = nc.tensor.matmul(PS[0:HD, 4 * q + 2, mh * 2 * N:(mh + 1) * 2 * N],
                                                  w_q1[:, kh, mh * HD:(mh + 1) * HD], xnT[:, q, kh],
                                                  start=(kh == 0), stop=(kh == 1))
                    mm.then_inc(sem("b_q_ps"), 1)

            def keys_values(i):
                for q in range(2):
                    for p in range(2):
                        pe.wait_ge(sem("b_kv"), i * 4 + 2 * q + p + 1)
                        for mh in range(2):
                            mm = nc.tensor.matmul(PS[0:HD, 4 * q + 3, (p * 2 + mh) * HD:(p * 2 + mh + 1) * HD],
                                                  kv1[:, q, p, mh * HD:(mh + 1) * HD],
                                                  kv1[:, q, p, D + mh * HD:D + (mh + 1) * HD], start=True, stop=True)
                        pe.wait_ge(sem("b_absk"), i * 4 + 2 * q + p + 1)
                        for mh in range(2):
                            at = 4 * HD + p * 2 + mh
                            mm = nc.tensor.matmul(PS[0:HD, 4 * q + 3, at:at + 1], abs_k[:, q, p, mh * HD:(mh + 1) * HD],
                                                  ones[0:N, 0:1], start=True, stop=True)
                    mm.then_inc(sem("b_kvp_ps"), 1)

            def linear_outputs(i):
                for q in range(2):
                    pe.wait_ge(sem("b_kvbd"), i * 8 + 4 * q + 4)
                    pe.wait_ge(sem("b_q1T"), i * 2 + q + 1)
                    for p in range(2):
                        for mh in range(2):
                            mm = nc.tensor.matmul(PS[0:HD, 4 * q, (p * 2 + mh) * N:(p * 2 + mh + 1) * N],
                                                  kv_bd[:, q, p, mh], q1T[:, q, mh, p * N:(p + 1) * N],
                                                  start=True, stop=True)
                    mm.then_inc(sem("b_oT_ps"), 1)
                for q in range(2):
                    pe.wait_ge(sem("b_o1T"), i * 2 + q + 1)
                    for p in range(2):
                        for mh in range(2):
                            mm = nc.tensor.matmul(PS[0:N, 4 * q + 1, p * D:(p + 1) * D], o1T[:, q, p, mh], w_proj1[:, mh],
                                                  start=(mh == 0), stop=(mh == 1))
                    mm.then_inc(sem("b_proj_ps"), 1)

            LAST = B // 4 - 1
            turn_comb(0)
            combine(0)
            with pe.Fori(0, LAST) as i:
                linear_inputs(i)
                pe.wait_ge(sem("b_kv"), i * 4 + 4)
                pe.wait_ge(sem("b_absk"), i * 4 + 4)
                turn_comb(i + 1)
                keys_values(i)
                pe.wait_ge(sem("b_q1T"), i * 2 + 2)
                combine(i + 1)
                linear_outputs(i)
            linear_inputs(LAST)
            keys_values(LAST)
            linear_outputs(LAST)

            pe.wait_ge(sem("slot_n"), 2)
            def soft_products(i, r):
                for p in range(4):
                    pe.wait_ge(sem("s_xs"), i * 4 + p + 1)
                    for kh in range(2):
                        mm = flip(PS[0:HD, kh, p * N:(p + 1) * N], xs[:, r, p, kh * HD:(kh + 1) * HD])
                mm.then_inc(sem("s_xsT_ps"), 1)
                pe.wait_ge(sem("s_xsT"), i * 2 + 2)
                for p in range(4):
                    for kh in range(2):
                        mm = nc.tensor.matmul(PS[0:N, 2, p * NP:(p + 1) * NP], xsT[:, kh, p * N:(p + 1) * N], slot_n[:, kh],
                                              start=(kh == 0), stop=(kh == 1))
                mm.then_inc(sem("s_log_ps"), 1)
                for kh in range(2):
                    for p in range(4):
                        mm = nc.tensor.matmul(PS[p * NP:(p + 1) * NP, 3, 0:N], slot_n[:, kh], xsT[:, kh, p * N:(p + 1) * N],
                                              start=(kh == 0), stop=(kh == 1), skip_group_check=True)
                mm.then_inc(sem("s_logT_ps"), 1)
                pe.wait_ge(sem("s_dspT"), i + 1)
                flip(PS[0:N, 4, 0:128], dspT[:]).then_inc(sem("s_dsp_ps"), 1)
                pe.wait_ge(sem("s_cmb"), i + 1)
                flip(PS[:, 5, 0:N], cmb[:].rearrange("t p n -> t (p n)")).then_inc(sem("s_cmbT_ps"), 1)
                pe.wait_ge(sem("s_dsp"), i + 1)
                for p in range(4):
                    for dh in range(2):
                        mm = nc.tensor.matmul(PS[0:HD, 6, dh * 128 + p * NP:dh * 128 + (p + 1) * NP],
                                              xs[:, r, p, dh * HD:(dh + 1) * HD], dsp[:, p * NP:(p + 1) * NP],
                                              start=True, stop=True)
                mm.then_inc(sem("s_xt_ps"), 1)

            with pe.Fori(0, 2) as i:
                for r in range(2):
                    soft_products(i * 2 + r, r)
            pe.wait_ge(sem("s_xtT"), 4)
            for mh in range(2):
                for kh in range(2):
                    mm = nc.tensor.matmul(PS[0:HD, mh], w_down[:, kh, mh * HD:(mh + 1) * HD], x_tT[:, kh],
                                          start=(kh == 0), stop=(kh == 1))
                mm.then_inc(sem("s_hid_ps"), 1)
            pe.wait_ge(sem("s_hidm"), 2)
            for j in range(4):
                if j >= 2:
                    pe.wait_ge(sem("s_yt"), j - 1)
                for mh in range(2):
                    mm = nc.tensor.matmul(PS[:, 2 + j % 2, 0:D], hidS[:, mh, j * 128:(j + 1) * 128], w_up[:, mh],
                                          start=(mh == 0), stop=(mh == 1))
                mm.then_inc(sem("s_yt_ps"), 1)
            for b in range(B):
                j, p = b // 4, b % 4
                pe.wait_ge(sem("s_yt"), j + 1)
                if b >= 4:
                    pe.wait_ge(sem("y_added"), b - 3)
                rows = slice(p * NP, (p + 1) * NP)
                nc.tensor.matmul(PS[0:N, 4 + b % 4, 0:D], cmbT[rows, j], y_t[rows, j], start=True,
                                 stop=True).then_inc(sem("s_y_ps"), 1)

        @block.scalar
        def _(act):
            def rsqrt_seed(var, tmp, dst, eps, done):
                nc.scalar.activation(tmp, var, ACT.Ln, bias=eps).then_inc(sem("act_ln"), 1)
                act.wait_ge(sem("act_ln"), done)
                return nc.scalar.activation(dst, tmp, ACT.Exp, scale=-0.5)

            act.sem_inc(sem("xeT"), 4)
            act.sem_inc(sem("hidT"), 2)
            eps = eps_col[:, 0:1]
            act.preload_act_table_set("natural_log_exp_and_others")
            act.wait_ge(sem("eps_ready"), 2)
            with act.Fori(0, PAIRS // 2) as i:
                for q in range(2):
                    act.wait_ge(sem(f"x_in{q}"), i * 32 + 32)
                    nc.scalar.activation(x_sq[:, q, 0:KT - 1], x_k[:, q, 0:KT - 1], ACT.Square)
                    nc.scalar.activation(x_sq[0:HALO2, q, KT - 1], x_k[0:HALO2, q, KT - 1], ACT.Square).then_inc(sem("x_sq"), 1)
                    act.wait_ge(sem("tok_var"), i * 2 + q + 1)
                    rsqrt_seed(tok_stat[:, 3:4], tok_stat[:, 4:5], tok_stat[:, 5:6], eps,
                               i * 2 + q + 1).then_inc(sem("tok_seed"), 1)
            LN0 = PAIRS
            act.wait_ge(sem("attn0_in"), 16 * 7)
            act.wait_ge(sem("pads_zero"), 4)
            def norm_seed(i):
                act.wait_ge(sem("a_mv"), i * 4 + 4)
                rsqrt_seed(mv[:, :, 1], rs_tmp[0:N, 0], rs_tmp[0:N, 1], eps[0:N],
                           i * 2 + LN0 + 1).then_inc(sem("a_seed"), 1)

            def route_seed(i):
                act.wait_ge(sem("r_mv"), i * 4 + 4)
                rsqrt_seed(mv[:, :, 1], rs_tmp[0:N, 0], rs_tmp[0:N, 1], eps[0:N],
                           i * 2 + LN0 + 2).then_inc(sem("r_seed"), 1)

            def route_drain(i):
                for q in range(2):
                    act.wait_ge(sem("r_xnT_ps"), i * 2 + q + 1)
                    nc.scalar.copy(xnT[:, q].rearrange("k a t -> k (a t)"), PS[0:HD, 4 * q + 3, 0:4 * N]
                                   ).then_inc(sem("r_xnT"), 1)
                for q in range(2):
                    act.wait_ge(sem("r_logit_ps"), i * 2 + q + 1)
                    nc.scalar.copy(logits_all[:, bass.ds(i * 4 + 2 * q, 2), :],
                                   PS[0:N, 4 * q + 3, 4 * N:4 * N + 2 * E].rearrange("t (p e) -> t p e", p=2)
                                   ).then_inc(sem("r_logit"), 1)

            norm_seed(0)
            with act.Fori(0, B // 4) as i:
                for q in range(2):
                    act.wait_ge(sem("a_xnT_ps"), i * 2 + q + 1)
                    nc.scalar.copy(xnT[:, q].rearrange("k a t -> k (a t)"), PS[0:HD, 4 * q, 0:4 * N]).then_inc(sem("a_xnT"), 1)
                route_seed(i)
                for q in range(2):
                    act.wait_ge(sem("a_xr_ps"), i * 2 + q + 1)
                    nc.scalar.activation(xrT[:, q], PS[0:C1, 4 * q + 1, 0:2 * N], ACT.Identity, bias=b_red[:]
                                         ).then_inc(sem("a_xrT"), 1)
                    nc.scalar.activation(xr_rep[:, q], PS[0:C1, 4 * q + 1, 0:2 * N].rearrange("c (a t) -> c a t", t=SEG)
                                         .unsqueeze(2).to_broadcast([C1, 2 * SEGS, GRP, SEG]), ACT.Identity, bias=b_red[:]
                                         ).then_inc(sem("a_xrT"), 1)
                for q in range(2):
                    act.wait_ge(sem("a_kexp"), i * 2 + q + 1)
                    nc.scalar.activation(qT[:, q, :, :, 0:SEG],
                                         PS[0:C1, 4 * q, 0:2 * N].rearrange("c (p s t) -> c p s t", p=2, s=SEGS),
                                         ACT.Identity, bias=b_qkv0[:, 0:1]).then_inc(sem("a_qT"), 1)
                for q in range(2):
                    act.wait_ge(sem("a_sub"), i * 2 + q + 1)
                    nc.scalar.activation(prob[:, q], prob[:, q], ACT.Exp, scale=SCALE0).then_inc(sem("a_exp"), 1)
                route_drain(i)
                norm_seed(i + 1)
                for q in range(2):
                    for p in range(2):
                        act.wait_ge(sem("a_probT_ps"), i * 4 + 2 * q + p + 1)
                        nc.scalar.copy(probT[:, q, p].rearrange("k g t -> k (g t)"),
                                       PS[0:GRP * SEG, 4 * q + (0 if p else 3), 0:NGRP * 128]).then_inc(sem("a_probT"), 1)
                for q in range(2):
                    act.wait_ge(sem("a_oT_ps"), i * 2 + q + 1)
                    nc.scalar.activation(oT[:, q], PS[0:C1, 4 * q + 1, 0:2 * N], ACT.Identity, bias=b_qkv0[:, 2:3]
                                         ).then_inc(sem("a_oT"), 1)
            route_seed(B // 4)
            route_drain(B // 4)
            LN1 = LN0 + 2 * (B // 4) + 2
            act.wait_ge(sem("r_shift"), 1)
            nc.scalar.activation(r_e[:, 1], r_e[:, 0], ACT.Exp).then_inc(sem("r_exp"), 1)
            with act.Fori(0, PAIRS // 2) as i:
                for q in range(2):
                    for dh in range(2):
                        act.wait_ge(sem("disp_ps"), i * 4 + 2 * q + dh + 5)
                        nc.scalar.copy(xeT[:, dh, :, bass.ds(i * 2 + q, 1)].rearrange("k e g c -> k e (g c)"),
                                       PS[0:HD, 4 + 2 * q + dh, 0:E * CAP].rearrange("k (e c) -> k e c", e=E)
                                       ).then_inc(sem("xeT"), 1)
            with act.Fori(0, E // 2) as i:
                for q in range(2):
                    for f in range(FT):
                        act.wait_ge(sem("hid_ps"), i * 2 * FT + q * FT + f + 1)
                        if f == 0:
                            act.wait_ge(sem("eo_ps"), i * 4 + 2 * q + 2)
                        nc.scalar.activation(hidT[:, q, f], PS[:, f % 2, 0:SLOTS], ACT.Relu).then_inc(sem("hidT"), 1)
            def drain_comb(i):
                for q in range(2):
                    for p in range(2):
                        act.wait_ge(sem("combT_ps"), i * 4 + 2 * q + p + 1)
                        nc.scalar.copy(combT[:, q, p].rearrange("s e t -> s (e t)"), PS[:, 4 * q + p, 0:E // 2 * N]
                                       ).then_inc(sem("combT"), 1)

            def linear_seed(i):
                act.wait_ge(sem("b_mv"), i * 4 + 4)
                rsqrt_seed(mv[:, :, 1], rs_tmp[0:N, 0], rs_tmp[0:N, 1], eps[0:N], i + LN1 + 1).then_inc(sem("b_seed"), 1)

            def drain_inputs(i):
                for q in range(2):
                    act.wait_ge(sem("b_xnT_ps"), i * 2 + q + 1)
                    nc.scalar.copy(xnT[:, q].rearrange("k a t -> k (a t)"), PS[0:HD, 4 * q + 3, 0:4 * N]
                                   ).then_inc(sem("b_xnT"), 1)
                for q in range(2):
                    for p in range(2):
                        act.wait_ge(sem("b_kv"), i * 4 + 2 * q + p + 1)
                        nc.scalar.activation(abs_k[:, q, p], PS[0:N, 4 * q + p, 0:D], ACT.Abs).then_inc(sem("b_absk"), 1)
                    act.wait_ge(sem("b_q_ps"), i * 2 + q + 1)
                    nc.scalar.copy(q1T[:, q].rearrange("k a t -> k (a t)"), PS[0:HD, 4 * q + 2, 0:4 * N]).then_inc(sem("b_q1T"), 1)

            def drain_outputs(i):
                for q in range(2):
                    act.wait_ge(sem("b_oT_ps"), i * 2 + q + 1)
                    nc.scalar.copy(o1T[:, q].rearrange("k p a t -> k (p a t)"), PS[0:HD, 4 * q, 0:4 * N]
                                   ).then_inc(sem("b_o1T"), 1)

            LAST = B // 4 - 1
            drain_comb(0)
            linear_seed(0)
            with act.Fori(0, LAST) as i:
                drain_inputs(i)
                drain_comb(i + 1)
                drain_outputs(i)
                linear_seed(i + 1)
            drain_inputs(LAST)
            drain_outputs(LAST)
            LN2 = LN1 + B // 4
            act.wait_ge(sem("slot_ss"), 1)
            rsqrt_seed(slot_s[:, 0], slot_s[:, 1], slot_s[:, 2], 0.0, LN2 + 1).then_inc(sem("slot_seed"), 1)
            LN3 = LN2 + 1
            def soft_seeds(i):
                act.wait_ge(sem("s_mv"), i * 4 + 4)
                rsqrt_seed(mv[:, :, 1], rs_tmp[0:N, 0], rs_tmp[0:N, 1], eps[0:N], i * 2 + LN3 + 1).then_inc(sem("s_seed"), 1)
                act.wait_ge(sem("s_varmax"), i + 1)
                rsqrt_seed(rs_tmp[0:N, 5], rs_tmp[0:N, 6], rs_tmp[0:N, 7], 0.0, i * 2 + LN3 + 2).then_inc(sem("s_seed"), 1)

            soft_seeds(0)
            with act.Fori(0, 4) as i:
                act.wait_ge(sem("s_xsT_ps"), i + 1)
                for kh in range(2):
                    nc.scalar.copy(xsT[:, kh], PS[0:HD, kh, 0:4 * N]).then_inc(sem("s_xsT"), 1)
                soft_seeds(i + 1)
                act.wait_ge(sem("s_dmax"), i + 1)
                nc.scalar.activation(dspT[:], PS[:, 3, 0:N], ACT.Exp, bias=d_st[:, 0:1],
                                     accum_out=d_st[:, 1:2]).then_inc(sem("s_dexp"), 1)
                act.wait_ge(sem("s_csub"), i + 1)
                nc.scalar.activation(cmb[:], cmb[:], ACT.Exp).then_inc(sem("s_cexp"), 1)
                act.wait_ge(sem("s_dsp_ps"), i + 1)
                nc.scalar.copy(dsp[:], PS[0:N, 4, 0:128]).then_inc(sem("s_dsp"), 1)
                act.wait_ge(sem("s_cmbT_ps"), i + 1)
                nc.scalar.copy(cmbT[:, bass.ds(i, 1), :], PS[:, 5:6, 0:N]).then_inc(sem("s_cmbT"), 1)
                act.wait_ge(sem("s_xt_ps"), i + 2)
                nc.scalar.copy(x_tT[:, :, bass.ds(i * 128, 128)], PS[0:HD, 6, 0:256].rearrange("k (a s) -> k a s", a=2)
                               ).then_inc(sem("s_xtT"), 1)
            for mh in range(2):
                act.wait_ge(sem("s_hid_ps"), mh + 1)
                nc.scalar.activation(hidS[:, mh], PS[0:HD, mh], ACT.Gelu, bias=b_down[:, mh:mh + 1]).then_inc(sem("s_gelu"), 1)

        @block.vector
        def _(ve):

            def refine(var, eps, seed, t, dst, base, per, i, k):
                def tick(ins, j):
                    ins.then_inc(sem("dve_newton"), 1)
                    ve.wait_ge(sem("dve_newton"), i * (4 * per) + (base + 4 * k + j))
                tick(ve.scalar_tensor_tensor(t[0], var, eps, seed, ALU.add, ALU.mult), 1)
                tick(ve.tensor_tensor(t[1], t[0], seed, ALU.mult), 2)
                tick(ve.tensor_scalar(t[2], t[1], -0.5, 1.5, ALU.mult, ALU.add), 3)
                tick(ve.tensor_tensor(dst, t[2], seed, ALU.mult), 4)

            ve.sem_inc(sem("e_out"), 4)
            ve.memset(eps_col[:, 0:1], LN_EPS).then_inc(sem("eps_ready"), 1)
            ve.memset(eps_col[:, 1:2], 0.0).then_inc(sem("eps_ready"), 1)
            ve.wait_ge(sem("lnwb_in"), 32)
            ve.wait_ge(sem("wtok_in0"), 16)
            n = 0
            for t in range(KT - 1):
                shifts = range(5 * t, 5 * t + 5) if t < KT_IN else range(5 * t, 5 * t + 1)
                for k in shifts:
                    if k in (10, 20):
                        ve.wait_ge(sem(f"wtok_in{k // 10}"), 16)
                    dst = w_eff[:, t, 0:D]
                    if k == shifts[0]:
                        ins = ve.tensor_scalar(dst, w_tok[:, k], ln_w[:, k:k + 1], None, ALU.mult)
                    else:
                        ve.wait_ge(sem("fold"), n)
                        ins = ve.scalar_tensor_tensor(dst, w_tok[:, k], ln_w[:, k:k + 1], dst, ALU.mult, ALU.add)
                    if k == shifts[-1]:
                        ins.then_inc(sem("w_eff"), 1)
                    else:
                        ins.then_inc(sem("fold"), 1)
                        n += 1
            ve.wait_ge(sem("wtok2_in"), 16)
            ve.tensor_scalar(w_eff[0:HALO2, KT - 1, 0:D], w_tok2[:], ln_w[0:HALO2, W_TILES:W_TILES + 1], None,
                             ALU.mult).then_inc(sem("w_eff"), 1)
            ve.wait_ge(sem("bias_row_ps"), 1)
            ve.wait_ge(sem("tokbias_in"), 16)
            ve.tensor_tensor(bias_row[:], PS[:, 0, 0:D], tok_bias[:], ALU.add).then_inc(sem("bias_row"), 1)
            ve.wait_ge(sem("col_sum_ps"), 1)
            ve.tensor_copy(col_sum[:], PS[:, 1, 0:D]).then_inc(sem("bias_row"), 1)
            ve.wait_ge(sem("bias_row"), 2)
            ve.sem_inc(sem("tok_mid"), 2)
            st = tok_stat
            with ve.Fori(0, PAIRS // 2) as i:
                for q in range(2):
                    ps = PS[:, 2 + q]
                    ve.wait_ge(sem("tok_ps"), i * 2 + q + 1)
                    ve.tensor_scalar(st[:, 0:1], ps[:, D:D + 1], -1.0 / PATCH_DIM, None, ALU.mult).then_inc(sem("tok_m"), 1)
                    ve.tensor_scalar(st[:, 1:2], ps[:, 200:201], 1.0 / PATCH_DIM, None, ALU.mult).then_inc(sem("tok_m"), 1)
                    ve.wait_ge(sem("tok_m"), i * 6 + q * 3 + 2)
                    ve.tensor_tensor(st[:, 2:3], st[:, 0:1], st[:, 0:1], ALU.mult).then_inc(sem("tok_m"), 1)
                    ve.wait_ge(sem("tok_m"), i * 6 + q * 3 + 3)
                    ve.tensor_tensor(st[:, 3:4], st[:, 1:2], st[:, 2:3], ALU.subtract).then_inc(sem("tok_var"), 1)
                    ve.scalar_tensor_tensor(tok_mid[:], col_sum[:], st[:, 0:1], ps[:, 0:D], ALU.mult, ALU.add
                                            ).then_inc(sem("tok_mid"), 1)
                    ve.wait_ge(sem("tok_seed"), i * 2 + q + 1)
                    refine(st[:, 3:4], LN_EPS, st[:, 5:6], [st[:, 6:7], st[:, 7:8], st[:, 8:9]], st[:, 9:10], 0, 2, i, q)
                    ve.wait_ge(sem("tok_mid"), i * 2 + q + 3)
                    for p in range(2):
                        rows = slice(p * IMG_TOK, (p + 1) * IMG_TOK)
                        ve.scalar_tensor_tensor(h[0:IMG_TOK, bass.ds(i * 4 + 2 * q + p, 1), :].rearrange("t b d -> t (b d)"),
                                                tok_mid[rows], st[rows, 9:10], bias_row[rows], ALU.mult, ALU.add
                                                ).then_inc(sem("h_tok"), 1)
            NW0 = 4 * PAIRS

            def moments(i, np_, name, base, per, at=4):
                stand(ve)
                for p in range(np_):
                    ve.bn_stats(stat6[:, p], h_all[:, bass.ds(i * np_ + (at + p), 1), :].rearrange("t b d -> t (b d)")
                                ).then_inc(sem("stat6"), 1)
                for p in range(np_):
                    ve.wait_ge(sem("stat6"), i * per + (base + p + 1))
                    stand(ve)
                    ve.bn_aggr(mv[:, p], stat6[:, p]).then_inc(sem(name + "_mv"), 1)

            def normalize(i, np_, name, dst, scale, at=4):
                for p in range(np_):
                    ve.tensor_scalar(dst[:, p], h_all[:, bass.ds(i * np_ + (at + p), 1), :].rearrange("t b d -> t (b d)"),
                                     mv[:, p, 0:1], scale[0:N, p:p + 1], ALU.subtract, ALU.mult).then_inc(sem(name), 1)

            tmp4 = [rs_tmp[0:N, 2], rs_tmp[0:N, 3], rs_tmp[0:N, 4]]
            ve.wait_ge(sem("txt_in"), 16)
            ve.wait_ge(sem("h_tok"), B)
            ve.wait_ge(sem("attn0_in"), 16 * 7)
            hm = const("headmask", C1).unsqueeze(2).to_broadcast([C1, GRP, 2 * N])
            vm = const("vmask", GRP * SEG)
            every_key = [128, NGRP, 2 * GRP, SEG]

            def norm_rest(i):
                ve.wait_ge(sem("a_seed"), i + 1)
                refine(mv[:, :, 1], LN_EPS, rs_tmp[0:N, 1], tmp4, rs[0:N], NW0, 2, i, 0)
                normalize(i, 4, "a_xn", xn, rs)

            def route_norm(i):
                moments(i, 4, "r", 4, 8, at=0)
                ve.wait_ge(sem("r_seed"), i + 1)
                refine(mv[:, :, 1], LN_EPS, rs_tmp[0:N, 1], tmp4, rs[0:N], NW0, 2, i, 1)
                normalize(i, 4, "r_xn", xnr, rs, at=0)

            ve.wait_ge(sem("pads_zero"), 4)
            moments(0, 4, "a", 0, 8)
            norm_rest(0)
            with ve.Fori(0, B // 4) as i:
                route_norm(i)
                for q in range(2):
                    ve.wait_ge(sem("a_qk_ps"), i * 2 + q + 1)
                    ve.scalar_tensor_tensor(k_exp[:, q], PS[0:C1, 4 * q, 2 * N:4 * N].unsqueeze(1).to_broadcast([C1, GRP, 2 * N]),
                                            b_qkv0[:, 1:2], hm, ALU.add, ALU.mult).then_inc(sem("a_kexp"), 1)
                for q in range(2):
                    for p in range(2):
                        ve.wait_ge(sem("a_v_ps"), i * 4 + 2 * q + p + 1)
                        ve.tensor_tensor(v_exp[:, q, p].rearrange("k s (g c) -> k (s g) c", g=NGRP),
                                         PS[0:GRP * SEG, 4 * q + 2 + p, 0:SEGS * C1].rearrange("k (a c) -> k a c", c=32),
                                         vm.unsqueeze(1).to_broadcast([GRP * SEG, SEGS * NGRP, 32]), ALU.mult
                                         ).then_inc(sem("a_vexp"), 1)
                for q in range(2):
                    s_ps = PS[:, 4 * q:4 * q + NGRP, 0:2 * GRP * SEG].rearrange("q g (h k) -> q g h k", k=SEG)
                    pr = prob[:, q].rearrange("q g p (h k) -> q g (p h) k", k=SEG)
                    ve.wait_ge(sem("a_s_ps"), i * 2 + q + 1)
                    ve.tensor_reduce(smax[:, q], s_ps, AX_X, ALU.max).then_inc(sem("a_max"), 1)
                    ve.wait_ge(sem("a_max"), i * 2 + q + 1)
                    ve.tensor_tensor(pr, s_ps, smax[:, q].unsqueeze(3).to_broadcast(every_key), ALU.subtract
                                     ).then_inc(sem("a_sub"), 1)
                moments(i + 1, 4, "a", 0, 8)
                for q in range(2):
                    pr = prob[:, q].rearrange("q g p (h k) -> q g (p h) k", k=SEG)
                    ve.wait_ge(sem("a_exp"), i * 2 + q + 1)
                    ve.tensor_reduce(ssum[:, q], pr, AX_X, ALU.add).then_inc(sem("a_sum"), 1)
                    ve.wait_ge(sem("a_sum"), i * 4 + 2 * q + 1)
                    ve.reciprocal(ssum[:, q], ssum[:, q]).then_inc(sem("a_sum"), 1)
                    ve.wait_ge(sem("a_sum"), i * 4 + 2 * q + 2)
                    ve.tensor_tensor(pr, pr, ssum[:, q].unsqueeze(3).to_broadcast(every_key), ALU.mult
                                     ).then_inc(sem("a_prob"), 1)
                ve.wait_ge(sem("a_xnT_ps"), i * 2 + 2)
                norm_rest(i + 1)
                for q in range(2):
                    ve.wait_ge(sem("a_proj_ps"), i * 2 + q + 1)
                    ve.wait_ge(sem("h_biased"), i * 4 + 4)
                    hp = h[:, bass.ds(i * 4 + 2 * q, 2), :]
                    ve.tensor_tensor(hp, hp, PS[0:N, 4 * q + 2, 0:2 * D].rearrange("t (p d) -> t p d", p=2), ALU.add
                                     ).then_inc(sem("a_h"), 1)
                ve.wait_ge(sem("r_kept"), i + 1)
                ve.wait_ge(sem("r_xnT_ps"), i * 2 + 2)
                ve.wait_ge(sem("a_h"), i * 2 + 2)
            route_norm(B // 4)
            NW1 = NW0 + 8 * (B // 4) + 8

            def wide(x):
                return x.unsqueeze(2).to_broadcast([N, B, E])

            step = [0]

            def then(ins):
                step[0] += 1
                ins.then_inc(sem("r_step"), 1)
                ve.wait_ge(sem("r_step"), step[0])

            rev = const("rev", N).unsqueeze(1).to_broadcast([N, B, E])
            ve.wait_ge(sem("r_logit"), PAIRS + 2)
            then(ve.tensor_reduce(r_top[:, 0], logits[:], AX_X, ALU.max))
            ve.tensor_tensor(r_e[:, 0], logits[:], wide(r_top[:, 0]), ALU.subtract).then_inc(sem("r_shift"), 1)

            def pick(src, best, tmp, dst):
                then(ve.tensor_tensor(tmp, src, wide(best), ALU.is_equal))
                then(ve.tensor_tensor(tmp, tmp, rev, ALU.mult))
                then(ve.tensor_reduce(r_top[:, 1], tmp, AX_X, ALU.max))
                return ve.tensor_tensor(dst, tmp, wide(r_top[:, 1]), ALU.is_equal)

            then(pick(logits[:], r_top[:, 0], r_e[:, 5], r_e[:, 2]))
            then(ve.scalar_tensor_tensor(r_e[:, 3], r_e[:, 2], -3e38, logits[:], ALU.mult, ALU.add))
            then(ve.tensor_reduce(r_top[:, 2], r_e[:, 3], AX_X, ALU.max))
            pick(r_e[:, 3], r_top[:, 2], r_e[:, 5], r_e[:, 4]).then_inc(sem("r_choice"), 2)
            ve.wait_ge(sem("r_choice"), 2)
            ve.wait_ge(sem("r_exp"), 1)
            then(ve.tensor_reduce(r_top[:, 3], r_e[:, 1], AX_X, ALU.add))
            then(ve.reciprocal(r_top[:, 4], r_top[:, 3]))
            then(ve.tensor_tensor(r_e[:, 0], r_e[:, 1], wide(r_top[:, 4]), ALU.mult))
            then(ve.tensor_tensor(r_e[:, 5], r_e[:, 2], r_e[:, 4], ALU.add))
            then(ve.tensor_tensor(gate_of[:], r_e[:, 0], r_e[:, 5], ALU.mult))
            ve.wait_ge(sem("r_count_ps"), 1)
            count = PS[0:N, 3, 0:4 * PAIRS * E].rearrange("t (k p g e) -> t k g p e", k=2, p=2, g=PAIRS)
            four = lambda x: x.rearrange("t (g p) e -> t g p e", p=2)
            then(ve.tensor_tensor(four(r_e[:, 0]), four(r_e[:, 2]), count[:, 0], ALU.mult))
            then(ve.tensor_tensor(four(r_e[:, 1]), four(r_e[:, 4]), count[:, 1], ALU.mult))
            then(ve.scalar_tensor_tensor(slot_of[:], r_e[:, 0], -1.0, r_e[:, 1], ALU.add, ALU.add))

            iota = const("iota", N).unsqueeze(1).to_broadcast([N, E, CAP])

            def place(b):
                return slot_of[:, bass.ds(b, 1), :].rearrange("t b e -> t (b e)").unsqueeze(2).to_broadcast([N, E, CAP])

            with ve.Fori(0, PAIRS // 2) as i:
                for q in range(2):
                    ve.wait_ge(sem("disp_ps"), i * 4 + 2 * q + 2)
                    for p in range(2):
                        ve.tensor_tensor(onehot[:, q, p].rearrange("t (e c) -> t e c", e=E), iota,
                                         place(i * 4 + (2 * q + p)), ALU.is_equal).then_inc(sem("onehot"), 1)
            ve.wait_ge(sem("pads_zero"), 4)
            with ve.Fori(0, E // 2) as i:
                for q in range(2):
                    for half in range(2):
                        ve.wait_ge(sem("eo_ps"), i * 4 + 2 * q + half + 5)
                        for z in range(2):
                            ve.tensor_copy(
                                e_out[64 * q:64 * q + CAP, half * 4 + z:half * 4 + z + 3:2, bass.ds(i, 1)].rearrange("s g e d -> s g (e d)"),
                                PS[64 * z:64 * z + CAP, 2 + half, 0:2 * D].rearrange("s (g d) -> s g d", g=2)
                            ).then_inc(sem("e_out"), 1)
            ve.wait_ge(sem("layer1_in"), 16 * 10)
            l1m = const("l1mask", HD)
            ve.wait_ge(sem("pads_zero"), 5)
            def build_comb(i):
                for q in range(2):
                    for p in range(2):
                        cm = comb[:, q, p, :, 0:CAP]
                        b = i * 4 + (2 * q + p)
                        ve.tensor_tensor(cm, iota, place(b), ALU.is_equal).then_inc(sem("comb_hot"), 1)
                        ve.wait_ge(sem("comb_hot"), i * 4 + 2 * q + p + 1)
                        g = gate_of[:, bass.ds(b, 1), :].rearrange("t b e -> t (b e)").unsqueeze(2).to_broadcast([N, E, CAP])
                        ve.tensor_tensor(cm, cm, g, ALU.mult).then_inc(sem("comb"), 1)

            def add_combined(i):
                for q in range(2):
                    ve.wait_ge(sem("moe_ps"), i * 2 + q + 1)
                    hp = h[:, bass.ds(i * 4 + 2 * q, 2), :]
                    ve.tensor_tensor(hp, hp, PS[0:N, 4 * q + 2, 0:2 * D].rearrange("t (p d) -> t p d", p=2), ALU.add
                                     ).then_inc(sem("moe_h"), 1)
                ve.wait_ge(sem("moe_h"), i * 2 + 2)
                moments(i, 4, "b", 2 * B + 8, 4)
                ve.wait_ge(sem("b_seed"), i + 1)
                refine(mv[:, :, 1], LN_EPS, rs_tmp[0:N, 1], tmp4, rs[0:N], NW1, 1, i, 0)
                normalize(i, 4, "b_xn", xn, rs)

            def linear_middle(i):
                for q in range(2):
                    for p in range(2):
                        ve.wait_ge(sem("b_kv_ps"), i * 4 + 2 * q + p + 1)
                        ve.tensor_copy(kv1[:, q, p], PS[0:N, 4 * q + p, 0:2 * D]).then_inc(sem("b_kv"), 1)
                for q in range(2):
                    dn = den[:, q]
                    c = i * 12 + 6 * q
                    ve.wait_ge(sem("b_q1T"), i * 2 + q + 1)
                    for mh in range(2):
                        ve.tensor_reduce(dn[:, 0].rearrange("k (p a) -> k a p", a=2)[:, mh],
                                         q1T[:, q, mh].rearrange("k (p t) -> k p t", p=2), AX_X, ALU.add,
                                         apply_absolute_value=True).then_inc(sem("b_den"), 1)
                    ve.wait_ge(sem("b_den"), c + 2)
                    ve.tensor_scalar(dn[:, 1], dn[:, 0], L1_EPS, None, ALU.max).then_inc(sem("b_den"), 1)
                    ve.wait_ge(sem("b_kvp_ps"), i * 2 + q + 1)
                    ve.tensor_scalar(dn[:, 2], PS[0:HD, 4 * q + 3, 4 * HD:4 * HD + 4], L1_EPS, None, ALU.max
                                     ).then_inc(sem("b_den"), 1)
                    ve.wait_ge(sem("b_den"), c + 4)
                    ve.reciprocal(dn[:, 3:5], dn[:, 1:3]).then_inc(sem("b_den"), 1)
                    ve.wait_ge(sem("b_den"), c + 5)
                    ve.tensor_tensor(dn[:, 5], dn[:, 3], dn[:, 4], ALU.mult).then_inc(sem("b_den"), 1)
                    ve.wait_ge(sem("b_den"), c + 6)
                    for p in range(2):
                        for mh in range(2):
                            j = p * 2 + mh
                            ve.scalar_tensor_tensor(kv_bd[:, q, p, mh], PS[0:HD, 4 * q + 3, j * HD:(j + 1) * HD],
                                                    dn[:, 5, j:j + 1], l1m, ALU.mult, ALU.mult).then_inc(sem("b_kvbd"), 1)

            def add_projected(i):
                for q in range(2):
                    ve.wait_ge(sem("b_proj_ps"), i * 2 + q + 1)
                    ve.wait_ge(sem("h_biased"), i * 4 + (B + 4))
                    hp = h[:, bass.ds(i * 4 + 2 * q, 2), :]
                    ve.tensor_tensor(hp, hp, PS[0:N, 4 * q + 1, 0:2 * D].rearrange("t (p d) -> t p d", p=2), ALU.add
                                     ).then_inc(sem("b_h"), 1)

            LAST = B // 4 - 1
            build_comb(0)
            add_combined(0)
            with ve.Fori(0, LAST) as i:
                ve.wait_ge(sem("combT_ps"), i * 4 + 4)
                build_comb(i + 1)
                linear_middle(i)
                add_combined(i + 1)
                add_projected(i)
            linear_middle(LAST)
            add_projected(LAST)
            NW2 = NW1 + 4 * (B // 4)

            ve.tensor_tensor(slot_sq[:], slot_raw[:], slot_raw[:], ALU.mult).then_inc(sem("slot_step"), 1)
            ve.wait_ge(sem("slot_step"), 1)
            ve.tensor_reduce(slot_s[:, 3].rearrange("k (a s) -> k a s", a=2),
                             slot_sq[:].rearrange("k a (n s) -> k a s n", n=NS), AX_X, ALU.add).then_inc(sem("slot_step"), 1)
            ve.wait_ge(sem("slot_step"), 2)
            ve.tensor_scalar(slot_s[:, 0], slot_s[:, 3], TINY, None, ALU.max).then_inc(sem("slot_ss"), 1)
            ve.wait_ge(sem("slot_seed"), 1)
            refine(slot_s[:, 0], 0.0, slot_s[:, 2], [slot_s[:, 4], slot_s[:, 5], slot_s[:, 1]], slot_s[:, 4], NW2, 0, 0, 0)
            NW3 = NW2 + 4
            ve.tensor_tensor(slot_s[:, 5], slot_s[:, 3], slot_s[:, 4], ALU.mult).then_inc(sem("slot_step"), 1)
            ve.wait_ge(sem("slot_step"), 3)
            ve.tensor_scalar(slot_s[:, 1], slot_s[:, 5], L2_EPS, None, ALU.add).then_inc(sem("slot_step"), 1)
            ve.wait_ge(sem("slot_step"), 4)
            ve.reciprocal(slot_s[:, 2], slot_s[:, 1]).then_inc(sem("slot_step"), 1)
            ve.wait_ge(sem("slot_step"), 5)
            ve.tensor_scalar(slot_s[:, 5], slot_s[:, 2], l_scale[:], None, ALU.mult).then_inc(sem("slot_step"), 1)
            ve.wait_ge(sem("slot_step"), 6)
            for a in range(2):
                ve.tensor_tensor(slot_n[:, a].rearrange("k (n s) -> k n s", n=NS),
                                 slot_raw[:, a].rearrange("k (n s) -> k n s", n=NS),
                                 slot_s[:, 5, a * PS_:(a + 1) * PS_].unsqueeze(1).to_broadcast([HD, NS, PS_]), ALU.mult
                                 ).then_inc(sem("slot_n"), 1)
            ve.wait_ge(sem("b_h"), PAIRS + 2)
            tmp4 = [rs_tmp[0:N, 2], rs_tmp[0:N, 3], rs_tmp[0:N, 4]]
            def soft_rows(i, r):
                moments(i, 4, "s", 3 * B + 8, 4)
                ve.wait_ge(sem("s_mv"), i * 4 + 4)
                ve.tensor_scalar(rs_tmp[0:N, 5], mv[:, :, 1], TINY, None, ALU.max).then_inc(sem("s_varmax"), 1)
                ve.wait_ge(sem("s_varmax"), i + 1)
                ve.wait_ge(sem("s_seed"), i * 2 + 2)
                refine(mv[:, :, 1], LN_EPS, rs_tmp[0:N, 1], tmp4, rs[0:N], NW3, 2, i, 0)
                refine(rs_tmp[0:N, 5], 0.0, rs_tmp[0:N, 7], tmp4, rs_tmp[0:N, 6], NW3, 2, i, 1)

                def tick(ins, j):
                    ins.then_inc(sem("s_scale"), 1)
                    ve.wait_ge(sem("s_scale"), i * 5 + j)
                tick(ve.tensor_tensor(rs_tmp[0:N, 2], mv[:, :, 1], rs_tmp[0:N, 6], ALU.mult), 1)
                tick(ve.scalar_tensor_tensor(rs_tmp[0:N, 3], rs_tmp[0:N, 2], float(D) ** 0.5, rs[0:N], ALU.mult, ALU.mult), 2)
                tick(ve.tensor_scalar(rs_tmp[0:N, 4], rs_tmp[0:N, 3], L2_EPS, None, ALU.add), 3)
                tick(ve.reciprocal(rs_tmp[0:N, 2], rs_tmp[0:N, 4]), 4)
                tick(ve.tensor_tensor(rs_tmp[0:N, 3], rs_tmp[0:N, 2], rs[0:N], ALU.mult), 5)
                normalize(i, 4, "s_xs", xs[:, r], rs_tmp[:, 3])

            def soft_weights(i):
                log = PS[0:N, 2, 0:4 * NP].rearrange("t (p n) -> t p n", p=4)
                ve.wait_ge(sem("s_log_ps"), i + 1)
                ve.tensor_reduce(c_st[:, 0], log, AX_X, ALU.max).then_inc(sem("s_soft"), 1)
                ve.wait_ge(sem("s_soft"), i * 4 + 1)
                ve.tensor_tensor(cmb[:], log, c_st[:, 0].unsqueeze(2).to_broadcast([N, 4, NP]), ALU.subtract
                                 ).then_inc(sem("s_csub"), 1)
                ve.wait_ge(sem("s_logT_ps"), i + 1)
                ve.tensor_reduce(d_st[:, 0:1], PS[:, 3, 0:N], AX_X, ALU.max, negate=True).then_inc(sem("s_dmax"), 1)
                ve.wait_ge(sem("s_dexp"), i + 1)
                ve.reciprocal(d_st[:, 2:3], d_st[:, 1:2]).then_inc(sem("s_soft"), 1)
                ve.wait_ge(sem("s_soft"), i * 4 + 2)
                ve.tensor_scalar(dspT[:], dspT[:], d_st[:, 2:3], None, ALU.mult).then_inc(sem("s_dspT"), 1)
                ve.wait_ge(sem("s_cexp"), i + 1)
                ve.tensor_reduce(c_st[:, 1], cmb[:], AX_X, ALU.add).then_inc(sem("s_soft"), 1)
                ve.wait_ge(sem("s_soft"), i * 4 + 3)
                ve.reciprocal(c_st[:, 2], c_st[:, 1]).then_inc(sem("s_soft"), 1)
                ve.wait_ge(sem("s_soft"), i * 4 + 4)
                ve.tensor_tensor(cmb[:], cmb[:], c_st[:, 2].unsqueeze(2).to_broadcast([N, 4, NP]), ALU.mult
                                 ).then_inc(sem("s_cmb"), 1)

            soft_rows(0, 0)
            with ve.Fori(0, 2) as i:
                for r in range(2):
                    j = i * 2 + r
                    ve.wait_ge(sem("s_xt_ps"), j + 1)
                    soft_rows(j + 1, 1 - r)
                    soft_weights(j)
            upm = const("upmask", HD)
            for mh in range(2):
                ve.wait_ge(sem("s_gelu"), mh + 1)
                m = upm[:, mh * NS:(mh + 1) * NS].unsqueeze(2).to_broadcast([HD, NS, PS_]).unsqueeze(1)
                hv = hidS[:, mh].rearrange("k (b n s) -> k b n s", b=B, n=NS)
                for n in range(NS):
                    hn = hv[:, :, n]
                    ins = ve.tensor_scalar(hn, hn, upm[:, mh * NS + n:mh * NS + n + 1], None, ALU.mult)
                ins.then_inc(sem("s_hidm"), 1)
            for j in range(4):
                ve.wait_ge(sem("s_yt_ps"), j + 1)
                ve.tensor_tensor(y_t[:, j], PS[:, 2 + j % 2, 0:D], b_up[:], ALU.add).then_inc(sem("s_yt"), 1)
            for b in range(B):
                ve.wait_ge(sem("s_y_ps"), b + 1)
                ve.tensor_tensor(h[:, b], h[:, b], PS[0:N, 4 + b % 4, 0:D], ALU.add).then_inc(sem("y_added"), 1)


def constants():
    import numpy as np
    c = {}
    c["ident"] = np.eye(128)
    c["ones"] = np.ones((128, 128))
    c["tri"] = np.triu(np.ones((N, N)))
    r = np.arange(128)
    c["l1mask"] = (r[:HD, None] // 16 == r[None, :HD] // 16)
    c["iota"] = np.tile(np.arange(CAP), (128, 1))
    c["vmask"] = (r[:GRP * SEG, None] // SEG == r[None, :32] // HDIM0)
    c["upmask"] = np.concatenate([(r[:HD, None] // HS + mh * 4 == r[None, :NS]) for mh in range(2)], axis=1)
    c["rev"] = np.tile(E - np.arange(E), (128, 1))
    i = np.arange(PATCH)
    inner = (i > 0).astype(int) + (i < PATCH - 1)
    m = np.zeros((KT, 128))
    m[:KT_IN] = np.tile((1 + inner[:, None] + inner[None, :]).reshape(-1), C).reshape(KT_IN, 128)
    m[KT_IN] = 1
    m[KT_IN + 1, :HALO2] = 1
    c["mult"] = m.T
    c["headmask"] = ((r[:C1, None] % 32) // HDIM0 == r[None, :GRP])
    out = np.zeros((128, CONST_W), np.float32)
    for name, (a, w) in CONST_AT.items():
        out[:c[name].shape[0], a:a + w] = c[name]
    return out


def halo(t):
    import numpy as np
    return np.concatenate([t[..., 1:-1, 0], t[..., 1:-1, -1], t[..., 0, 1:-1], t[..., -1, 1:-1]], axis=-1)


def kernel(**inputs):
    import numpy as np
    import concourse.bacc as bacc
    from concourse.bass_utils import run_bass_kernel_spmd

    v = {k: np.ascontiguousarray(a) for k, a in inputs.items()}
    P = PATCH
    xp = np.zeros((B, C, IMG + 2, IMG + 2), np.float32)
    xp[:, :, 1:-1, 1:-1] = v["x"]
    win = np.stack([np.stack([xp[:, :, P * a:P * a + P + 2, P * b:P * b + P + 2] for b in range(SIDE)], 2)
                    for a in range(SIDE)], 2)
    inner = win[..., 1:-1, 1:-1].reshape(B, C, IMG_TOK, P * P).transpose(1, 3, 0, 2).reshape(K_IN, B * IMG_TOK)
    outer = halo(win).reshape(B, C, IMG_TOK, 4 * P).transpose(1, 3, 0, 2).reshape(K_HALO, B * IMG_TOK)
    allk = np.concatenate([inner, outer], 0)
    xin = allk[:(KT - 1) * 128].reshape(KT - 1, 128, PAIRS, 128).transpose(2, 1, 0, 3)
    xhalo = allk[(KT - 1) * 128:].reshape(HALO2, PAIRS, 128).transpose(1, 0, 2)

    def fold(t):
        t = t.reshape(-1, P, P, 5, C).transpose(3, 4, 1, 2, 0)
        win = np.zeros((5, C, P + 2, P + 2, t.shape[-1]), np.float32)
        for s, (dy, dx) in enumerate([(0, 0), (0, -1), (0, 1), (-1, 0), (1, 0)]):
            win[s, :, 1 + dy:1 + dy + P, 1 + dx:1 + dx + P] = t[s]
        inn = win[:, :, 1:-1, 1:-1].reshape(5, KT_IN, 128, -1).transpose(2, 1, 0, 3).reshape(128, 5 * KT_IN, -1)
        ring = [win[1][:, 1:-1, 0], win[2][:, 1:-1, -1], win[3][:, 0, 1:-1], win[4][:, -1, 1:-1]]
        ring = np.stack(ring, 1).reshape(K_HALO, -1)
        return np.concatenate([inn, ring[:128, None]], 1), ring[128:]

    wtok, wtok2 = fold(v["L0_tok_proj_weight"])

    def columns(t):
        a, b = fold(t[None])
        out = np.zeros((128, W_TILES + 1), np.float32)
        out[:, :W_TILES] = a[..., 0]
        out[:HALO2, W_TILES] = b[:, 0]
        return out

    def halves(w):
        return w.reshape(2, HD, -1).transpose(1, 0, 2)

    wqkv1 = v["L1_attn_w_qkv"].T
    arrays = {
        "xin": xin, "xhalo": xhalo, "txt": v["txt"], "wtok": wtok, "wtok2": wtok2,
        "lnw": columns(v["L0_tok_ln_weight"]), "lnb": columns(v["L0_tok_ln_bias"]), "tokbias": v["L0_tok_proj_bias"],
        "consts": constants(),
        "wred": halves(v["L0_attn_W_reduce"]), "bred": v["L0_attn_b_reduce"][:, None], "wqkv0": v["L0_attn_W_qkv"],
        "bqkv0": v["L0_attn_b_qkv"].reshape(3, C1).T, "wproj0": v["L0_attn_W_proj"], "bproj0": v["L0_attn_b_proj"],
        "wrouter": halves(v["L0_ffn_w_router"]),
        "wi": v["L0_ffn_wi"].reshape(E, 2, HD, F).transpose(0, 2, 1, 3),
        "wo": v["L0_ffn_wo"].reshape(E, FT, 128, D).transpose(0, 2, 1, 3),
        "wq1": halves(wqkv1[:, :D]), "wkv1": halves(wqkv1[:, D:]), "wproj1": halves(v["L1_attn_w_proj"].T),
        "bproj1": v["L1_attn_b_proj"],
        "slots": halves(v["L1_ffn_slot_params"].reshape(D, NP)), "lscale": v["L1_ffn_scale"].reshape(1),
        "wdown": halves(v["L1_ffn_W_down"].transpose(1, 0, 2).reshape(D, NS * HS)),
        "bdown": v["L1_ffn_b_down"].reshape(2, HD).T,
        "wup": halves(v["L1_ffn_W_up"].reshape(NS * HS, D)),
        "bup": np.tile(np.repeat(v["L1_ffn_b_up"], PS_, axis=0), (4, 1)),
    }
    nc = bacc.Bacc("TRN2", target_bir_lowering=False, num_devices=1)
    feeds, args = {}, {}
    for name, a in arrays.items():
        a = np.ascontiguousarray(a)
        feeds[f"in_{name}"] = a
        args[name] = nc.dram_tensor(f"in_{name}", a.shape, F32, kind="ExternalInput").ap()
    args["out"] = nc.dram_tensor("out_0", (B, N, D), F32, kind="ExternalOutput").ap()
    build(nc, **args)
    r = run_bass_kernel_spmd(nc, [feeds], core_ids=[0])
    return r.results[0]["out_0"]
```

```python
from contextlib import ExitStack

import concourse.bass as bass
from concourse import mybir

ALU = mybir.AluOpType
ACT = mybir.ActivationFunctionType
F32 = mybir.dt.float32
AX_X = mybir.AxisListType.X

B, C, IMG, PATCH = 16, 3, 128, 16
SIDE = IMG // PATCH
IMG_TOK = SIDE * SIDE
TXT_TOK = 32
N = IMG_TOK + TXT_TOK
D = 192
HD = D // 2
PAIRS = B // 2
PATCH_DIM = PATCH * PATCH * 5 * C
K_IN = C * PATCH * PATCH
K_HALO = C * 4 * PATCH
KT_IN = K_IN // 128
KT = KT_IN + 2
HALO2 = K_HALO - 128
W_TILES = 5 * KT_IN + 1

C1, HEADS0, HDIM0, SEGS = 96, 12, 8, 4
SEG = N // SEGS
GRP = 4
NGRP = HEADS0 // GRP
PADSEG = 32
SCALE0 = float(HDIM0) ** -0.5

E, F = 8, 768
S = 2 * N
CAP = int(2 * 1.25 * S / E)
PADCAP = 64
FT = F // 128
SLOTS = PAIRS * CAP

NS, PS_, HS = 8, 4, 24
NP = NS * PS_

LN_EPS = 1e-5
L1_EPS = 1e-12
L2_EPS = 1e-6
TINY = 1e-18

CONSTS = [("ident", 128), ("ones", 128), ("tri", 96), ("l1mask", 96), ("iota", CAP), ("vmask", 32),
          ("upmask", 2 * NS), ("rev", E), ("mult", KT), ("headmask", GRP)]
CONST_AT, _at = {}, 0
for _n, _w in CONSTS:
    CONST_AT[_n] = (_at, _w)
    _at += _w
CONST_W = _at


def build(nc, xin, xhalo, txt, wtok, wtok2, lnw, lnb, tokbias, consts, wred, bred, wqkv0, bqkv0, wproj0, bproj0,
          wrouter, wi, wo, wq1, wkv1, wproj1, bproj1, slots, lscale, wdown, bdown, wup, bup, out):
    with ExitStack() as ctx:
        def sb(name, shape, dt=F32):
            return ctx.enter_context(nc.sbuf_tensor("sb_" + name, shape, dt))

        sems = {}

        def sem(name):
            if name not in sems:
                sems[name] = ctx.enter_context(nc.semaphore(name))
            return sems[name]

        PS = ctx.enter_context(nc.psum_tensor("banks", [128, 8, 512], F32))

        cst = sb("cst", [128, CONST_W])

        def const(name, rows=128):
            a, w = CONST_AT[name]
            return cst[0:rows, a:a + w]

        h_all = sb("h", [N, B + 8, D])
        h = h_all[:, 4:4 + B]
        shared = sb("w_tok_e_out", [128, PAIRS * E // 2, D])
        w_tok = shared[:, 0:W_TILES]
        w_tok2 = sb("w_tok2", [HALO2, D])
        ln_w = sb("ln_w", [128, W_TILES + 1])
        ln_b = sb("ln_b", [128, W_TILES + 1])
        shared2 = sb("tok_xeT", [128, 2 * E * PAIRS * CAP])
        nx = 2 * KT * 128
        x_k = shared2[:, 0:nx].rearrange("k (q t n) -> k q t n", q=2, t=KT)
        x_sq = shared2[:, nx:2 * nx].rearrange("k (q t n) -> k q t n", q=2, t=KT)
        w_eff = shared2[:, 2 * nx:2 * nx + KT * (D + 1)].rearrange("k (t n) -> k t n", t=KT)
        tok_bias = sb("tok_bias", [128, D])
        bias_row = sb("bias_row", [128, D])
        col_sum = sb("col_sum", [128, D])
        tok_stat = sb("tok_stat", [128, 16])
        tok_mid = sb("tok_mid", [128, D])
        eps_col = sb("eps_col", [128, 2])
        w_red = sb("w_red", [HD, 2, C1])
        b_red = sb("b_red", [C1, 1])
        w_qkv0 = sb("w_qkv0", [C1, 3 * C1])
        b_qkv0 = sb("b_qkv0", [C1, 3])
        w_proj0 = sb("w_proj0", [C1, D])
        b_proj0 = sb("b_proj0", [N, D])
        stat6 = sb("stat6", [N, 4, 6])
        mv = sb("mv", [N, 4, 2])
        rs_tmp = sb("rs_tmp", [128, 8, 4])
        rs = sb("rs", [128, 4])
        xn = sb("xn", [N, 4, D])
        xnr = sb("xnr", [N, 4, D])
        xnT = sb("xnT", [HD, 2, 2, 2 * N])
        xrT = sb("xrT", [C1, 2, 2 * N])
        xr_rep = sb("xr_rep", [C1, 2, 2 * SEGS, GRP, SEG])
        qT = sb("qT", [C1, 2, 2, SEGS, PADSEG])
        k_exp = sb("k_exp", [C1, 2, GRP, 2 * N])
        smax = sb("smax", [128, 2, NGRP, 2 * GRP])
        ssum = sb("ssum", [128, 2, NGRP, 2 * GRP])
        oT = sb("oT", [C1, 2, 2 * N])
        shared4 = sb("hidT_attn", [128, 2 * FT * SLOTS])
        v_exp = shared4[0:GRP * SEG, 0:1536].rearrange("k (q p s c) -> k q p s c", q=2, p=2, s=SEGS)
        prob = shared4[:, 1536:1536 + 1152].rearrange("t (q g p k) -> t q g p k", q=2, g=NGRP, p=2)
        probT = shared4[0:GRP * SEG, 2688:2688 + 1536].rearrange("k (q p g t) -> k q p g t", q=2, p=2, g=NGRP)
        w_router = sb("w_router", [HD, 2, E])
        xn2_all = sb("xn2", [N, B + 4, D])
        xn2 = xn2_all[:, 4:]
        logits_all = sb("logits", [N, B + 4, E])
        logits = logits_all[:, 4:]
        r_top = sb("r_top", [N, 6, B])
        r_e = sb("r_e", [N, 6, B, E])
        slot_of = sb("slot_of", [N, B, E])
        gate_of = sb("gate_of", [N, B, E])
        shared3 = sb("dispatch_comb_slots", [N, 4 * E * CAP + 4 * D])
        onehot = shared3[:, 0:4 * E * CAP].rearrange("t (q p s) -> t q p s", q=2, p=2)
        x_disp = shared3[:, 4 * E * CAP:].rearrange("t (q p d) -> t q p d", q=2, p=2)
        comb = shared3[:, 0:4 * E * PADCAP].rearrange("t (q p e c) -> t q p e c", q=2, p=2, e=E)
        xeT = shared2[0:HD].rearrange("k (a e g c) -> k a e g c", a=2, e=E, g=PAIRS)
        wi_sl = sb("wi_sl", [HD, 2, 2, F])
        wo_sl = sb("wo_sl", [128, 2, FT, D])
        hidT = shared4[:].rearrange("f (q t s) -> f q t s", q=2, t=FT)
        e_out = shared[:].rearrange("s (g e) d -> s g e d", g=PAIRS)
        combT = sb("combT", [128, 2, 2, E // 2, N])
        w_q1 = sb("w_q1", [HD, 2, D])
        w_kv1 = sb("w_kv1", [HD, 2, 2 * D])
        w_proj1 = sb("w_proj1", [HD, 2, D])
        b_proj1 = sb("b_proj1", [N, D])
        q1T = shared4[0:HD, 0:768].rearrange("k (q a t) -> k q a t", q=2, a=2)
        kv1 = shared4[0:N, 768:768 + 1536].rearrange("t (q p n) -> t q p n", q=2, p=2)
        abs_k = shared4[0:N, 2304:2304 + 768].rearrange("t (q p n) -> t q p n", q=2, p=2)
        kv_bd = shared4[0:HD, 3072:3072 + 768].rearrange("k (q p a n) -> k q p a n", q=2, p=2, a=2)
        o1T = shared4[0:HD, 3840:3840 + 768].rearrange("k (q p a t) -> k q p a t", q=2, p=2, a=2)
        den = sb("den", [HD, 2, 6, 4])
        slot_raw = sb("slot_raw", [HD, 2, NP])
        slot_sq = sb("slot_sq", [HD, 2, NP])
        slot_n = sb("slot_n", [HD, 2, NP])
        slot_s = sb("slot_s", [HD, 6, 2 * PS_])
        l_scale = sb("l_scale", [HD, 1])
        w_down = sb("w_down", [HD, 2, D])
        b_down = sb("b_down", [HD, 2])
        w_up = sb("w_up", [HD, 2, D])
        b_up = sb("b_up", [128, D])
        xs = shared2[0:N, 4 * D:20 * D].rearrange("t (r p d) -> t r p d", r=4, p=4)
        xsT = shared2[0:HD, 20 * D:20 * D + 8 * N].rearrange("k (a t) -> k a t", a=2)
        soft_st = sb("soft_rows_stat", [N, 12, 4])
        cmb = sb("cmb", [N, 2, 4, NP])
        c_st = sb("c_st", [N, 3, 4])
        cmbT = sb("cmbT", [128, 4, N])
        dspT = sb("dspT", [128, 2, N])
        d_st = sb("d_st", [128, 3])
        dsp = sb("dsp", [N, 4 * NP])
        x_tT = shared3[:, 0:2 * B * NP].rearrange("k (a s) -> k a s", a=2)
        hidS = shared4[0:HD, 4608:4608 + 2 * B * NP].rearrange("k (a s) -> k a s", a=2)
        y_t = shared2[:, 0:4 * D].rearrange("s (j d) -> s j d", j=4)

        W_CHUNKS = (0, 5, 15, 25, W_TILES)
        Y_BANK = (4, 5, 6, 0)
        DONE = ((0, 3), (3, 4))

        ident = const("ident")
        ones = const("ones")

        def stand(eng):
            eng.sem_inc(sem("carried_" + ("ve" if eng is nc.vector else "pe")), 1)

        def flip(dst, src):
            rows = src.shape[0]
            return nc.tensor.transpose(dst, src, ident[0:rows, 0:rows])

        block = ctx.enter_context(nc.Block())

        @block.sync
        def _(sp):
            sp.dma_start(ln_w[:], lnw).then_inc(sem("lnwb_in"), 16)
            sp.dma_start(ln_b[:], lnb).then_inc(sem("lnwb_in"), 16)
            for c, (a, b) in enumerate(zip(W_CHUNKS, W_CHUNKS[1:])):
                sp.dma_start(w_tok[:, a:b], wtok[:, a:b]).then_inc(sem(f"wtok_in{c}"), 16)
            sp.dma_start(w_tok2[:], wtok2).then_inc(sem("wtok2_in"), 16)
            sp.dma_start(cst[:], consts).then_inc(sem("cst_in"), 16)
            sp.dma_start(tok_bias[:], tokbias.partition_broadcast(128)).then_inc(sem("tokbias_in"), 16)
            sp.dma_start(h[IMG_TOK:N], txt.rearrange("b t d -> t b d")).then_inc(sem("txt_in"), 16)
            for q in range(2):
                sp.dma_start(x_k[:, q, 0:KT - 1], xin[q]).then_inc(sem(f"x_in{q}"), 16)
                sp.dma_start(x_k[0:HALO2, q, KT - 1], xhalo[q]).then_inc(sem(f"x_in{q}"), 16)
            for dst, src in [(w_red[:], wred), (b_red[:], bred), (w_qkv0[:], wqkv0), (b_qkv0[:], bqkv0),
                             (w_proj0[:], wproj0), (b_proj0[:], bproj0.partition_broadcast(N)),
                             (w_router[:], wrouter)]:
                sp.dma_start(dst, src).then_inc(sem("attn0_in"), 16)
            with sp.Fori(1, PAIRS // 2) as i:
                for q in range(2):
                    sp.wait_ge(sem("tok_ps"), i * 2 + (q - 1))
                    sp.dma_start(x_k[:, q, 0:KT - 1], xin[bass.ds(i * 2 + q, 1)]).then_inc(sem(f"x_in{q}"), 16)
                    sp.dma_start(x_k[0:HALO2, q, KT - 1], xhalo[bass.ds(i * 2 + q, 1)]).then_inc(sem(f"x_in{q}"), 16)
            for dst, src in [(w_q1[:], wq1), (w_kv1[:], wkv1), (w_proj1[:], wproj1),
                             (b_proj1[:], bproj1.partition_broadcast(N)), (slot_raw[:], slots),
                             (l_scale[:], lscale.partition_broadcast(HD)), (w_down[:], wdown), (b_down[:], bdown),
                             (w_up[:], wup), (b_up[:], bup)]:
                sp.dma_start(dst, src).then_inc(sem("layer1_in"), 16)
            with sp.Fori(0, E // 2) as i:
                for q in range(2):
                    sp.wait_ge(sem("eo_ps"), i * 4 + 2 * q + 2)
                    sp.dma_start(wi_sl[:, q], wi[bass.ds(i * 2 + q, 1)]).then_inc(sem(f"wexp_in{q}"), 16)
                    sp.dma_start(wo_sl[:, q], wo[bass.ds(i * 2 + q, 1)]).then_inc(sem(f"wexp_in{q}"), 16)
            out_v = out.rearrange("b t d -> t b d")
            for b in range(0, B, 4):
                sp.wait_ge(sem("y_added"), b + 4)
                sp.dma_start(out_v[:, b:b + 4], h[:, b:b + 4]).then_inc(sem("stored"), 16)
            sp.wait_ge(sem("stored"), 16 * (B // 4))

        @block.gpsimd
        def _(gp):
            gp.wait_ge(sem("cst_in"), 16)
            gp.tensor_copy(w_eff[:, :, D], const("mult")).then_inc(sem("mult_ready"), 1)
            gp.memset(qT[:], 0.0).then_inc(sem("pads_zero"), 1)
            gp.memset(h_all[:, 0:4], 0.0).then_inc(sem("pads_zero"), 1)
            gp.memset(h_all[:, B + 4:B + 8], 0.0).then_inc(sem("pads_zero"), 1)
            gp.wait_ge(sem("w_eff"), KT)
            gp.wait_ge(sem("bias_row_ps"), 1)
            gp.memset(shared[:], 0.0).then_inc(sem("pads_zero"), 1)
            gp.wait_ge(sem("attn0_in"), 16 * 7)
            def keep_normalized(i):
                gp.wait_ge(sem("r_xn"), i * 4 + 4)
                gp.tensor_copy(xn2_all[:, bass.ds(i * 4, 4), :], xnr[:]).then_inc(sem("r_kept"), 1)

            with gp.Fori(0, B // 4) as i:
                gp.wait_ge(sem("a_xn"), i * 4 + 4)
                for p in range(4):
                    hp = h_all[:, bass.ds(i * 4 + (4 + p), 1), :]
                    gp.tensor_tensor(hp, hp, b_proj0[:].unsqueeze(1), ALU.add).then_inc(sem("h_biased"), 1)
                keep_normalized(i)
            keep_normalized(B // 4)
            with gp.Fori(0, PAIRS // 2) as i:
                for q in range(2):
                    gp.wait_ge(sem("disp_ps"), i * 4 + 2 * q + 2)
                    if q == 0:
                        gp.wait_ge(sem("r_kept"), B // 4 + 1)
                    gp.tensor_copy(x_disp[:, q], xn2[:, bass.ds(i * 4 + 2 * q, 2), :]).then_inc(sem("xdisp"), 1)
            gp.wait_ge(sem("layer1_in"), 16 * 10)
            gp.wait_ge(sem("xeT"), 2 * PAIRS + 4)
            gp.memset(shared3[:], 0.0).then_inc(sem("pads_zero"), 1)
            with gp.Fori(0, B // 4) as i:
                gp.wait_ge(sem("b_xn"), i * 4 + 4)
                for p in range(4):
                    hp = h[:, bass.ds(i * 4 + p, 1), :]
                    gp.tensor_tensor(hp, hp, b_proj1[:].unsqueeze(1), ALU.add).then_inc(sem("h_biased"), 1)

        @block.tensor
        def _(pe):
            pe.sem_inc(sem("disp_ps"), 4)
            pe.sem_inc(sem("eo_ps"), 4)
            pe.sem_inc(sem("b_h"), 2)
            pe.wait_ge(sem("lnwb_in"), 32)
            for t in range(W_TILES):
                if t in W_CHUNKS:
                    pe.wait_ge(sem(f"wtok_in{W_CHUNKS.index(t)}"), 16)
                nc.tensor.matmul(PS[:, 0, 0:D], ln_b[:, t:t + 1].to_broadcast([128, 128]), w_tok[:, t],
                                 start=(t == 0), stop=False)
            pe.wait_ge(sem("wtok2_in"), 16)
            nc.tensor.matmul(PS[:, 0, 0:D], ln_b[0:HALO2, W_TILES:W_TILES + 1].to_broadcast([HALO2, 128]), w_tok2[:],
                             start=False, stop=True).then_inc(sem("bias_row_ps"), 1)
            pe.wait_ge(sem("cst_in"), 16)
            pe.wait_ge(sem("w_eff"), KT)
            for t in range(KT):
                rows = 128 if t < KT - 1 else HALO2
                mm = nc.tensor.matmul(PS[:, 1, 0:D], ones[0:rows], w_eff[0:rows, t, 0:D], start=(t == 0), stop=(t == KT - 1))
            mm.then_inc(sem("col_sum_ps"), 1)
            pe.wait_ge(sem("mult_ready"), 1)
            with pe.Fori(0, PAIRS // 2) as i:
                for q in range(2):
                    pe.wait_ge(sem(f"x_in{q}"), i * 32 + 32)
                    pe.wait_ge(sem("tok_mid"), i * 2 + q + 1)
                    for t in range(KT):
                        rows = 128 if t < KT - 1 else HALO2
                        nc.tensor.matmul(PS[:, 2 + q, 0:D + 1], x_k[0:rows, q, t], w_eff[0:rows, t],
                                         start=(t == 0), stop=(t == KT - 1))
                    pe.wait_ge(sem("x_sq"), i * 2 + q + 1)
                    for t in range(KT):
                        rows = 128 if t < KT - 1 else HALO2
                        mm = nc.tensor.matmul(PS[:, 2 + q, 200:201], x_sq[0:rows, q, t], const("mult")[0:rows, t:t + 1],
                                              start=(t == 0), stop=(t == KT - 1))
                    mm.then_inc(sem("tok_ps"), 1)

            pe.wait_ge(sem("attn0_in"), 16 * 7)
            pe.wait_ge(sem("pads_zero"), 4)
            def route_products(i):
                for q in range(2):
                    pe.wait_ge(sem("r_xn"), i * 4 + 2 * q + 2)
                    if not isinstance(i, int):
                        pe.wait_ge(sem("a_vexp"), i * 4 + 2 * q + 2)
                    for p in range(2):
                        for kh in range(2):
                            mm = flip(PS[0:HD, 4 * q + 3, (kh * 2 + p) * N:(kh * 2 + p + 1) * N],
                                      xnr[:, 2 * q + p, kh * HD:(kh + 1) * HD])
                    mm.then_inc(sem("r_xnT_ps"), 1)
                for q in range(2):
                    pe.wait_ge(sem("r_xnT"), i * 2 + q + 1)
                    for p in range(2):
                        for kh in range(2):
                            mm = nc.tensor.matmul(PS[0:N, 4 * q + 3, 4 * N + p * E:4 * N + (p + 1) * E],
                                                  xnT[:, q, kh, p * N:(p + 1) * N], w_router[:, kh],
                                                  start=(kh == 0), stop=(kh == 1))
                    mm.then_inc(sem("r_logit_ps"), 1)

            with pe.Fori(0, B // 4) as i:
                for q in range(2):
                    pe.wait_ge(sem("a_xn"), i * 4 + 2 * q + 2)
                    for p in range(2):
                        for kh in range(2):
                            mm = flip(PS[0:HD, 4 * q, (kh * 2 + p) * N:(kh * 2 + p + 1) * N],
                                      xn[:, 2 * q + p, kh * HD:(kh + 1) * HD])
                    mm.then_inc(sem("a_xnT_ps"), 1)
                for q in range(2):
                    pe.wait_ge(sem("a_xnT"), i * 2 + q + 1)
                    for kh in range(2):
                        mm = nc.tensor.matmul(PS[0:C1, 4 * q + 1, 0:2 * N], w_red[:, kh], xnT[:, q, kh],
                                              start=(kh == 0), stop=(kh == 1))
                    mm.then_inc(sem("a_xr_ps"), 1)
                for q in range(2):
                    pe.wait_ge(sem("a_xrT"), i * 4 + q + 1)
                    for j in range(2):
                        mm = nc.tensor.matmul(PS[0:C1, 4 * q, j * 2 * N:(j + 1) * 2 * N], w_qkv0[:, j * C1:(j + 1) * C1],
                                              xrT[:, q], start=True, stop=True)
                    mm.then_inc(sem("a_qk_ps"), 1)
                pe.wait_ge(sem("r_mv"), i * 4 + 4)
                for q in range(2):
                    pe.wait_ge(sem("a_xrT"), i * 4 + q + 3)
                    for p in range(2):
                        for s in range(SEGS):
                            mm = nc.tensor.matmul(PS[0:GRP * SEG, 4 * q + 2 + p, s * C1:(s + 1) * C1],
                                                  xr_rep[:, q, p * SEGS + s].rearrange("c r t -> c (r t)"),
                                                  w_qkv0[:, 2 * C1:3 * C1], start=True, stop=True)
                        mm.then_inc(sem("a_v_ps"), 1)
                for q in range(2):
                    pe.wait_ge(sem("a_qT"), i * 2 + q + 1)
                    pe.wait_ge(sem("a_kexp"), i * 2 + q + 1)
                    stand(pe)
                    for g in range(NGRP):
                        if g == 2:
                            pe.wait_ge(sem("a_vexp"), i * 4 + 2 * q + 1)
                            stand(pe)
                        rows = slice(g * 32, g * 32 + 32)
                        for p in range(2):
                            for s in range(SEGS):
                                mm = nc.tensor.matmul(
                                    PS[s * 32:s * 32 + 32, 4 * q + g, p * GRP * SEG:(p + 1) * GRP * SEG],
                                    qT[rows, q, p, s], k_exp[rows, q, :, p * N + s * SEG:p * N + (s + 1) * SEG],
                                    start=True, stop=True)
                    mm.then_inc(sem("a_s_ps"), 1)
                route_products(i)
                for q in range(2):
                    pe.wait_ge(sem("a_prob"), i * 2 + q + 1)
                    pe.wait_ge(sem("r_logit"), i * 2 + q + 1)
                    pe.wait_ge(sem("a_vexp"), i * 4 + 2 * q + 2)
                    for p in range(2):
                        for g in range(NGRP):
                            mm = flip(PS[0:GRP * SEG, 4 * q + (0 if p else 3), g * 128:(g + 1) * 128], prob[:, q, g, p])
                        mm.then_inc(sem("a_probT_ps"), 1)
                for q in range(2):
                    for p in range(2):
                        pe.wait_ge(sem("a_probT"), i * 4 + 2 * q + p + 1)
                        for s in range(SEGS):
                            for g in range(NGRP):
                                mm = nc.tensor.matmul(
                                    PS[g * 32:g * 32 + 32, 4 * q + 1, p * N + s * SEG:p * N + (s + 1) * SEG],
                                    v_exp[:, q, p, s, g * 32:g * 32 + 32], probT[:, q, p, g, s * PADSEG:s * PADSEG + SEG],
                                    start=True, stop=True)
                    mm.then_inc(sem("a_oT_ps"), 1)
                for q in range(2):
                    pe.wait_ge(sem("a_oT"), i * 2 + q + 1)
                    for p in range(2):
                        mm = nc.tensor.matmul(PS[0:N, 4 * q + 2, p * D:(p + 1) * D], oT[:, q, p * N:(p + 1) * N], w_proj0[:],
                                              start=True, stop=True)
                    mm.then_inc(sem("a_proj_ps"), 1)
            route_products(B // 4)

            pe.wait_ge(sem("r_first"), 1)
            tri, one96 = const("tri", N), ones[0:N, 0:N]
            first, second = r_e[:, 2].rearrange("t (g p) e -> t p g e", p=2), r_e[:, 4].rearrange("t (g p) e -> t p g e", p=2)
            for k, p, terms in [(0, 0, [(tri, first[:, 0])]),
                                (0, 1, [(one96, first[:, 0]), (tri, first[:, 1])]),
                                (1, 0, [(one96, first[:, 0]), (one96, first[:, 1]), (tri, second[:, 0])]),
                                (1, 1, [(one96, first[:, 0]), (one96, first[:, 1]), (one96, second[:, 0]),
                                        (tri, second[:, 1])])]:
                dst = PS[0:N, 3, (k * 2 + p) * PAIRS * E:(k * 2 + p + 1) * PAIRS * E]
                for j, (lhs, rhs) in enumerate(terms):
                    if (k, p, j) == (1, 0, 2):
                        pe.wait_ge(sem("r_choice"), 2)
                    mm = nc.tensor.matmul(dst, lhs, rhs, start=(j == 0), stop=(j == len(terms) - 1))
            mm.then_inc(sem("r_count_ps"), 1)

            with pe.Fori(0, PAIRS // 2) as i:
                for q in range(2):
                    pe.wait_ge(sem("xdisp"), i * 2 + q + 1)
                    pe.wait_ge(sem("onehot"), i * 4 + 2 * q + 2)
                    pe.wait_ge(sem("xeT"), i * 4 + 2 * q + 2)
                    for dh in range(2):
                        for p in range(2):
                            mm = nc.tensor.matmul(PS[0:HD, 4 + 2 * q + dh, 0:E * CAP],
                                                  x_disp[:, q, p, dh * HD:(dh + 1) * HD], onehot[:, q, p],
                                                  start=(p == 0), stop=(p == 1))
                        mm.then_inc(sem("disp_ps"), 1)

            pe.wait_ge(sem("xeT"), 2 * PAIRS + 4)
            with pe.Fori(0, E // 2) as i:
                for q in range(2):
                    pe.wait_ge(sem(f"wexp_in{q}"), i * 32 + 32)
                    for f in range(FT):
                        pe.wait_ge(sem("hidT"), i * 2 * FT + q * FT + f + 1)
                        for kh in range(2):
                            mm = nc.tensor.matmul(PS[:, f % 2, 0:SLOTS], wi_sl[:, q, kh, f * 128:(f + 1) * 128],
                                                  xeT[:, kh, bass.ds(i * 2 + q, 1)].rearrange("k e g c -> k (e g c)"),
                                                  start=(kh == 0), stop=(kh == 1))
                        mm.then_inc(sem("hid_ps"), 1)
                    for half in range(2):
                        pe.wait_ge(sem("e_out"), i * 8 + 4 * q + 2 * half + 2)
                        for gp_ in range(2):
                            for f in range(FT):
                                if half == 0 and gp_ == 0:
                                    pe.wait_ge(sem("hidT"), i * 2 * FT + q * FT + f + 3)
                                for z in range(2):
                                    g = half * 4 + gp_ * 2 + z
                                    mm = nc.tensor.matmul(PS[64 * z:64 * z + CAP, 2 + half, gp_ * D:(gp_ + 1) * D],
                                                          hidT[:, q, f, g * CAP:(g + 1) * CAP], wo_sl[:, q, f],
                                                          start=(f == 0), stop=(f == FT - 1), skip_group_check=True)
                        mm.then_inc(sem("eo_ps"), 1)

            pe.wait_ge(sem("e_out"), 4 * E + 4)
            pe.wait_ge(sem("layer1_in"), 16 * 10)
            def turn_comb(i):
                for q in range(2):
                    for p in range(2):
                        pe.wait_ge(sem("comb"), i * 4 + 2 * q + p + 1)
                        for ep in range(E // 2):
                            mm = flip(PS[:, 4 * q + p, ep * N:(ep + 1) * N],
                                      comb[:, q, p, 2 * ep:2 * ep + 2].rearrange("t e c -> t (e c)"))
                        mm.then_inc(sem("combT_ps"), 1)

            def combine(i):
                for q in range(2):
                    for p in range(2):
                        pe.wait_ge(sem("combT"), i * 4 + 2 * q + p + 1)
                        for ep in range(E // 2):
                            mm = nc.tensor.matmul(PS[0:N, 4 * q + 2, p * D:(p + 1) * D], combT[:, q, p, ep],
                                                  e_out[:, bass.ds(i * 2 + q, 1), ep].rearrange("s g d -> s (g d)"),
                                                  start=(ep == 0), stop=(ep == E // 2 - 1))
                    mm.then_inc(sem("moe_ps"), 1)

            def linear_inputs(i):
                for q in range(2):
                    pe.wait_ge(sem("b_xn"), i * 4 + 2 * q + 2)
                    for p in range(2):
                        for kh in range(2):
                            mm = flip(PS[0:HD, 4 * q + 3, (kh * 2 + p) * N:(kh * 2 + p + 1) * N],
                                      xn[:, 2 * q + p, kh * HD:(kh + 1) * HD])
                    mm.then_inc(sem("b_xnT_ps"), 1)
                for q in range(2):
                    pe.wait_ge(sem("b_xnT"), i * 2 + q + 1)
                    pe.wait_ge(sem("b_h"), i * 2 + q + 1)
                    for p in range(2):
                        for kh in range(2):
                            mm = nc.tensor.matmul(PS[0:N, 4 * q + p, 0:2 * D], xnT[:, q, kh, p * N:(p + 1) * N],
                                                  w_kv1[:, kh], start=(kh == 0), stop=(kh == 1))
                        mm.then_inc(sem("b_kv_ps"), 1)
                    for mh in range(2):
                        for kh in range(2):
                            mm = nc.tensor.matmul(PS[0:HD, 4 * q + 2, mh * 2 * N:(mh + 1) * 2 * N],
                                                  w_q1[:, kh, mh * HD:(mh + 1) * HD], xnT[:, q, kh],
                                                  start=(kh == 0), stop=(kh == 1))
                    mm.then_inc(sem("b_q_ps"), 1)

            def keys_values(i):
                for q in range(2):
                    for p in range(2):
                        pe.wait_ge(sem("b_kv"), i * 4 + 2 * q + p + 1)
                        for mh in range(2):
                            mm = nc.tensor.matmul(PS[0:HD, 4 * q + 3, (p * 2 + mh) * HD:(p * 2 + mh + 1) * HD],
                                                  kv1[:, q, p, mh * HD:(mh + 1) * HD],
                                                  kv1[:, q, p, D + mh * HD:D + (mh + 1) * HD], start=True, stop=True)
                        pe.wait_ge(sem("b_absk"), i * 4 + 2 * q + p + 1)
                        for mh in range(2):
                            at = 4 * HD + p * 2 + mh
                            mm = nc.tensor.matmul(PS[0:HD, 4 * q + 3, at:at + 1], abs_k[:, q, p, mh * HD:(mh + 1) * HD],
                                                  ones[0:N, 0:1], start=True, stop=True)
                    mm.then_inc(sem("b_kvp_ps"), 1)

            def linear_outputs(i):
                for q in range(2):
                    pe.wait_ge(sem("b_kvbd"), i * 8 + 4 * q + 4)
                    pe.wait_ge(sem("b_q1T"), i * 2 + q + 1)
                    for p in range(2):
                        for mh in range(2):
                            mm = nc.tensor.matmul(PS[0:HD, 4 * q, (p * 2 + mh) * N:(p * 2 + mh + 1) * N],
                                                  kv_bd[:, q, p, mh], q1T[:, q, mh, p * N:(p + 1) * N],
                                                  start=True, stop=True)
                    mm.then_inc(sem("b_oT_ps"), 1)
                for q in range(2):
                    pe.wait_ge(sem("b_o1T"), i * 2 + q + 1)
                    for p in range(2):
                        for mh in range(2):
                            mm = nc.tensor.matmul(PS[0:N, 4 * q + 1, p * D:(p + 1) * D], o1T[:, q, p, mh], w_proj1[:, mh],
                                                  start=(mh == 0), stop=(mh == 1))
                    mm.then_inc(sem("b_proj_ps"), 1)

            LAST = B // 4 - 1
            turn_comb(0)
            combine(0)
            with pe.Fori(0, LAST) as i:
                linear_inputs(i)
                pe.wait_ge(sem("b_kv"), i * 4 + 4)
                pe.wait_ge(sem("b_absk"), i * 4 + 4)
                turn_comb(i + 1)
                keys_values(i)
                pe.wait_ge(sem("b_q1T"), i * 2 + 2)
                combine(i + 1)
                linear_outputs(i)
            linear_inputs(LAST)
            keys_values(LAST)
            linear_outputs(LAST)

            pe.wait_ge(sem("slot_n"), 2)

            def soft_logits(j):
                if j > 0:
                    pe.wait_ge(sem("s_xsT"), 2 * j)
                for p in range(4):
                    pe.wait_ge(sem("s_xs"), j * 4 + p + 1)
                    for kh in range(2):
                        mm = flip(PS[0:HD, 2 + kh, p * N:(p + 1) * N], xs[:, j, p, kh * HD:(kh + 1) * HD])
                mm.then_inc(sem("s_xsT_ps"), 1)
                pe.wait_ge(sem("s_xsT"), j * 2 + 2)
                if j > 0:
                    pe.wait_ge(sem("s_csub"), j)
                    pe.wait_ge(sem("s_dexp"), j)
                for p in range(4):
                    for kh in range(2):
                        mm = nc.tensor.matmul(PS[0:N, 0, p * NP:(p + 1) * NP], xsT[:, kh, p * N:(p + 1) * N], slot_n[:, kh],
                                              start=(kh == 0), stop=(kh == 1))
                mm.then_inc(sem("s_log_ps"), 1)
                for kh in range(2):
                    for p in range(4):
                        mm = nc.tensor.matmul(PS[p * NP:(p + 1) * NP, 4, 0:N], slot_n[:, kh], xsT[:, kh, p * N:(p + 1) * N],
                                              start=(kh == 0), stop=(kh == 1), skip_group_check=True)
                mm.then_inc(sem("s_logT_ps"), 1)

            def soft_inputs(j):
                pe.wait_ge(sem("s_dspT"), j + 1)
                if j > 0:
                    pe.wait_ge(sem("s_xtT"), j)
                flip(PS[0:N, 5, 0:128], dspT[:, j % 2]).then_inc(sem("s_dsp_ps"), 1)
                pe.wait_ge(sem("s_cmb"), j + 1)
                if j > 0:
                    pe.wait_ge(sem("s_cmbT"), j)
                flip(PS[:, 6, 0:N], cmb[:, j % 2].rearrange("t p n -> t (p n)")).then_inc(sem("s_cmbT_ps"), 1)
                pe.wait_ge(sem("s_dsp"), j + 1)
                for p in range(4):
                    for dh in range(2):
                        mm = nc.tensor.matmul(PS[0:HD, 5, (dh + 1) * 128 + p * NP:(dh + 1) * 128 + (p + 1) * NP],
                                              xs[:, j, p, dh * HD:(dh + 1) * HD], dsp[:, p * NP:(p + 1) * NP],
                                              start=True, stop=True)
                mm.then_inc(sem("s_xt_ps"), 1)

            def soft_hidden(j):
                pe.wait_ge(sem("s_xtT"), j + 1)
                for mh in range(2):
                    for kh in range(2):
                        mm = nc.tensor.matmul(PS[0:HD, (1, 7)[mh], j * 128:(j + 1) * 128], w_down[:, kh, mh * HD:(mh + 1) * HD],
                                              x_tT[:, kh, j * 128:(j + 1) * 128], start=(kh == 0), stop=(kh == 1))
                mm.then_inc(sem("s_hid_ps"), 1)

            def slot_outputs(j):
                if j >= 2:
                    pe.wait_ge(sem("s_yt"), j - 1)
                for mh in range(2):
                    mm = nc.tensor.matmul(PS[:, 2 + j % 2, 0:D], hidS[:, mh, j * 128:(j + 1) * 128], w_up[:, mh],
                                          start=(mh == 0), stop=(mh == 1))
                mm.then_inc(sem("s_yt_ps"), 1)

            def token_outputs(b):
                j, p = b // 4, b % 4
                pe.wait_ge(sem("s_yt"), j + 1)
                if b >= 4:
                    pe.wait_ge(sem("y_added"), b - 3)
                rows = slice(p * NP, (p + 1) * NP)
                nc.tensor.matmul(PS[0:N, Y_BANK[b % 4], 0:D], cmbT[rows, j], y_t[rows, j], start=True,
                                 stop=True).then_inc(sem("s_y_ps"), 1)

            soft_logits(0)
            for j in range(4):
                if j < 3:
                    soft_logits(j + 1)
                if j > 0:
                    soft_hidden(j - 1)
                soft_inputs(j)
            soft_hidden(3)
            pe.wait_ge(sem("s_hidm"), 2)
            for j in range(3):
                slot_outputs(j)
            for b in range(4):
                token_outputs(b)
            pe.wait_ge(sem("s_hidm"), 4)
            slot_outputs(3)
            for b in range(4, B):
                token_outputs(b)

        @block.scalar
        def _(act):
            def rsqrt_seed(var, tmp, dst, eps, done):
                nc.scalar.activation(tmp, var, ACT.Ln, bias=eps).then_inc(sem("act_ln"), 1)
                act.wait_ge(sem("act_ln"), done)
                return nc.scalar.activation(dst, tmp, ACT.Exp, scale=-0.5)

            act.sem_inc(sem("xeT"), 4)
            act.sem_inc(sem("hidT"), 2)
            eps = eps_col[:, 0:1]
            act.preload_act_table_set("natural_log_exp_and_others")
            act.wait_ge(sem("eps_ready"), 2)
            def square_and_seed(i, ahead):
                for q in range(2):
                    act.wait_ge(sem(f"x_in{q}"), i * 32 + 32)
                    nc.scalar.activation(x_sq[:, q, 0:KT - 1], x_k[:, q, 0:KT - 1], ACT.Square)
                    nc.scalar.activation(x_sq[0:HALO2, q, KT - 1], x_k[0:HALO2, q, KT - 1], ACT.Square).then_inc(sem("x_sq"), 1)
                    act.wait_ge(sem("tok_var"), i * 2 + q + 1)
                    rsqrt_seed(tok_stat[:, 3:4], tok_stat[:, 4:5], tok_stat[:, 5:6], eps,
                               i * 2 + (q + 1 + ahead)).then_inc(sem("tok_seed"), 1)

            with act.Fori(0, PAIRS // 2 - 1) as i:
                square_and_seed(i, 0)
            act.wait_ge(sem("a_mv"), 4)
            rsqrt_seed(mv[:, :, 1], rs_tmp[0:N, 0], rs_tmp[0:N, 1], eps[0:N], PAIRS - 1).then_inc(sem("a_seed"), 1)
            square_and_seed(PAIRS // 2 - 1, 1)
            LN0 = PAIRS
            act.wait_ge(sem("attn0_in"), 16 * 7)
            act.wait_ge(sem("pads_zero"), 4)
            def norm_seed(i):
                act.wait_ge(sem("a_mv"), i * 4 + 4)
                rsqrt_seed(mv[:, :, 1], rs_tmp[0:N, 0], rs_tmp[0:N, 1], eps[0:N],
                           i * 2 + LN0 + 1).then_inc(sem("a_seed"), 1)

            def route_seed(i):
                act.wait_ge(sem("r_mv"), i * 4 + 4)
                rsqrt_seed(mv[:, :, 1], rs_tmp[0:N, 0], rs_tmp[0:N, 1], eps[0:N],
                           i * 2 + LN0 + 2).then_inc(sem("r_seed"), 1)

            def route_drain(i):
                for q in range(2):
                    act.wait_ge(sem("r_xnT_ps"), i * 2 + q + 1)
                    nc.scalar.copy(xnT[:, q].rearrange("k a t -> k (a t)"), PS[0:HD, 4 * q + 3, 0:4 * N]
                                   ).then_inc(sem("r_xnT"), 1)
                for q in range(2):
                    act.wait_ge(sem("r_logit_ps"), i * 2 + q + 1)
                    nc.scalar.copy(logits_all[:, bass.ds(i * 4 + 2 * q, 2), :],
                                   PS[0:N, 4 * q + 3, 4 * N:4 * N + 2 * E].rearrange("t (p e) -> t p e", p=2)
                                   ).then_inc(sem("r_logit"), 1)

            with act.Fori(0, B // 4) as i:
                for q in range(2):
                    act.wait_ge(sem("a_xnT_ps"), i * 2 + q + 1)
                    nc.scalar.copy(xnT[:, q].rearrange("k a t -> k (a t)"), PS[0:HD, 4 * q, 0:4 * N]).then_inc(sem("a_xnT"), 1)
                for q in range(2):
                    act.wait_ge(sem("a_xr_ps"), i * 2 + q + 1)
                    nc.scalar.activation(xrT[:, q], PS[0:C1, 4 * q + 1, 0:2 * N], ACT.Identity, bias=b_red[:]
                                         ).then_inc(sem("a_xrT"), 1)
                for q in range(2):
                    nc.scalar.activation(xr_rep[:, q], PS[0:C1, 4 * q + 1, 0:2 * N].rearrange("c (a t) -> c a t", t=SEG)
                                         .unsqueeze(2).to_broadcast([C1, 2 * SEGS, GRP, SEG]), ACT.Identity, bias=b_red[:]
                                         ).then_inc(sem("a_xrT"), 1)
                route_seed(i)
                for q in range(2):
                    act.wait_ge(sem("a_kexp"), i * 2 + q + 1)
                    nc.scalar.activation(qT[:, q, :, :, 0:SEG],
                                         PS[0:C1, 4 * q, 0:2 * N].rearrange("c (p s t) -> c p s t", p=2, s=SEGS),
                                         ACT.Identity, bias=b_qkv0[:, 0:1]).then_inc(sem("a_qT"), 1)
                for q in range(2):
                    act.wait_ge(sem("a_sub"), i * 2 + q + 1)
                    nc.scalar.activation(prob[:, q], prob[:, q], ACT.Exp, scale=SCALE0).then_inc(sem("a_exp"), 1)
                route_drain(i)
                norm_seed(i + 1)
                for q in range(2):
                    for p in range(2):
                        act.wait_ge(sem("a_probT_ps"), i * 4 + 2 * q + p + 1)
                        nc.scalar.copy(probT[:, q, p].rearrange("k g t -> k (g t)"),
                                       PS[0:GRP * SEG, 4 * q + (0 if p else 3), 0:NGRP * 128]).then_inc(sem("a_probT"), 1)
                for q in range(2):
                    act.wait_ge(sem("a_oT_ps"), i * 2 + q + 1)
                    nc.scalar.activation(oT[:, q], PS[0:C1, 4 * q + 1, 0:2 * N], ACT.Identity, bias=b_qkv0[:, 2:3]
                                         ).then_inc(sem("a_oT"), 1)
            route_seed(B // 4)
            route_drain(B // 4)
            LN1 = LN0 + 2 * (B // 4) + 3
            act.wait_ge(sem("r_shift"), 1)
            nc.scalar.activation(r_e[:, 1], r_e[:, 0], ACT.Exp).then_inc(sem("r_exp"), 1)
            with act.Fori(0, PAIRS // 2) as i:
                for q in range(2):
                    for dh in range(2):
                        act.wait_ge(sem("disp_ps"), i * 4 + 2 * q + dh + 5)
                        nc.scalar.copy(xeT[:, dh, :, bass.ds(i * 2 + q, 1)].rearrange("k e g c -> k e (g c)"),
                                       PS[0:HD, 4 + 2 * q + dh, 0:E * CAP].rearrange("k (e c) -> k e c", e=E)
                                       ).then_inc(sem("xeT"), 1)
            act.wait_ge(sem("slot_ss"), 1)
            rsqrt_seed(slot_s[:, 0], slot_s[:, 1], slot_s[:, 2], 0.0, LN1).then_inc(sem("slot_seed"), 1)
            with act.Fori(0, E // 2) as i:
                for q in range(2):
                    for f in range(FT):
                        act.wait_ge(sem("hid_ps"), i * 2 * FT + q * FT + f + 1)
                        if f == 0:
                            act.wait_ge(sem("eo_ps"), i * 4 + 2 * q + 2)
                        nc.scalar.activation(hidT[:, q, f], PS[:, f % 2, 0:SLOTS], ACT.Relu).then_inc(sem("hidT"), 1)
            def drain_comb(i):
                for q in range(2):
                    for p in range(2):
                        act.wait_ge(sem("combT_ps"), i * 4 + 2 * q + p + 1)
                        nc.scalar.copy(combT[:, q, p].rearrange("s e t -> s (e t)"), PS[:, 4 * q + p, 0:E // 2 * N]
                                       ).then_inc(sem("combT"), 1)

            def linear_seed(i):
                act.wait_ge(sem("b_mv"), i * 4 + 4)
                rsqrt_seed(mv[:, :, 1], rs_tmp[0:N, 0], rs_tmp[0:N, 1], eps[0:N], i + LN1 + 1).then_inc(sem("b_seed"), 1)

            def drain_inputs(i):
                for q in range(2):
                    act.wait_ge(sem("b_xnT_ps"), i * 2 + q + 1)
                    nc.scalar.copy(xnT[:, q].rearrange("k a t -> k (a t)"), PS[0:HD, 4 * q + 3, 0:4 * N]
                                   ).then_inc(sem("b_xnT"), 1)

            def drain_keys(i):
                for q in range(2):
                    for p in range(2):
                        act.wait_ge(sem("b_kv"), i * 4 + 2 * q + p + 1)
                        nc.scalar.activation(abs_k[:, q, p], PS[0:N, 4 * q + p, 0:D], ACT.Abs).then_inc(sem("b_absk"), 1)
                    act.wait_ge(sem("b_q_ps"), i * 2 + q + 1)
                    nc.scalar.copy(q1T[:, q].rearrange("k a t -> k (a t)"), PS[0:HD, 4 * q + 2, 0:4 * N]).then_inc(sem("b_q1T"), 1)

            def drain_outputs(i):
                for q in range(2):
                    act.wait_ge(sem("b_oT_ps"), i * 2 + q + 1)
                    nc.scalar.copy(o1T[:, q].rearrange("k p a t -> k (p a t)"), PS[0:HD, 4 * q, 0:4 * N]
                                   ).then_inc(sem("b_o1T"), 1)

            def soft_seed(j):
                act.wait_ge(sem("s_var"), 2 * j + 2)
                rsqrt_seed(soft_st[:, 0:2], soft_st[:, 2:4], soft_st[:, 4:6], 0.0, LN2 + j + 1).then_inc(sem("s_seed"), 1)

            def soft_drain(j):
                act.wait_ge(sem("s_dsp_ps"), j + 1)
                if j > 0:
                    act.wait_ge(sem("s_xt_ps"), j)
                nc.scalar.copy(dsp[:], PS[0:N, 5, 0:128]).then_inc(sem("s_dsp"), 1)
                act.wait_ge(sem("s_cmbT_ps"), j + 1)
                nc.scalar.copy(cmbT[:, j], PS[:, 6, 0:N]).then_inc(sem("s_cmbT"), 1)

            def soft_drain_inputs(j):
                act.wait_ge(sem("s_xt_ps"), j + 1)
                nc.scalar.copy(x_tT[:, :, j * 128:(j + 1) * 128], PS[0:HD, 5, 128:384].rearrange("k (a s) -> k a s", a=2)
                               ).then_inc(sem("s_xtT"), 1)

            LAST = B // 4 - 1
            LN2 = LN1 + B // 4
            drain_comb(0)
            linear_seed(0)
            with act.Fori(0, LAST) as i:
                drain_inputs(i)
                drain_keys(i)
                drain_comb(i + 1)
                drain_outputs(i)
                linear_seed(i + 1)
            drain_inputs(LAST)
            soft_seed(0)
            drain_keys(LAST)
            drain_outputs(LAST)
            soft_seed(1)
            for j in range(4):
                act.wait_ge(sem("s_xsT_ps"), j + 1)
                for kh in range(2):
                    nc.scalar.copy(xsT[:, kh], PS[0:HD, 2 + kh, 0:4 * N]).then_inc(sem("s_xsT"), 1)
                if 0 < j < 3:
                    soft_seed(j + 1)
                if j > 0:
                    soft_drain(j - 1)
                act.wait_ge(sem("s_dmax"), j + 1)
                if j > 1:
                    act.wait_ge(sem("s_dsp_ps"), j - 1)
                nc.scalar.activation(dspT[:, j % 2], PS[:, 4, 0:N], ACT.Exp, bias=d_st[:, 0:1],
                                     accum_out=d_st[:, 1:2]).then_inc(sem("s_dexp"), 1)
                act.wait_ge(sem("s_csub"), j + 1)
                nc.scalar.activation(cmb[:, j % 2], cmb[:, j % 2], ACT.Exp).then_inc(sem("s_cexp"), 1)
                if j > 0:
                    soft_drain_inputs(j - 1)
            def soft_gelu(part):
                a, b = DONE[part]
                act.wait_ge(sem("s_hid_ps"), b)
                for mh in range(2):
                    nc.scalar.activation(hidS[:, mh, a * 128:b * 128], PS[0:HD, (1, 7)[mh], a * 128:b * 128], ACT.Gelu,
                                         bias=b_down[:, mh:mh + 1]).then_inc(sem("s_gelu"), 1)

            soft_drain(3)
            soft_gelu(0)
            soft_drain_inputs(3)
            soft_gelu(1)

        @block.vector
        def _(ve):

            def refine(var, eps, seed, t, dst, base, per, i, k):
                def tick(ins, j):
                    ins.then_inc(sem("dve_newton"), 1)
                    ve.wait_ge(sem("dve_newton"), i * (4 * per) + (base + 4 * k + j))
                tick(ve.scalar_tensor_tensor(t[0], var, eps, seed, ALU.add, ALU.mult), 1)
                tick(ve.tensor_tensor(t[1], t[0], seed, ALU.mult), 2)
                tick(ve.tensor_scalar(t[2], t[1], -0.5, 1.5, ALU.mult, ALU.add), 3)
                tick(ve.tensor_tensor(dst, t[2], seed, ALU.mult), 4)

            ve.sem_inc(sem("e_out"), 4)
            ve.memset(eps_col[:, 0:1], LN_EPS).then_inc(sem("eps_ready"), 1)
            ve.memset(eps_col[:, 1:2], 0.0).then_inc(sem("eps_ready"), 1)
            ve.wait_ge(sem("lnwb_in"), 32)
            ve.wait_ge(sem("wtok_in0"), 16)
            n = 0
            for t in range(KT - 1):
                shifts = range(5 * t, 5 * t + 5) if t < KT_IN else range(5 * t, 5 * t + 1)
                for k in shifts:
                    if k > 0 and k in W_CHUNKS:
                        ve.wait_ge(sem(f"wtok_in{W_CHUNKS.index(k)}"), 16)
                    dst = w_eff[:, t, 0:D]
                    if k == shifts[0]:
                        ins = ve.tensor_scalar(dst, w_tok[:, k], ln_w[:, k:k + 1], None, ALU.mult)
                    else:
                        ve.wait_ge(sem("fold"), n)
                        ins = ve.scalar_tensor_tensor(dst, w_tok[:, k], ln_w[:, k:k + 1], dst, ALU.mult, ALU.add)
                    if k == shifts[-1]:
                        ins.then_inc(sem("w_eff"), 1)
                    else:
                        ins.then_inc(sem("fold"), 1)
                        n += 1
            ve.wait_ge(sem("wtok2_in"), 16)
            ve.tensor_scalar(w_eff[0:HALO2, KT - 1, 0:D], w_tok2[:], ln_w[0:HALO2, W_TILES:W_TILES + 1], None,
                             ALU.mult).then_inc(sem("w_eff"), 1)
            ve.wait_ge(sem("bias_row_ps"), 1)
            ve.wait_ge(sem("tokbias_in"), 16)
            ve.tensor_tensor(bias_row[:], PS[:, 0, 0:D], tok_bias[:], ALU.add).then_inc(sem("bias_row"), 1)
            ve.wait_ge(sem("col_sum_ps"), 1)
            ve.tensor_copy(col_sum[:], PS[:, 1, 0:D]).then_inc(sem("bias_row"), 1)
            ve.wait_ge(sem("bias_row"), 2)
            ve.sem_inc(sem("tok_mid"), 2)
            st = tok_stat
            def tokens(i, done):
                for q in range(2):
                    ps = PS[:, 2 + q]
                    ve.wait_ge(sem("tok_ps"), i * 2 + q + 1)
                    ve.tensor_scalar(st[:, 0:1], ps[:, D:D + 1], -1.0 / PATCH_DIM, None, ALU.mult).then_inc(sem("tok_m"), 1)
                    ve.tensor_scalar(st[:, 1:2], ps[:, 200:201], 1.0 / PATCH_DIM, None, ALU.mult).then_inc(sem("tok_m"), 1)
                    ve.wait_ge(sem("tok_m"), i * 6 + q * 3 + 2)
                    ve.tensor_tensor(st[:, 2:3], st[:, 0:1], st[:, 0:1], ALU.mult).then_inc(sem("tok_m"), 1)
                    ve.wait_ge(sem("tok_m"), i * 6 + q * 3 + 3)
                    ve.tensor_tensor(st[:, 3:4], st[:, 1:2], st[:, 2:3], ALU.subtract).then_inc(sem("tok_var"), 1)
                    ve.scalar_tensor_tensor(tok_mid[:], col_sum[:], st[:, 0:1], ps[:, 0:D], ALU.mult, ALU.add
                                            ).then_inc(sem("tok_mid"), 1)
                    ve.wait_ge(sem("tok_seed"), i * 2 + q + 1)
                    refine(st[:, 3:4], LN_EPS, st[:, 5:6], [st[:, 6:7], st[:, 7:8], st[:, 8:9]], st[:, 9:10], done, 2, i, q)
                    ve.wait_ge(sem("tok_mid"), i * 2 + q + 3)
                    for p in range(2):
                        rows = slice(p * IMG_TOK, (p + 1) * IMG_TOK)
                        ve.scalar_tensor_tensor(h[0:IMG_TOK, bass.ds(i * 4 + 2 * q + p, 1), :].rearrange("t b d -> t (b d)"),
                                                tok_mid[rows], st[rows, 9:10], bias_row[rows], ALU.mult, ALU.add
                                                ).then_inc(sem("h_tok"), 1)
            def moments(i, np_, name, base, per, at=4):
                stand(ve)
                for p in range(np_):
                    ve.bn_stats(stat6[:, p], h_all[:, bass.ds(i * np_ + (at + p), 1), :].rearrange("t b d -> t (b d)")
                                ).then_inc(sem("stat6"), 1)
                for p in range(np_):
                    ve.wait_ge(sem("stat6"), i * per + (base + p + 1))
                    stand(ve)
                    ve.bn_aggr(mv[:, p], stat6[:, p]).then_inc(sem(name + "_mv"), 1)

            def normalize(i, np_, name, dst, scale, at=4):
                for p in range(np_):
                    ve.tensor_scalar(dst[:, p], h_all[:, bass.ds(i * np_ + (at + p), 1), :].rearrange("t b d -> t (b d)"),
                                     mv[:, p, 0:1], scale[0:N, p:p + 1], ALU.subtract, ALU.mult).then_inc(sem(name), 1)

            tmp4 = [rs_tmp[0:N, 2], rs_tmp[0:N, 3], rs_tmp[0:N, 4]]
            with ve.Fori(0, PAIRS // 2 - 1) as i:
                tokens(i, 0)
            ve.wait_ge(sem("txt_in"), 16)
            ve.wait_ge(sem("h_tok"), 4)
            moments(0, 4, "a", 0, 8)
            ve.wait_ge(sem("a_seed"), 1)
            refine(mv[:, :, 1], LN_EPS, rs_tmp[0:N, 1], tmp4, rs[0:N], 4 * (PAIRS - 2), 0, 0, 0)
            normalize(0, 4, "a_xn", xn, rs)
            tokens(PAIRS // 2 - 1, 4)
            NW0 = 4 * PAIRS

            ve.wait_ge(sem("cst_in"), 16)
            ve.wait_ge(sem("h_tok"), B)
            ve.wait_ge(sem("attn0_in"), 16 * 7)
            hm = const("headmask", C1).unsqueeze(2).to_broadcast([C1, GRP, 2 * N])
            vm = const("vmask", GRP * SEG)
            every_key = [128, NGRP, 2 * GRP, SEG]

            def norm_rest(i):
                ve.wait_ge(sem("a_seed"), i + 1)
                refine(mv[:, :, 1], LN_EPS, rs_tmp[0:N, 1], tmp4, rs[0:N], NW0, 2, i, 0)
                normalize(i, 4, "a_xn", xn, rs)

            def route_moments(i):
                moments(i, 4, "r", 4, 8, at=0)

            def route_norm(i):
                ve.wait_ge(sem("r_seed"), i + 1)
                refine(mv[:, :, 1], LN_EPS, rs_tmp[0:N, 1], tmp4, rs[0:N], NW0, 2, i, 1)
                normalize(i, 4, "r_xn", xnr, rs, at=0)

            ve.wait_ge(sem("pads_zero"), 4)
            with ve.Fori(0, B // 4) as i:
                route_moments(i)
                for q in range(2):
                    ve.wait_ge(sem("a_qk_ps"), i * 2 + q + 1)
                    ve.scalar_tensor_tensor(k_exp[:, q], PS[0:C1, 4 * q, 2 * N:4 * N].unsqueeze(1).to_broadcast([C1, GRP, 2 * N]),
                                            b_qkv0[:, 1:2], hm, ALU.add, ALU.mult).then_inc(sem("a_kexp"), 1)
                route_norm(i)
                for q in range(2):
                    for p in range(2):
                        ve.wait_ge(sem("a_v_ps"), i * 4 + 2 * q + p + 1)
                        ve.tensor_tensor(v_exp[:, q, p].rearrange("k s (g c) -> k (s g) c", g=NGRP),
                                         PS[0:GRP * SEG, 4 * q + 2 + p, 0:SEGS * C1].rearrange("k (a c) -> k a c", c=32),
                                         vm.unsqueeze(1).to_broadcast([GRP * SEG, SEGS * NGRP, 32]), ALU.mult
                                         ).then_inc(sem("a_vexp"), 1)
                for q in range(2):
                    s_ps = PS[:, 4 * q:4 * q + NGRP, 0:2 * GRP * SEG].rearrange("q g (h k) -> q g h k", k=SEG)
                    pr = prob[:, q].rearrange("q g p (h k) -> q g (p h) k", k=SEG)
                    ve.wait_ge(sem("a_s_ps"), i * 2 + q + 1)
                    ve.tensor_reduce(smax[:, q], s_ps, AX_X, ALU.max).then_inc(sem("a_max"), 1)
                    ve.wait_ge(sem("a_max"), i * 2 + q + 1)
                    ve.tensor_tensor(pr, s_ps, smax[:, q].unsqueeze(3).to_broadcast(every_key), ALU.subtract
                                     ).then_inc(sem("a_sub"), 1)
                moments(i + 1, 4, "a", 0, 8)
                for q in range(2):
                    pr = prob[:, q].rearrange("q g p (h k) -> q g (p h) k", k=SEG)
                    ve.wait_ge(sem("a_exp"), i * 2 + q + 1)
                    ve.tensor_reduce(ssum[:, q], pr, AX_X, ALU.add).then_inc(sem("a_sum"), 1)
                    ve.wait_ge(sem("a_sum"), i * 4 + 2 * q + 1)
                    ve.reciprocal(ssum[:, q], ssum[:, q]).then_inc(sem("a_sum"), 1)
                    ve.wait_ge(sem("a_sum"), i * 4 + 2 * q + 2)
                    ve.tensor_tensor(pr, pr, ssum[:, q].unsqueeze(3).to_broadcast(every_key), ALU.mult
                                     ).then_inc(sem("a_prob"), 1)
                ve.wait_ge(sem("a_xnT_ps"), i * 2 + 2)
                norm_rest(i + 1)
                for q in range(2):
                    ve.wait_ge(sem("a_proj_ps"), i * 2 + q + 1)
                    ve.wait_ge(sem("h_biased"), i * 4 + 4)
                    hp = h[:, bass.ds(i * 4 + 2 * q, 2), :]
                    ve.tensor_tensor(hp, hp, PS[0:N, 4 * q + 2, 0:2 * D].rearrange("t (p d) -> t p d", p=2), ALU.add
                                     ).then_inc(sem("a_h"), 1)
                ve.wait_ge(sem("r_kept"), i + 1)
                ve.wait_ge(sem("r_xnT_ps"), i * 2 + 2)
                ve.wait_ge(sem("a_h"), i * 2 + 2)
            route_moments(B // 4)
            route_norm(B // 4)
            NW1 = NW0 + 8 * (B // 4) + 12

            def wide(x):
                return x.unsqueeze(2).to_broadcast([N, B, E])

            step = [0]

            def then(ins):
                step[0] += 1
                ins.then_inc(sem("r_step"), 1)
                ve.wait_ge(sem("r_step"), step[0])

            rev = const("rev", N).unsqueeze(1).to_broadcast([N, B, E])
            ve.wait_ge(sem("r_logit"), PAIRS + 2)
            then(ve.tensor_reduce(r_top[:, 0], logits[:], AX_X, ALU.max))
            ve.tensor_tensor(r_e[:, 0], logits[:], wide(r_top[:, 0]), ALU.subtract).then_inc(sem("r_shift"), 1)

            def pick(src, best, tmp, dst):
                then(ve.tensor_tensor(tmp, src, wide(best), ALU.is_equal))
                then(ve.tensor_tensor(tmp, tmp, rev, ALU.mult))
                then(ve.tensor_reduce(r_top[:, 1], tmp, AX_X, ALU.max))
                return ve.tensor_tensor(dst, tmp, wide(r_top[:, 1]), ALU.is_equal)

            pick(logits[:], r_top[:, 0], r_e[:, 5], r_e[:, 2]).then_inc(sem("r_first"), 1)
            ve.wait_ge(sem("r_first"), 1)
            then(ve.scalar_tensor_tensor(r_e[:, 3], r_e[:, 2], -3e38, logits[:], ALU.mult, ALU.add))
            then(ve.tensor_reduce(r_top[:, 2], r_e[:, 3], AX_X, ALU.max))
            pick(r_e[:, 3], r_top[:, 2], r_e[:, 5], r_e[:, 4]).then_inc(sem("r_choice"), 2)
            ve.wait_ge(sem("r_choice"), 2)
            ve.wait_ge(sem("r_exp"), 1)
            then(ve.tensor_reduce(r_top[:, 3], r_e[:, 1], AX_X, ALU.add))
            then(ve.reciprocal(r_top[:, 4], r_top[:, 3]))
            then(ve.tensor_tensor(r_e[:, 0], r_e[:, 1], wide(r_top[:, 4]), ALU.mult))
            then(ve.tensor_tensor(r_e[:, 5], r_e[:, 2], r_e[:, 4], ALU.add))
            then(ve.tensor_tensor(gate_of[:], r_e[:, 0], r_e[:, 5], ALU.mult))
            ve.wait_ge(sem("r_count_ps"), 1)
            count = PS[0:N, 3, 0:4 * PAIRS * E].rearrange("t (k p g e) -> t k g p e", k=2, p=2, g=PAIRS)
            four = lambda x: x.rearrange("t (g p) e -> t g p e", p=2)
            then(ve.tensor_tensor(four(r_e[:, 0]), four(r_e[:, 2]), count[:, 0], ALU.mult))
            then(ve.tensor_tensor(four(r_e[:, 1]), four(r_e[:, 4]), count[:, 1], ALU.mult))
            then(ve.scalar_tensor_tensor(slot_of[:], r_e[:, 0], -1.0, r_e[:, 1], ALU.add, ALU.add))

            iota = const("iota", N).unsqueeze(1).to_broadcast([N, E, CAP])

            def place(b):
                return slot_of[:, bass.ds(b, 1), :].rearrange("t b e -> t (b e)").unsqueeze(2).to_broadcast([N, E, CAP])

            with ve.Fori(0, PAIRS // 2) as i:
                for q in range(2):
                    ve.wait_ge(sem("disp_ps"), i * 4 + 2 * q + 2)
                    for p in range(2):
                        ve.tensor_tensor(onehot[:, q, p].rearrange("t (e c) -> t e c", e=E), iota,
                                         place(i * 4 + (2 * q + p)), ALU.is_equal).then_inc(sem("onehot"), 1)
            ve.wait_ge(sem("layer1_in"), 16 * 10)
            ve.tensor_tensor(slot_sq[:], slot_raw[:], slot_raw[:], ALU.mult).then_inc(sem("slot_step"), 1)
            ve.wait_ge(sem("slot_step"), 1)
            ve.tensor_reduce(slot_s[:, 3].rearrange("k (a s) -> k a s", a=2),
                             slot_sq[:].rearrange("k a (n s) -> k a s n", n=NS), AX_X, ALU.add).then_inc(sem("slot_step"), 1)
            ve.wait_ge(sem("slot_step"), 2)
            ve.tensor_scalar(slot_s[:, 0], slot_s[:, 3], TINY, None, ALU.max).then_inc(sem("slot_ss"), 1)
            ve.wait_ge(sem("slot_seed"), 1)
            refine(slot_s[:, 0], 0.0, slot_s[:, 2], [slot_s[:, 4], slot_s[:, 5], slot_s[:, 1]], slot_s[:, 4], NW1 - 4, 0, 0, 0)
            ve.tensor_tensor(slot_s[:, 5], slot_s[:, 3], slot_s[:, 4], ALU.mult).then_inc(sem("slot_step"), 1)
            ve.wait_ge(sem("slot_step"), 3)
            ve.tensor_scalar(slot_s[:, 1], slot_s[:, 5], L2_EPS, None, ALU.add).then_inc(sem("slot_step"), 1)
            ve.wait_ge(sem("slot_step"), 4)
            ve.reciprocal(slot_s[:, 2], slot_s[:, 1]).then_inc(sem("slot_step"), 1)
            ve.wait_ge(sem("slot_step"), 5)
            ve.tensor_scalar(slot_s[:, 5], slot_s[:, 2], l_scale[:], None, ALU.mult).then_inc(sem("slot_step"), 1)
            ve.wait_ge(sem("slot_step"), 6)
            for a in range(2):
                ve.tensor_tensor(slot_n[:, a].rearrange("k (n s) -> k n s", n=NS),
                                 slot_raw[:, a].rearrange("k (n s) -> k n s", n=NS),
                                 slot_s[:, 5, a * PS_:(a + 1) * PS_].unsqueeze(1).to_broadcast([HD, NS, PS_]), ALU.mult
                                 ).then_inc(sem("slot_n"), 1)
            ve.wait_ge(sem("pads_zero"), 5)
            def build_comb(i):
                for q in range(2):
                    for p in range(2):
                        cm = comb[:, q, p, :, 0:CAP]
                        b = i * 4 + (2 * q + p)
                        ve.tensor_tensor(cm, iota, place(b), ALU.is_equal).then_inc(sem("comb_hot"), 1)
                        ve.wait_ge(sem("comb_hot"), i * 4 + 2 * q + p + 1)
                        g = gate_of[:, bass.ds(b, 1), :].rearrange("t b e -> t (b e)").unsqueeze(2).to_broadcast([N, E, CAP])
                        ve.tensor_tensor(cm, cm, g, ALU.mult).then_inc(sem("comb"), 1)

            build_comb(0)
            ve.wait_ge(sem("pads_zero"), 4)
            with ve.Fori(0, E // 2) as i:
                for q in range(2):
                    for half in range(2):
                        ve.wait_ge(sem("eo_ps"), i * 4 + 2 * q + half + 5)
                        for z in range(2):
                            ve.tensor_copy(
                                e_out[64 * q:64 * q + CAP, half * 4 + z:half * 4 + z + 3:2, bass.ds(i, 1)].rearrange("s g e d -> s g (e d)"),
                                PS[64 * z:64 * z + CAP, 2 + half, 0:2 * D].rearrange("s (g d) -> s g d", g=2)
                            ).then_inc(sem("e_out"), 1)
            ve.wait_ge(sem("layer1_in"), 16 * 10)
            l1m = const("l1mask", HD)
            ve.wait_ge(sem("pads_zero"), 5)
            def add_combined(i):
                for q in range(2):
                    ve.wait_ge(sem("moe_ps"), i * 2 + q + 1)
                    hp = h[:, bass.ds(i * 4 + 2 * q, 2), :]
                    ve.tensor_tensor(hp, hp, PS[0:N, 4 * q + 2, 0:2 * D].rearrange("t (p d) -> t p d", p=2), ALU.add
                                     ).then_inc(sem("moe_h"), 1)
                ve.wait_ge(sem("moe_h"), i * 2 + 2)
                moments(i, 4, "b", 2 * B + 8, 4)
                ve.wait_ge(sem("b_seed"), i + 1)
                refine(mv[:, :, 1], LN_EPS, rs_tmp[0:N, 1], tmp4, rs[0:N], NW1, 1, i, 0)
                normalize(i, 4, "b_xn", xn, rs)

            def linear_middle(i):
                for q in range(2):
                    for p in range(2):
                        ve.wait_ge(sem("b_kv_ps"), i * 4 + 2 * q + p + 1)
                        ve.tensor_copy(kv1[:, q, p], PS[0:N, 4 * q + p, 0:2 * D]).then_inc(sem("b_kv"), 1)
                for q in range(2):
                    dn = den[:, q]
                    c = i * 12 + 6 * q
                    ve.wait_ge(sem("b_q1T"), i * 2 + q + 1)
                    for mh in range(2):
                        ve.tensor_reduce(dn[:, 0].rearrange("k (p a) -> k a p", a=2)[:, mh],
                                         q1T[:, q, mh].rearrange("k (p t) -> k p t", p=2), AX_X, ALU.add,
                                         apply_absolute_value=True).then_inc(sem("b_den"), 1)
                    ve.wait_ge(sem("b_den"), c + 2)
                    ve.tensor_scalar(dn[:, 1], dn[:, 0], L1_EPS, None, ALU.max).then_inc(sem("b_den"), 1)
                    ve.wait_ge(sem("b_kvp_ps"), i * 2 + q + 1)
                    ve.tensor_scalar(dn[:, 2], PS[0:HD, 4 * q + 3, 4 * HD:4 * HD + 4], L1_EPS, None, ALU.max
                                     ).then_inc(sem("b_den"), 1)
                    ve.wait_ge(sem("b_den"), c + 4)
                    ve.reciprocal(dn[:, 3:5], dn[:, 1:3]).then_inc(sem("b_den"), 1)
                    ve.wait_ge(sem("b_den"), c + 5)
                    ve.tensor_tensor(dn[:, 5], dn[:, 3], dn[:, 4], ALU.mult).then_inc(sem("b_den"), 1)
                    ve.wait_ge(sem("b_den"), c + 6)
                    for p in range(2):
                        for mh in range(2):
                            j = p * 2 + mh
                            ve.scalar_tensor_tensor(kv_bd[:, q, p, mh], PS[0:HD, 4 * q + 3, j * HD:(j + 1) * HD],
                                                    dn[:, 5, j:j + 1], l1m, ALU.mult, ALU.mult).then_inc(sem("b_kvbd"), 1)

            def add_projected(i):
                for q in range(2):
                    ve.wait_ge(sem("b_proj_ps"), i * 2 + q + 1)
                    ve.wait_ge(sem("h_biased"), i * 4 + (B + 4))
                    hp = h[:, bass.ds(i * 4 + 2 * q, 2), :]
                    ve.tensor_tensor(hp, hp, PS[0:N, 4 * q + 1, 0:2 * D].rearrange("t (p d) -> t p d", p=2), ALU.add
                                     ).then_inc(sem("b_h"), 1)

            def soft_rows(j):
                ve.wait_ge(sem("b_h"), 2 * j + 4)
                moments(j, 4, "s", 3 * B + 8, 4)
                ve.wait_ge(sem("s_mv"), j * 4 + 4)
                ve.tensor_scalar(soft_st[:, 0], mv[:, :, 1], LN_EPS, None, ALU.add).then_inc(sem("s_var"), 1)
                ve.tensor_scalar(soft_st[:, 1], mv[:, :, 1], TINY, None, ALU.max).then_inc(sem("s_var"), 1)
                ve.wait_ge(sem("s_var"), 2 * j + 2)
                ve.wait_ge(sem("s_seed"), j + 1)
                refine(soft_st[:, 0:2], 0.0, soft_st[:, 4:6],
                       [soft_st[:, 6:8], soft_st[:, 8:10], soft_st[:, 10:12]], soft_st[:, 2:4], NW2, 1, j, 0)

                def tick(ins, k):
                    ins.then_inc(sem("s_scale"), 1)
                    ve.wait_ge(sem("s_scale"), j * 5 + k)
                tick(ve.tensor_tensor(soft_st[:, 6], mv[:, :, 1], soft_st[:, 3], ALU.mult), 1)
                tick(ve.scalar_tensor_tensor(soft_st[:, 7], soft_st[:, 6], float(D) ** 0.5, soft_st[:, 2], ALU.mult, ALU.mult), 2)
                tick(ve.tensor_scalar(soft_st[:, 8], soft_st[:, 7], L2_EPS, None, ALU.add), 3)
                tick(ve.reciprocal(soft_st[:, 9], soft_st[:, 8]), 4)
                tick(ve.tensor_tensor(soft_st[:, 10], soft_st[:, 9], soft_st[:, 2], ALU.mult), 5)
                normalize(j, 4, "s_xs", xs[:, j], soft_st[:, 10])

            def soft_weights(j):
                log = PS[0:N, 0, 0:4 * NP].rearrange("t (p n) -> t p n", p=4)
                ve.wait_ge(sem("s_log_ps"), j + 1)
                ve.tensor_reduce(c_st[:, 0], log, AX_X, ALU.max).then_inc(sem("s_soft"), 1)
                ve.wait_ge(sem("s_soft"), j * 4 + 1)
                if j > 1:
                    ve.wait_ge(sem("s_cmbT_ps"), j - 1)
                ve.tensor_tensor(cmb[:, j % 2], log, c_st[:, 0].unsqueeze(2).to_broadcast([N, 4, NP]), ALU.subtract
                                 ).then_inc(sem("s_csub"), 1)
                ve.wait_ge(sem("s_logT_ps"), j + 1)
                ve.tensor_reduce(d_st[:, 0:1], PS[:, 4, 0:N], AX_X, ALU.max, negate=True).then_inc(sem("s_dmax"), 1)
                ve.wait_ge(sem("s_dexp"), j + 1)
                ve.reciprocal(d_st[:, 2:3], d_st[:, 1:2]).then_inc(sem("s_soft"), 1)
                ve.wait_ge(sem("s_soft"), j * 4 + 2)
                ve.tensor_scalar(dspT[:, j % 2], dspT[:, j % 2], d_st[:, 2:3], None, ALU.mult).then_inc(sem("s_dspT"), 1)
                ve.wait_ge(sem("s_cexp"), j + 1)
                ve.tensor_reduce(c_st[:, 1], cmb[:, j % 2], AX_X, ALU.add).then_inc(sem("s_soft"), 1)
                ve.wait_ge(sem("s_soft"), j * 4 + 3)
                ve.reciprocal(c_st[:, 2], c_st[:, 1]).then_inc(sem("s_soft"), 1)
                ve.wait_ge(sem("s_soft"), j * 4 + 4)
                ve.tensor_tensor(cmb[:, j % 2], cmb[:, j % 2], c_st[:, 2].unsqueeze(2).to_broadcast([N, 4, NP]), ALU.mult
                                 ).then_inc(sem("s_cmb"), 1)

            LAST = B // 4 - 1
            NW2 = NW1 + 4 * (B // 4)
            add_combined(0)
            with ve.Fori(0, LAST) as i:
                ve.wait_ge(sem("combT_ps"), i * 4 + 4)
                build_comb(i + 1)
                linear_middle(i)
                add_combined(i + 1)
                add_projected(i)
            soft_rows(0)
            linear_middle(LAST)
            soft_rows(1)
            add_projected(LAST)
            for j in range(4):
                soft_weights(j)
                if j < 2:
                    soft_rows(j + 2)
            upm = const("upmask", HD)

            def keep_own(part):
                a, b = DONE[part]
                for mh in range(2):
                    ve.wait_ge(sem("s_gelu"), 2 * part + mh + 1)
                    hv = hidS[:, mh, a * 128:b * 128].rearrange("k (b n s) -> k b n s", n=NS, s=PS_)
                    own = upm[:, mh * NS:(mh + 1) * NS].unsqueeze(1).unsqueeze(3).to_broadcast([HD, (b - a) * 4, NS, PS_])
                    ve.tensor_tensor(hv, hv, own, ALU.mult).then_inc(sem("s_hidm"), 1)

            def add_up_bias(j):
                ve.wait_ge(sem("s_yt_ps"), j + 1)
                ve.tensor_tensor(y_t[:, j], PS[:, 2 + j % 2, 0:D], b_up[:], ALU.add).then_inc(sem("s_yt"), 1)

            def add_soft(b):
                ve.wait_ge(sem("s_y_ps"), b + 1)
                ve.tensor_tensor(h[:, b], h[:, b], PS[0:N, Y_BANK[b % 4], 0:D], ALU.add).then_inc(sem("y_added"), 1)

            keep_own(0)
            for j in range(3):
                add_up_bias(j)
            keep_own(1)
            for b in range(4):
                add_soft(b)
            add_up_bias(3)
            for b in range(4, B):
                add_soft(b)


def constants():
    import numpy as np
    c = {}
    c["ident"] = np.eye(128)
    c["ones"] = np.ones((128, 128))
    c["tri"] = np.triu(np.ones((N, N)))
    r = np.arange(128)
    c["l1mask"] = (r[:HD, None] // 16 == r[None, :HD] // 16)
    c["iota"] = np.tile(np.arange(CAP), (128, 1))
    c["vmask"] = (r[:GRP * SEG, None] // SEG == r[None, :32] // HDIM0)
    c["upmask"] = np.concatenate([(r[:HD, None] // HS + mh * 4 == r[None, :NS]) for mh in range(2)], axis=1)
    c["rev"] = np.tile(E - np.arange(E), (128, 1))
    i = np.arange(PATCH)
    inner = (i > 0).astype(int) + (i < PATCH - 1)
    m = np.zeros((KT, 128))
    m[:KT_IN] = np.tile((1 + inner[:, None] + inner[None, :]).reshape(-1), C).reshape(KT_IN, 128)
    m[KT_IN] = 1
    m[KT_IN + 1, :HALO2] = 1
    c["mult"] = m.T
    c["headmask"] = ((r[:C1, None] % 32) // HDIM0 == r[None, :GRP])
    out = np.zeros((128, CONST_W), np.float32)
    for name, (a, w) in CONST_AT.items():
        out[:c[name].shape[0], a:a + w] = c[name]
    return out


def halo(t):
    import numpy as np
    return np.concatenate([t[..., 1:-1, 0], t[..., 1:-1, -1], t[..., 0, 1:-1], t[..., -1, 1:-1]], axis=-1)


def kernel(**inputs):
    import numpy as np
    import concourse.bacc as bacc
    from concourse.bass_utils import run_bass_kernel_spmd

    v = {k: np.ascontiguousarray(a) for k, a in inputs.items()}
    P = PATCH
    xp = np.zeros((B, C, IMG + 2, IMG + 2), np.float32)
    xp[:, :, 1:-1, 1:-1] = v["x"]
    win = np.stack([np.stack([xp[:, :, P * a:P * a + P + 2, P * b:P * b + P + 2] for b in range(SIDE)], 2)
                    for a in range(SIDE)], 2)
    inner = win[..., 1:-1, 1:-1].reshape(B, C, IMG_TOK, P * P).transpose(1, 3, 0, 2).reshape(K_IN, B * IMG_TOK)
    outer = halo(win).reshape(B, C, IMG_TOK, 4 * P).transpose(1, 3, 0, 2).reshape(K_HALO, B * IMG_TOK)
    allk = np.concatenate([inner, outer], 0)
    xin = allk[:(KT - 1) * 128].reshape(KT - 1, 128, PAIRS, 128).transpose(2, 1, 0, 3)
    xhalo = allk[(KT - 1) * 128:].reshape(HALO2, PAIRS, 128).transpose(1, 0, 2)

    def fold(t):
        t = t.reshape(-1, P, P, 5, C).transpose(3, 4, 1, 2, 0)
        win = np.zeros((5, C, P + 2, P + 2, t.shape[-1]), np.float32)
        for s, (dy, dx) in enumerate([(0, 0), (0, -1), (0, 1), (-1, 0), (1, 0)]):
            win[s, :, 1 + dy:1 + dy + P, 1 + dx:1 + dx + P] = t[s]
        inn = win[:, :, 1:-1, 1:-1].reshape(5, KT_IN, 128, -1).transpose(2, 1, 0, 3).reshape(128, 5 * KT_IN, -1)
        ring = [win[1][:, 1:-1, 0], win[2][:, 1:-1, -1], win[3][:, 0, 1:-1], win[4][:, -1, 1:-1]]
        ring = np.stack(ring, 1).reshape(K_HALO, -1)
        return np.concatenate([inn, ring[:128, None]], 1), ring[128:]

    wtok, wtok2 = fold(v["L0_tok_proj_weight"])

    def columns(t):
        a, b = fold(t[None])
        out = np.zeros((128, W_TILES + 1), np.float32)
        out[:, :W_TILES] = a[..., 0]
        out[:HALO2, W_TILES] = b[:, 0]
        return out

    def halves(w):
        return w.reshape(2, HD, -1).transpose(1, 0, 2)

    wqkv1 = v["L1_attn_w_qkv"].T
    arrays = {
        "xin": xin, "xhalo": xhalo, "txt": v["txt"], "wtok": wtok, "wtok2": wtok2,
        "lnw": columns(v["L0_tok_ln_weight"]), "lnb": columns(v["L0_tok_ln_bias"]), "tokbias": v["L0_tok_proj_bias"],
        "consts": constants(),
        "wred": halves(v["L0_attn_W_reduce"]), "bred": v["L0_attn_b_reduce"][:, None], "wqkv0": v["L0_attn_W_qkv"],
        "bqkv0": v["L0_attn_b_qkv"].reshape(3, C1).T, "wproj0": v["L0_attn_W_proj"], "bproj0": v["L0_attn_b_proj"],
        "wrouter": halves(v["L0_ffn_w_router"]),
        "wi": v["L0_ffn_wi"].reshape(E, 2, HD, F).transpose(0, 2, 1, 3),
        "wo": v["L0_ffn_wo"].reshape(E, FT, 128, D).transpose(0, 2, 1, 3),
        "wq1": halves(wqkv1[:, :D]), "wkv1": halves(wqkv1[:, D:]), "wproj1": halves(v["L1_attn_w_proj"].T),
        "bproj1": v["L1_attn_b_proj"],
        "slots": halves(v["L1_ffn_slot_params"].reshape(D, NP)), "lscale": v["L1_ffn_scale"].reshape(1),
        "wdown": halves(v["L1_ffn_W_down"].transpose(1, 0, 2).reshape(D, NS * HS)),
        "bdown": v["L1_ffn_b_down"].reshape(2, HD).T,
        "wup": halves(v["L1_ffn_W_up"].reshape(NS * HS, D)),
        "bup": np.tile(np.repeat(v["L1_ffn_b_up"], PS_, axis=0), (4, 1)),
    }
    nc = bacc.Bacc("TRN2", target_bir_lowering=False, num_devices=1)
    feeds, args = {}, {}
    for name, a in arrays.items():
        a = np.ascontiguousarray(a)
        feeds[f"in_{name}"] = a
        args[name] = nc.dram_tensor(f"in_{name}", a.shape, F32, kind="ExternalInput").ap()
    args["out"] = nc.dram_tensor("out_0", (B, N, D), F32, kind="ExternalOutput").ap()
    build(nc, **args)
    r = run_bass_kernel_spmd(nc, [feeds], core_ids=[0])
    return r.results[0]["out_0"]
```
